# Optimizing a Trainium2 kernel written in Bass

```python
import numpy as np
import jax
import jax.numpy as jnp

def _softmax(x, axis=-1):
    return jax.nn.softmax(x, axis=axis)

def _gelu(x):
    return jax.nn.gelu(x, approximate=True)

def _silu(x):
    return jax.nn.silu(x)

def _sigmoid(x):
    return jax.nn.sigmoid(x)

def _layernorm(x, axis=-1, eps=1e-05):
    m = jnp.mean(x, axis=axis, keepdims=True)
    v = jnp.var(x, axis=axis, keepdims=True)
    return (x - m) / jnp.sqrt(v + eps)

def _scatter_add(tgt, idx, src, axis=0):
    return tgt.at[idx].add(src)

def _segment_sum(src, seg, n):
    return jax.ops.segment_sum(src, seg, n)
kernel_name = 'mk_lm_tower_d2_tok_ids512_r4_2b44c7'

def setup_inputs(seed: int=0):
    np.random.seed(seed)
    _w = jnp.asarray

    def _rec_inputs():
        import jax
        import jax.numpy as jnp
        _rk = jax.random.key(seed)
        x = jax.random.randint(jax.random.fold_in(_rk, 1), (4, 512), 0, 5, jnp.int32)
        return x
    x = _rec_inputs()

    def _L0_tok_setup():
        import jax, jax.numpy as jnp
        import numpy as np
        K = 6
        VOCAB = 5
        HIDDEN = 128
        key = jax.random.key(seed)
        k1, k2 = jax.random.split(key)
        input_ids = jax.random.randint(k1, (8, 4096), 0, VOCAB, dtype=jnp.int32)
        table = jax.random.normal(k2, (VOCAB ** K, HIDDEN), dtype=jnp.float32)
        return {'input_ids': input_ids, 'table': table}
    _L0_tok_all = _L0_tok_setup()
    _L0_tok_in = {k: v for k, v in _L0_tok_all.items() if k in ('table',)}
    del _L0_tok_all

    def _L0_attn_setup():
        import jax, jax.numpy as jnp
        import numpy as np
        EMBED_DIM = 128
        NUM_HEADS = 8
        HEAD_DIM = EMBED_DIM // NUM_HEADS
        key = jax.random.key(seed)
        k_x, k_qkv, k_proj, k_pb = jax.random.split(key, 4)
        B, N, C = (2, 1024, EMBED_DIM)
        x = jax.random.normal(k_x, (B, N, C), dtype=jnp.float32)
        s = 1.0 / np.sqrt(C)
        w_qkv = jax.random.uniform(k_qkv, (3 * C, C), dtype=jnp.float32, minval=-s, maxval=s)
        w_proj = jax.random.uniform(k_proj, (C, C), dtype=jnp.float32, minval=-s, maxval=s)
        b_proj = jax.random.uniform(k_pb, (C,), dtype=jnp.float32, minval=-s, maxval=s)
        return {'x': x, 'w_qkv': w_qkv, 'w_proj': w_proj, 'b_proj': b_proj}
    _L0_attn_all = _L0_attn_setup()
    _L0_attn_in = {k: v for k, v in _L0_attn_all.items() if k in ('w_qkv', 'w_proj', 'b_proj')}
    del _L0_attn_all

    def _L0_ffn_setup():
        import jax, jax.numpy as jnp
        import numpy as np
        from jax import lax
        N_EXPERTS = 16
        TOP_K = 2
        D_MODEL = 128
        D_FF = 512
        key = jax.random.key(seed)
        ks = jax.random.split(key, 7)
        s_in = 1.0 / np.sqrt(D_MODEL)
        s_ff = 1.0 / np.sqrt(D_FF)
        x = jax.random.normal(ks[0], (2, 512, D_MODEL), dtype=jnp.float32)
        router_w = jax.random.uniform(ks[1], (N_EXPERTS, D_MODEL), jnp.float32, -s_in, s_in)
        router_b = jax.random.uniform(ks[2], (N_EXPERTS,), jnp.float32, -s_in, s_in)
        w1 = jax.random.uniform(ks[3], (N_EXPERTS, D_FF, D_MODEL), jnp.float32, -s_in, s_in)
        b1 = jax.random.uniform(ks[4], (N_EXPERTS, D_FF), jnp.float32, -s_in, s_in)
        w2 = jax.random.uniform(ks[5], (N_EXPERTS, D_MODEL, D_FF), jnp.float32, -s_ff, s_ff)
        b2 = jax.random.uniform(ks[6], (N_EXPERTS, D_MODEL), jnp.float32, -s_ff, s_ff)
        return {'x': x, 'router_w': router_w, 'router_b': router_b, 'w1': w1, 'b1': b1, 'w2': w2, 'b2': b2}
    _L0_ffn_all = _L0_ffn_setup()
    _L0_ffn_in = {k: v for k, v in _L0_ffn_all.items() if k in ('router_w', 'router_b', 'w1', 'b1', 'w2', 'b2')}
    del _L0_ffn_all

    def _L1_attn_setup():
        import jax, jax.numpy as jnp
        import numpy as np
        import math
        B, S, H = (2, 1024, 128)
        NUM_HEADS = 8
        HEAD_DIM = H // NUM_HEADS
        RECENCY_DECAY = 0.9
        key = jax.random.key(seed)
        k1, k2, k3 = jax.random.split(key, 3)
        scale = 1.0 / math.sqrt(H)
        x = jax.random.normal(k1, (B, S, H), dtype=jnp.float32)
        w_qkv = jax.random.normal(k2, (3 * H, H), dtype=jnp.float32) * scale
        w_out = jax.random.normal(k3, (H, H), dtype=jnp.float32) * scale
        b_out = jnp.zeros((H,), dtype=jnp.float32)
        return {'x': x, 'w_qkv': w_qkv, 'w_out': w_out, 'b_out': b_out}
    _L1_attn_all = _L1_attn_setup()
    _L1_attn_in = {k: v for k, v in _L1_attn_all.items() if k in ('w_qkv', 'w_out', 'b_out')}
    del _L1_attn_all

    def _L1_ffn_setup():
        import jax, jax.numpy as jnp
        import numpy as np
        B, S, D = (4, 512, 128)
        I = 96
        E = 16
        K = 2

        def _inv_softplus(v):
            return float(np.log(np.expm1(v)))

        def swiglu5(h, alpha, gate_scale, up_shift, gate_clamp_raw, up_clamp_raw):
            gate_clamp = jax.nn.softplus(gate_clamp_raw)
            up_clamp = jax.nn.softplus(up_clamp_raw)
            g = jnp.clip(h[..., ::2], -gate_clamp, gate_clamp)
            u = jnp.clip(h[..., 1::2], -up_clamp, up_clamp)
            return g * jax.nn.sigmoid(g * alpha) * gate_scale * (u + up_shift)
        key = jax.random.key(seed)
        ks = jax.random.split(key, 10)
        std = 0.02
        raw = _inv_softplus(7.0)
        act = jnp.array([1.702, 1.0, 1.0, raw, raw], dtype=jnp.float32)
        return {'x': jax.random.normal(ks[0], (B, S, D), dtype=jnp.float32), 'gate_w': jax.random.normal(ks[1], (D, E), dtype=jnp.float32) * 0.01, 'gate_b': jnp.zeros((E,), dtype=jnp.float32), 'shared_w1': jax.random.normal(ks[2], (D, 2 * I), dtype=jnp.float32) * std, 'shared_b1': jnp.zeros((2 * I,), dtype=jnp.float32), 'shared_w2': jax.random.normal(ks[3], (I, D), dtype=jnp.float32) * std, 'shared_b2': jnp.zeros((D,), dtype=jnp.float32), 'shared_act': act, 'expert_w1': jax.random.normal(ks[4], (E, D, 2 * I), dtype=jnp.float32) * std, 'expert_b1': jnp.zeros((E, 2 * I), dtype=jnp.float32), 'expert_w2': jax.random.normal(ks[5], (E, I, D), dtype=jnp.float32) * std, 'expert_b2': jnp.zeros((E, D), dtype=jnp.float32), 'expert_act': jnp.tile(act[None, :], (E, 1))}
    _L1_ffn_all = _L1_ffn_setup()
    _L1_ffn_in = {k: v for k, v in _L1_ffn_all.items() if k in ('gate_w', 'gate_b', 'shared_w1', 'shared_b1', 'shared_w2', 'shared_b2', 'shared_act', 'expert_w1', 'expert_b1', 'expert_w2', 'expert_b2', 'expert_act')}
    del _L1_ffn_all
    return {'x': x, 'L0_tok_table': _L0_tok_in['table'], 'L0_attn_w_qkv': _L0_attn_in['w_qkv'], 'L0_attn_w_proj': _L0_attn_in['w_proj'], 'L0_attn_b_proj': _L0_attn_in['b_proj'], 'L0_ffn_router_w': _L0_ffn_in['router_w'], 'L0_ffn_router_b': _L0_ffn_in['router_b'], 'L0_ffn_w1': _L0_ffn_in['w1'], 'L0_ffn_b1': _L0_ffn_in['b1'], 'L0_ffn_w2': _L0_ffn_in['w2'], 'L0_ffn_b2': _L0_ffn_in['b2'], 'L1_attn_w_qkv': _L1_attn_in['w_qkv'], 'L1_attn_w_out': _L1_attn_in['w_out'], 'L1_attn_b_out': _L1_attn_in['b_out'], 'L1_ffn_gate_w': _L1_ffn_in['gate_w'], 'L1_ffn_gate_b': _L1_ffn_in['gate_b'], 'L1_ffn_shared_w1': _L1_ffn_in['shared_w1'], 'L1_ffn_shared_b1': _L1_ffn_in['shared_b1'], 'L1_ffn_shared_w2': _L1_ffn_in['shared_w2'], 'L1_ffn_shared_b2': _L1_ffn_in['shared_b2'], 'L1_ffn_shared_act': _L1_ffn_in['shared_act'], 'L1_ffn_expert_w1': _L1_ffn_in['expert_w1'], 'L1_ffn_expert_b1': _L1_ffn_in['expert_b1'], 'L1_ffn_expert_w2': _L1_ffn_in['expert_w2'], 'L1_ffn_expert_b2': _L1_ffn_in['expert_b2'], 'L1_ffn_expert_act': _L1_ffn_in['expert_act']}

def reference(x, L0_tok_table, L0_attn_w_qkv, L0_attn_w_proj, L0_attn_b_proj, L0_ffn_router_w, L0_ffn_router_b, L0_ffn_w1, L0_ffn_b1, L0_ffn_w2, L0_ffn_b2, L1_attn_w_qkv, L1_attn_w_out, L1_attn_b_out, L1_ffn_gate_w, L1_ffn_gate_b, L1_ffn_shared_w1, L1_ffn_shared_b1, L1_ffn_shared_w2, L1_ffn_shared_b2, L1_ffn_shared_act, L1_ffn_expert_w1, L1_ffn_expert_b1, L1_ffn_expert_w2, L1_ffn_expert_b2, L1_ffn_expert_act):
    import jax
    import jax.numpy as jnp

    def _L0_tok_ref(input_ids, table):
        import jax, jax.numpy as jnp
        import numpy as np
        K = 6
        VOCAB = 5
        HIDDEN = 128
        B, L = input_ids.shape
        w = (VOCAB ** np.arange(K - 1, -1, -1)).astype(np.int32)
        pad_l = (K - 1) // 2
        pad_r = K - 1 - pad_l
        xp = jnp.pad(input_ids, ((0, 0), (pad_l, pad_r)))
        idx = sum((int(w[j]) * xp[:, j:j + L] for j in range(K)))
        return table[idx]

    def _L0_attn_ref(x, w_qkv, w_proj, b_proj):
        import jax, jax.numpy as jnp
        import numpy as np
        EMBED_DIM = 128
        NUM_HEADS = 8
        HEAD_DIM = EMBED_DIM // NUM_HEADS
        B, N, C = x.shape
        H, D = (NUM_HEADS, HEAD_DIM)
        scale = D ** (-0.5)
        qkv = jnp.einsum('bnc,fc->bnf', x, w_qkv)
        qkv = qkv.reshape(B, N, 3, H, D)
        q, k, v = [jnp.transpose(qkv[:, :, i], (0, 2, 1, 3)) for i in range(3)]
        attn = jnp.einsum('bhnd,bhmd->bhnm', q, k) * scale
        causal = jnp.triu(jnp.full((N, N), -jnp.inf, dtype=attn.dtype), k=1)
        attn = jax.nn.softmax(attn + causal, axis=-1)
        out = jnp.einsum('bhnm,bhmd->bhnd', attn, v)
        out = jnp.transpose(out, (0, 2, 1, 3)).reshape(B, N, C)
        return jnp.einsum('bnc,oc->bno', out, w_proj) + b_proj

    def _L0_ffn_ref(x, router_w, router_b, w1, b1, w2, b2):
        import jax, jax.numpy as jnp
        import numpy as np
        from jax import lax
        N_EXPERTS = 16
        TOP_K = 2
        D_MODEL = 128
        D_FF = 512
        B, S, D = x.shape
        xt = x.reshape(-1, D)
        logits = xt @ router_w.T + router_b
        probs = jax.nn.softmax(logits, axis=-1)
        topk_p, topk_i = lax.top_k(probs, TOP_K)
        onehot = jax.nn.one_hot(topk_i, N_EXPERTS, dtype=probs.dtype)
        gates = jnp.sum(onehot * topk_p[..., None], axis=1)

        def expert_step(acc, packed):
            w1e, b1e, w2e, b2e, ge = packed
            h = jax.nn.gelu(xt @ w1e.T + b1e, approximate=False)
            y = h @ w2e.T + b2e
            return (acc + y * ge[:, None], None)
        out, _ = lax.scan(expert_step, jnp.zeros_like(xt), (w1, b1, w2, b2, gates.T))
        return out.reshape(B, S, D)

    def _L1_attn_ref(x, w_qkv, w_out, b_out):
        import jax, jax.numpy as jnp
        import numpy as np
        import math
        B, S, H = (2, 1024, 128)
        NUM_HEADS = 8
        HEAD_DIM = H // NUM_HEADS
        RECENCY_DECAY = 0.9
        batch, seq_len, hidden = x.shape
        nh, hd = (NUM_HEADS, HEAD_DIM)
        qkv = jnp.einsum('bsh,oh->bso', x, w_qkv)
        qkv = qkv.reshape(batch, seq_len, 3, nh, hd)
        q, k, v = jnp.transpose(qkv, (2, 0, 3, 1, 4))
        attn = jnp.einsum('bhqd,bhkd->bhqk', q, k) / math.sqrt(hd)
        pos = jnp.arange(seq_len)[None, :] - jnp.arange(seq_len)[:, None]
        bias = jnp.where(pos <= 0, pos.astype(jnp.float32) * math.log(RECENCY_DECAY), jnp.zeros((), dtype=jnp.float32))
        attn = jax.nn.softmax(attn + bias[None, None, :, :], axis=-1)
        out = jnp.einsum('bhqk,bhkd->bqhd', attn, v).reshape(batch, seq_len, hidden)
        return jnp.einsum('bsh,oh->bso', out, w_out) + b_out

    def _L1_ffn_ref(x, gate_w, gate_b, shared_w1, shared_b1, shared_w2, shared_b2, shared_act, expert_w1, expert_b1, expert_w2, expert_b2, expert_act):
        import jax, jax.numpy as jnp
        import numpy as np
        B, S, D = (4, 512, 128)
        I = 96
        E = 16
        K = 2

        def _inv_softplus(v):
            return float(np.log(np.expm1(v)))

        def swiglu5(h, alpha, gate_scale, up_shift, gate_clamp_raw, up_clamp_raw):
            gate_clamp = jax.nn.softplus(gate_clamp_raw)
            up_clamp = jax.nn.softplus(up_clamp_raw)
            g = jnp.clip(h[..., ::2], -gate_clamp, gate_clamp)
            u = jnp.clip(h[..., 1::2], -up_clamp, up_clamp)
            return g * jax.nn.sigmoid(g * alpha) * gate_scale * (u + up_shift)
        shape = x.shape
        xf = x.reshape(-1, shape[-1])
        h = xf @ shared_w1 + shared_b1
        t = swiglu5(h, shared_act[0], shared_act[1], shared_act[2], shared_act[3], shared_act[4])
        z = t @ shared_w2 + shared_b2
        gate_logits = xf @ gate_w + gate_b
        gate_probs = jax.nn.softmax(gate_logits, -1)
        w, idx = jax.lax.top_k(gate_probs, K)
        w = w / jnp.sum(w, axis=-1, keepdims=True)
        cw = jnp.sum(jax.nn.one_hot(idx, E, dtype=xf.dtype) * w[..., None], axis=1)
        he = jnp.einsum('nd,edh->enh', xf, expert_w1) + expert_b1[:, None, :]
        a = expert_act
        te = swiglu5(he, a[:, 0, None, None], a[:, 1, None, None], a[:, 2, None, None], a[:, 3, None, None], a[:, 4, None, None])
        oe = jnp.einsum('enh,ehd->end', te, expert_w2) + expert_b2[:, None, :]
        y = jnp.einsum('ne,end->nd', cw, oe)
        return (y + z).reshape(shape)
    h = _L0_tok_ref(x, L0_tok_table)
    h = h + _L0_attn_ref(_layernorm(h, axis=-1), L0_attn_w_qkv, L0_attn_w_proj, L0_attn_b_proj)
    h = h + _L0_ffn_ref(_layernorm(h, axis=-1), L0_ffn_router_w, L0_ffn_router_b, L0_ffn_w1, L0_ffn_b1, L0_ffn_w2, L0_ffn_b2)
    h = h + _L1_attn_ref(_layernorm(h, axis=-1), L1_attn_w_qkv, L1_attn_w_out, L1_attn_b_out)
    h = h + _L1_ffn_ref(_layernorm(h, axis=-1), L1_ffn_gate_w, L1_ffn_gate_b, L1_ffn_shared_w1, L1_ffn_shared_b1, L1_ffn_shared_w2, L1_ffn_shared_b2, L1_ffn_shared_act, L1_ffn_expert_w1, L1_ffn_expert_b1, L1_ffn_expert_w2, L1_ffn_expert_b2, L1_ffn_expert_act)
    return h

_drawn_inputs = setup_inputs


def setup_inputs(seed=0):
    import zlib

    import numpy as np

    out = dict(_drawn_inputs(seed))
    spreads = {'L1_attn_b_out': (0.0, 0.1),
     'L1_ffn_gate_b': (0.0, 0.1),
     'L1_ffn_shared_b1': (0.0, 0.8),
     'L1_ffn_shared_b2': (0.0, 0.1),
     'L1_ffn_expert_b1': (0.0, 0.8),
     'L1_ffn_expert_b2': (0.0, 0.1)}
    factors = {'L0_ffn_router_b': 4.569,
     'L0_ffn_b1': 8.0,
     'L0_ffn_b2': 7.169,
     'L1_ffn_expert_w1': 3.617,
     'L1_ffn_expert_w2': 3.263}
    for name, (base, spread) in spreads.items():
        noise = np.random.default_rng([zlib.crc32(name.encode()), seed]).standard_normal(out[name].shape)
        drawn = base * np.exp(spread * noise) if base else spread * noise
        out[name] = jnp.asarray(drawn.astype(out[name].dtype))
    for name, factor in factors.items():
        out[name] = (out[name] * factor).astype(out[name].dtype)
    return out
```

```python
from contextlib import ExitStack
import math

import numpy as np

import concourse.bass as bass
from concourse import mybir

F32 = mybir.dt.float32
BF16 = mybir.dt.bfloat16
I32 = mybir.dt.int32
ALU = mybir.AluOpType
ACT = mybir.ActivationFunctionType
AX = mybir.AxisListType

P = 128
D = 128
BATCH, SEQ = 4, 512
TPB = SEQ // P
NT = BATCH * TPB
TOK = BATCH * SEQ
H, HD = 8, 16
GH = 4
NG = H // GH
E = 16
NE1 = E + 1
DFF = 512
FC = DFF // P
I1 = 96
KMER, VOCAB = 6, 5
EPS = 1e-5
UNITS = H * TPB
TILES = 48
PAIRS = 2 * TOK
SLOTS = TILES * P
DECAY = -math.log(0.9)
MASKED = -1.0e30

BLOCKS_Q = (0, 0, 0, 1, 1, 2)
BLOCKS_K = (0, 1, 2, 0, 1, 0)
R_DOT = len(BLOCKS_Q) * HD
R_MAX = R_DOT + 3
R_ALL = R_MAX + 4

FC_IDENT, FC_SEL = 0, 128
FC_RANK, FC_J128, FC_IOTA = 256, 272, 288
FC_A128, FC_TILE, FC_TRASH = 416, 464, 512
FC_KT, FC_PART, FC_POW, FC_END = 560, 592, 593, 597
BC_IDENT, BC_CAUSAL_Q, BC_CAUSAL_K, BC_PAST_Q, BC_PAST_K, BC_TRI, BC_ONES, BC_END = range(8)


class Memory:
    pass


def clear_semaphores(nc, sems):
    for s in sems:
        nc.gpsimd.sem_clear(s)
    nc.all_engine_barrier()


def embed_phase(nc, m):
    with ExitStack() as ctx:
        ids = ctx.enter_context(nc.sbuf_tensor("ids", [BATCH, SEQ + KMER - 1], I32))
        idx = ctx.enter_context(nc.sbuf_tensor("idx", [BATCH, KMER, SEQ], F32))
        idx_col = ctx.enter_context(nc.sbuf_tensor("idx_col", [P, BATCH, TPB], I32))
        sems = []

        def sem(name):
            sems.append(ctx.enter_context(nc.semaphore(name)))
            return sems[-1]

        consts_in, ids_in = sem("e_consts_in"), sem("e_ids_in")
        ids_zero, horner = sem("e_ids_zero"), sem("e_horner")
        idx_turned, idx_ready, rows_in = sem("e_idx_turned"), sem("e_idx_ready"), m.rows_in
        turned = m.bank[0]
        ctx.callback(clear_semaphores, nc, sems)
        block = ctx.enter_context(nc.Block())

        @block.sync
        def _(sp):
            sp.wait_ge(ids_zero, 1)
            sp.dma_start(ids[:, 2:2 + SEQ], m.x).then_inc(ids_in, 16)
            sp.dma_start(m.fconst[:, :], m.fconst_d).then_inc(consts_in, 16)
            sp.dma_start(m.bconst[:, :, :], m.bconst_d).then_inc(m.bconst_in, 16)
            for layer in range(2):
                for g in range(NG):
                    sp.dma_start(m.w_o[:, layer, g, :], m.w_o_d[layer][g]).then_inc(m.attn_w_in, 16)
                sp.dma_start(m.w_qkv[:, layer, :], m.w_qkv_d[layer]).then_inc(m.attn_w_in, 16)
            sp.dma_start(m.router_w[:, :, :], m.router_w_d).then_inc(m.attn_w_in, 16)
            for layer in range(2):
                sp.dma_start(m.router_b[:, layer, :],
                             m.router_b_d[layer].partition_broadcast(P)).then_inc(m.attn_w_in, 16)
            for e in range(0, E, 4):
                sp.dma_start(m.w1[:, e * DFF:(e + 4) * DFF], m.w1_d[:, e * DFF:(e + 4) * DFF]).then_inc(m.experts_in, 16)
                sp.dma_start(m.w2[:, e * DFF:(e + 4) * DFF], m.w2_d[:, e * DFF:(e + 4) * DFF]).then_inc(m.experts_in, 16)
            sp.dma_start(m.b1[:, :], m.b1_d).then_inc(m.experts_in, 16)
            sp.dma_start(m.b2[:, :], m.b2_d.partition_broadcast(P)).then_inc(m.experts_in, 16)

        @block.gpsimd
        def _(pool):
            pool.wait_ge(idx_ready, 1)
            for t in range(NT):
                pool.indirect_dma_start(
                    m.h[:, t, :], None, m.table,
                    bass.IndirectOffsetOnAxis(ap=idx_col[:, t // TPB, t % TPB:t % TPB + 1], axis=0)
                ).then_inc(rows_in, 16)
            pool.wait_ge(rows_in, 16 * NT)

        @block.vector
        def _(dve):
            nc.vector.memset(ids[:, :], 0).then_inc(ids_zero, 1)
            dve.wait_ge(ids_in, 16)
            nc.vector.scalar_tensor_tensor(idx[:, 1, :], ids[:, 0:SEQ], float(VOCAB), ids[:, 1:1 + SEQ],
                                           ALU.mult, ALU.add).then_inc(horner, 1)
            for j in range(2, KMER):
                dve.wait_ge(horner, j - 1)
                nc.vector.scalar_tensor_tensor(idx[:, j, :], idx[:, j - 1, :], float(VOCAB), ids[:, j:j + SEQ],
                                               ALU.mult, ALU.add).then_inc(horner, 1)
            dve.wait_ge(idx_turned, 1)
            nc.vector.tensor_copy(idx_col[:, :, :],
                                  turned[:, 0:NT].rearrange("p (c b) -> p b c", b=BATCH)).then_inc(idx_ready, 1)

        @block.tensor
        def _(pe):
            pe.wait_ge(consts_in, 16)
            pe.wait_ge(horner, KMER - 1)
            for c in range(TPB):
                last = nc.tensor.transpose(turned[:, c * BATCH:(c + 1) * BATCH],
                                           idx[:, KMER - 1, c * P:(c + 1) * P],
                                           m.fconst[0:BATCH, FC_IDENT:FC_IDENT + BATCH])
            last.then_inc(idx_turned, 1)


def layer_norm_stats(nc, link, h, stats, moments):
    for t in range(TPB):
        last = nc.vector.bn_stats(stats[:, t, :], h[:, t, :])
    link(last)
    for t in range(TPB):
        last = nc.vector.bn_aggr(moments[:, t, :], stats[:, t, :])
    return last


def inverse_std(nc, pool, m, moments, var_eps, inv_std, var_eps_ready, b):
    nc.gpsimd.tensor_scalar(var_eps[:, :], moments[:, :, 1], EPS, None, ALU.add).then_inc(var_eps_ready, 1)
    pool.wait_ge(var_eps_ready, b + 1)
    return nc.gpsimd.tensor_tensor(inv_std[:, :], var_eps[:, :], m.fconst[:, FC_POW:FC_POW + TPB], ALU.pow)


def layer_norm_apply(nc, h, moments, inv_std, out):
    for t in range(TPB):
        last = nc.vector.tensor_scalar(out[:, t, :], h[:, t, :], moments[:, t, 0:1], inv_std[:, t:t + 1],
                                       ALU.subtract, ALU.mult)
    return last


def attention_phase(nc, m, layer):
    causal = layer == 0
    q_scale = 1.0 if causal else HD ** -0.5 / DECAY
    exp_scale = HD ** -0.5 if causal else DECAY
    diag_q, diag_k = (BC_CAUSAL_Q, BC_CAUSAL_K) if causal else (BC_PAST_Q, BC_PAST_K)
    n_loads = 2 * len(BLOCKS_Q) + 1
    STEPS = BATCH + 2

    uses_a = [("x", 0), ("v", 0)]
    uses_b = [("q", 0)]
    uses_c = [("k", 0)]
    for s in range(STEPS):
        if 0 <= s - 1 < BATCH:
            uses_a.append(("max", s - 1, 1))
        if 0 <= s - 2:
            uses_b.append(("sum", s - 2, 1))
            uses_c.append(("y", s - 2))
        if s + 1 < BATCH:
            uses_a += [("x", s + 1), ("v", s + 1)]
            uses_b.append(("q", s + 1))
            uses_c.append(("k", s + 1))
        if s < BATCH:
            uses_a.append(("max", s, 0))
        if 0 <= s - 1 < BATCH:
            uses_b.append(("sum", s - 1, 0))
    nth_a = {key: n for n, key in enumerate(uses_a)}
    nth_b = {key: n for n, key in enumerate(uses_b)}
    nth_c = {key: n for n, key in enumerate(uses_c)}

    with ExitStack() as ctx:
        def sb(name, shape, dt=F32):
            return ctx.enter_context(nc.sbuf_tensor(f"{name}_{layer}", shape, dt))

        sems = []

        def sem(name):
            sems.append(ctx.enter_context(nc.semaphore(f"a{layer}_{name}")))
            return sems[-1]

        stats, moments = sb("stats", [P, TPB, 6]), sb("moments", [P, TPB, 2])
        var_eps, inv_std = sb("var_eps", [P, TPB]), sb("inv_std", [P, TPB])
        xn, x_t = sb("xn", [P, TPB, D]), sb("x_t", [P, SEQ])
        q_pack, k_pack = sb("q_pack", [P, 3, H, SEQ], BF16), sb("k_pack", [P, 3, H, SEQ], BF16)
        v_ext = sb("v_ext", [P, 3, TPB, H, 2 * HD])
        parts = {"q": sb("q_parts", [P, 3, SEQ], BF16), "k": sb("k_parts", [P, 3, SEQ], BF16)}
        rest = {"q": sb("q_rest", [P, SEQ]), "k": sb("k_rest", [P, SEQ])}
        neg_max, max_rest = sb("neg_max", [P, NG, UNITS // NG]), sb("max_rest", [P, NG, UNITS // NG])
        max_parts = sb("max_parts", [P, NG, 3, UNITS // NG], BF16)
        max_rows = sb("max_rows", [3 * UNITS // NG, NG, P], BF16)
        probs = sb("probs", [P, 8, SEQ])
        inv_sums = sb("inv_sums", [P, SEQ])
        o_raw, o_norm = sb("o_raw", [P, NG, SEQ]), sb("o_norm", [P, NG, SEQ])

        bank_q = m.bank[0:2]
        bank_k = m.bank[2:4]
        bank_o = m.bank[4]
        bank_a, bank_b, bank_c = m.bank[5:8]

        dve_chain = sem("dve_chain")
        pack_rows_in, v_ext_zero = sem("pack_rows_in"), sem("v_ext_zero")
        var_eps_ready = sem("var_eps_ready")
        moments_ready, inv_std_ready, xn_ready = sem("moments_ready"), sem("inv_std_ready"), sem("xn_ready")
        a_filled, b_filled, c_filled = sem("a_filled"), sem("b_filled"), sem("c_filled")
        a_read, b_read, c_read = sem("a_read"), sem("b_read"), sem("c_read")
        high_ready, mid_ready, low_ready = sem("high_ready"), sem("mid_ready"), sem("low_ready")
        parts_out = sem("parts_out")
        pack_in = [sem("pack_in_even"), sem("pack_in_odd")]
        q_scores, q_scores_read = sem("q_scores"), sem("q_scores_read")
        max_parts_ready, max_in = sem("max_parts_ready"), [sem("max_in_0"), sem("max_in_1")]
        k_scores, probs_ready, pv_done = sem("k_scores"), sem("probs_ready"), sem("pv_done")
        o_read, o_normed = sem("o_read"), sem("o_normed")
        ctx.callback(clear_semaphores, nc, sems)
        block = ctx.enter_context(nc.Block())

        @block.sync
        def _(sp):
            if layer == 1:
                for j, (dest, src) in enumerate(m.second_experts):
                    sp.dma_start(dest, src).then_inc(m.experts2_in, 16)

            def pack(b):
                for n, name in enumerate("qk"):
                    sp.wait_ge(high_ready, 2 * b + n + 1)
                    sp.wait_ge(mid_ready, 2 * b + n + 1)
                    sp.wait_ge(low_ready, 2 * b + n + 1)
                    sp.dma_start(m.parts_d[b, n].rearrange("s h d t -> (h d) s t"),
                                 parts[name][:, :, :]).then_inc(parts_out, 16)
                if b == 0:
                    sp.wait_ge(pack_rows_in, 16 * 6)
                if b >= 3:
                    sp.wait_ge(pv_done, (b - 2) * UNITS // GH)
                sp.wait_ge(parts_out, 32 * (b + 1))
                for n, (dest, blocks) in enumerate(((q_pack, BLOCKS_Q), (k_pack, BLOCKS_K))):
                    for i, part in enumerate(blocks):
                        sp.dma_start(dest[i * HD:(i + 1) * HD, b % 3, :, :],
                                     m.parts_d[b, n, part].rearrange("h d t -> d h t")
                                     ).then_inc(pack_in[b % 2], 16)
                sp.dma_start(q_pack[R_DOT:R_MAX, b % 3, :, :],
                             m.q_rows_d[0:3].unsqueeze(1).to_broadcast([3, H, SEQ])).then_inc(pack_in[b % 2], 16)

            def max_to_rows(b, g):
                sp.wait_ge(a_read, nth_a["max", b, g] + 1)
                sp.wait_ge(q_scores, b * UNITS + (g + 1) * UNITS // NG)
                for s in range(3):
                    sp.dma_start(q_pack[R_DOT + s:R_DOT + s + 1, b % 3, g * GH:(g + 1) * GH, :],
                                 max_rows[s * 16:(s + 1) * 16, g, :]).then_inc(max_in[g], 16)

            for buf in range(3):
                for pack_buf, rows in ((k_pack, m.k_rows_d), (q_pack, m.q_rows_d)):
                    sp.dma_start(pack_buf[R_DOT:R_ALL, buf, :, :],
                                 rows.unsqueeze(1).to_broadcast([R_ALL - R_DOT, H, SEQ])
                                 ).then_inc(pack_rows_in, 16)
            pack(0)
            for s in range(STEPS):
                if 0 <= s - 1 < BATCH:
                    max_to_rows(s - 1, 1)
                if s + 1 < BATCH:
                    pack(s + 1)
                if s < BATCH:
                    max_to_rows(s, 0)

        @block.gpsimd
        def _(pool):
            for b in range(BATCH):
                pool.wait_ge(moments_ready, b + 1)
                inverse_std(nc, pool, m, moments, var_eps, inv_std, var_eps_ready, b).then_inc(inv_std_ready, 1)
                for n, name in enumerate("qk"):
                    if name == "q":
                        pool.wait_ge(b_read, nth_b["q", b] + 1)
                    else:
                        pool.wait_ge(c_read, nth_c["k", b] + 1)
                    if b:
                        pool.wait_ge(parts_out, 32 * b)
                    nc.gpsimd.tensor_copy(parts[name][:, 1, :], rest[name][:, :]).then_inc(mid_ready, 1)
                    pool.wait_ge(mid_ready, 2 * b + n + 1)
                    nc.gpsimd.tensor_tensor(parts[name][:, 2, :], rest[name][:, :], parts[name][:, 1, :],
                                            ALU.subtract).then_inc(low_ready, 1)

        @block.scalar
        def _(act):
            def take_x(b):
                act.wait_ge(a_filled, nth_a["x", b] + 1)
                if b:
                    act.wait_ge(c_filled, nth_c["k", b - 1] + 1)
                    act.wait_ge(a_filled, nth_a["v", b - 1] + 1)
                nc.scalar.activation(x_t[:, :], bank_a[:, :], ACT.Copy).then_inc(a_read, 1)

            def take_projections(b):
                for n, (name, bank, filled, nth) in enumerate((("q", bank_b, b_filled, nth_b),
                                                               ("k", bank_c, c_filled, nth_c))):
                    act.wait_ge(filled, nth[name, b] + 1)
                    if b:
                        act.wait_ge(parts_out, 32 * b)
                    nc.scalar.activation(parts[name][:, 0, :], bank[:, :], ACT.Copy,
                                         scale=q_scale if name == "q" else 1.0).then_inc(high_ready, 1)
                act.wait_ge(a_filled, nth_a["v", b] + 1)
                if b == 0:
                    act.wait_ge(v_ext_zero, 6)
                if b >= 3:
                    act.wait_ge(pv_done, (b - 2) * UNITS // GH)
                nc.scalar.activation(v_ext[:, b % 3, :, :, 0:HD],
                                     bank_a[:, :].rearrange("p (t h d) -> p t h d", t=TPB, h=H),
                                     ACT.Copy).then_inc(a_read, 1)

            def take_max_rows(b, g):
                act.wait_ge(a_filled, nth_a["max", b, g] + 1)
                if b:
                    act.wait_ge(max_in[g], 48 * b)
                nc.scalar.activation(max_rows[:, g, :], bank_a[0:48, 0:P // 2].bitcast(BF16),
                                     ACT.Copy).then_inc(a_read, 1)

            def exponential(b, u):
                n = b * UNITS + u
                ki = (u // GH) % TPB
                first = ki * P if causal else 0
                act.wait_ge(k_scores, n + 1)
                if n >= 8:
                    act.wait_ge(pv_done, (n - 8) // GH + 1)
                nc.scalar.activation(probs[:, n % 8, first:], bank_k[n % 2][:, first:], ACT.Exp,
                                     scale=exp_scale).then_inc(probs_ready, 1)

            def take_output(b, g):
                act.wait_ge(pv_done, (b * NG + g + 1) * TPB)
                if b:
                    act.wait_ge(o_normed, (b - 1) * NG + g + 1)
                nc.scalar.activation(o_raw[:, g, :], bank_o[:, :], ACT.Copy).then_inc(o_read, 1)

            take_x(0)
            take_projections(0)
            for s in range(STEPS):
                for u in range(UNITS):
                    if u == 3 and 0 <= s - 1 < BATCH:
                        take_max_rows(s - 1, 1)
                    if u == 5 and s + 1 < BATCH:
                        take_x(s + 1)
                    if u == 8 and s + 1 < BATCH:
                        take_projections(s + 1)
                    if u == 19 and s < BATCH:
                        take_max_rows(s, 0)
                    if u == 18 and 0 <= s - 1 < BATCH:
                        take_output(s - 1, 0)
                    if 0 <= s - 1 < BATCH:
                        exponential(s - 1, u)
                if 0 <= s - 1 < BATCH:
                    take_output(s - 1, 1)

        @block.vector
        def _(dve):
            chain = [0]

            def link(ins):
                chain[0] += 1
                ins.then_inc(dve_chain, 1)
                dve.wait_ge(dve_chain, chain[0])

            def norm(b):
                if b:
                    dve.wait_ge(a_filled, nth_a["x", b - 1] + 1)
                h = m.h[:, b * TPB:(b + 1) * TPB, :]
                layer_norm_stats(nc, link, h, stats, moments).then_inc(moments_ready, 1)
                dve.wait_ge(inv_std_ready, b + 1)
                layer_norm_apply(nc, h, moments, inv_std, xn).then_inc(xn_ready, 1)

            def split(b):
                for n, (name, bank, read) in enumerate((("q", bank_b, b_read), ("k", bank_c, c_read))):
                    dve.wait_ge(high_ready, 2 * b + n + 1)
                    if b:
                        dve.wait_ge(low_ready, 2 * (b - 1) + n + 1)
                    nc.vector.scalar_tensor_tensor(rest[name][:, :], bank[:, :], q_scale if name == "q" else 1.0,
                                                   parts[name][:, 0, :], ALU.mult, ALU.subtract
                                                   ).then_inc(read, 1)

            def row_max(b, u):
                n = b * UNITS + u
                width = (u % TPB + 1) * P if causal else SEQ
                g, col = u // (UNITS // NG), u % (UNITS // NG)
                dve.wait_ge(q_scores, n + 1)
                if u == 0 and b:
                    dve.wait_ge(max_parts_ready, 2 * b)
                nc.vector.tensor_reduce(neg_max[:, g, col:col + 1], bank_q[n % 2][:, 0:width], AX.X, ALU.max,
                                        negate=True).then_inc(q_scores_read, 1)

            def split_max(b, g):
                dve.wait_ge(q_scores_read, b * UNITS + (g + 1) * UNITS // NG)
                if b:
                    dve.wait_ge(a_filled, nth_a["max", b - 1, g] + 1)
                link(nc.vector.tensor_copy(max_parts[:, g, 0, :], neg_max[:, g, :]))
                link(nc.vector.tensor_tensor(max_rest[:, g, :], neg_max[:, g, :], max_parts[:, g, 0, :], ALU.subtract))
                link(nc.vector.tensor_copy(max_parts[:, g, 1, :], max_rest[:, g, :]))
                nc.vector.tensor_tensor(max_parts[:, g, 2, :], max_rest[:, g, :], max_parts[:, g, 1, :],
                                        ALU.subtract).then_inc(max_parts_ready, 1)

            def normalize(b, g):
                dve.wait_ge(b_filled, nth_b["sum", b, g] + 1)
                if b:
                    dve.wait_ge(c_filled, nth_c["y", b - 1] + 1)
                if b + g:
                    dve.wait_ge(o_normed, b * NG + g)
                nc.vector.reciprocal(inv_sums[:, :], bank_b[:, :]).then_inc(b_read, 1)
                dve.wait_ge(b_read, nth_b["sum", b, g] + 1)
                nc.vector.tensor_tensor(o_norm[:, g, :], o_raw[:, g, :], inv_sums[:, :], ALU.mult).then_inc(o_normed, 1)

            def add_output(b):
                dve.wait_ge(c_filled, nth_c["y", b] + 1)
                rows = m.h[:, b * TPB:(b + 1) * TPB, :]
                nc.vector.tensor_tensor(rows, rows, bank_c[:, :].rearrange("p (t d) -> p t d", t=TPB),
                                        ALU.add).then_inc(c_read, 1)

            norm(0)
            for buf in range(3):
                nc.vector.memset(v_ext[:, buf, :, :, HD:2 * HD], 0.0).then_inc(v_ext_zero, 1)
            for buf in range(3):
                dve.wait_ge(v_ext_zero, buf + 1)
                nc.vector.memset(v_ext[:, buf, :, :, HD:HD + 1], 1.0).then_inc(v_ext_zero, 1)
            split(0)
            for s in range(STEPS):
                for u in range(UNITS):
                    if u == 1 and s + 1 < BATCH:
                        norm(s + 1)
                    if u == 4 and 0 <= s - 2:
                        normalize(s - 2, 1)
                    if u == 6 and 0 <= s - 2:
                        add_output(s - 2)
                    if u == 8 and s + 1 < BATCH:
                        split(s + 1)
                    if u == 17 and s < BATCH:
                        split_max(s, 0)
                    if u == 21 and 0 <= s - 1 < BATCH:
                        normalize(s - 1, 0)
                    if s < BATCH:
                        row_max(s, u)
                if s < BATCH:
                    split_max(s, 1)

        @block.tensor
        def _(pe):
            ident = m.fconst[:, FC_IDENT:FC_IDENT + P]
            ident_bf = m.bconst[:, BC_IDENT, :]

            def free(read, nth, key):
                if nth[key]:
                    pe.wait_ge(read, nth[key])

            def turn_x(b):
                pe.wait_ge(xn_ready, b + 1)
                free(a_read, nth_a, ("x", b))
                for t in range(TPB):
                    last = nc.tensor.transpose(bank_a[:, t * P:(t + 1) * P], xn[:, t, :], ident)
                last.then_inc(a_filled, 1)

            def project(b):
                pe.wait_ge(a_read, nth_a["x", b] + 1)
                w = m.w_qkv[:, layer, :]
                free(b_read, nth_b, ("q", b))
                nc.tensor.matmul(bank_b[:, :], w[:, 0:D], x_t[:, :], start=True, stop=True).then_inc(b_filled, 1)
                free(c_read, nth_c, ("k", b))
                nc.tensor.matmul(bank_c[:, :], w[:, D:2 * D], x_t[:, :], start=True, stop=True).then_inc(c_filled, 1)
                for t in range(TPB):
                    last = nc.tensor.matmul(bank_a[:, t * P:(t + 1) * P], x_t[:, t * P:(t + 1) * P],
                                            w[:, 2 * D:3 * D], start=True, stop=True)
                last.then_inc(a_filled, 1)

            def score_q(b, u):
                n, h, qi = b * UNITS + u, u // TPB, u % TPB
                if u == 0:
                    pe.wait_ge(pack_in[b % 2], 16 * n_loads * (b // 2 + 1))
                if n >= 2:
                    pe.wait_ge(q_scores_read, n - 1)
                q = q_pack[:, b % 3, h, qi * P:(qi + 1) * P]
                k = k_pack[:, b % 3, h, :]
                out = bank_q[n % 2]
                lo = qi * P
                if causal:
                    nc.tensor.matmul(out[:, 0:lo + P], q[0:R_DOT], k[0:R_DOT, 0:lo + P], start=True, stop=False,
                                     skip_group_check=True)
                else:
                    if qi:
                        nc.tensor.matmul(out[:, 0:lo], q[0:R_ALL], k[0:R_ALL, 0:lo], start=True, stop=True,
                                         skip_group_check=True)
                    nc.tensor.matmul(out[:, lo:], q[0:R_DOT], k[0:R_DOT, lo:], start=True, stop=False,
                                     skip_group_check=True)
                nc.tensor.matmul(out[:, lo:lo + P], ident_bf, m.bconst[:, diag_q, :], start=False, stop=True,
                                 skip_group_check=True).then_inc(q_scores, 1)

            def turn_max(b, g):
                pe.wait_ge(max_parts_ready, b * NG + g + 1)
                free(a_read, nth_a, ("max", b, g))
                nc.tensor.transpose(bank_a[0:48, 0:P // 2].bitcast(BF16),
                                    max_parts[:, g, :, :].rearrange("p s c -> p (s c)"), ident_bf).then_inc(a_filled, 1)

            def score_k(b, u):
                n, h, ki = b * UNITS + u, (u // (GH * TPB)) * GH + u % GH, (u // GH) % TPB
                if u % (UNITS // NG) == 0:
                    pe.wait_ge(max_in[u // (UNITS // NG)], 48 * (b + 1))
                if n >= 2:
                    pe.wait_ge(probs_ready, n - 1)
                k = k_pack[:, b % 3, h, ki * P:(ki + 1) * P]
                q = q_pack[:, b % 3, h, :]
                out = bank_k[n % 2]
                lo = ki * P
                if causal:
                    nc.tensor.matmul(out[:, lo:], k[0:R_MAX], q[0:R_MAX, lo:], start=True, stop=False,
                                     skip_group_check=True)
                else:
                    if lo + P < SEQ:
                        nc.tensor.matmul(out[:, lo + P:], k[0:R_ALL], q[0:R_ALL, lo + P:], start=True, stop=True,
                                         skip_group_check=True)
                    nc.tensor.matmul(out[:, 0:lo + P], k[0:R_MAX], q[0:R_MAX, 0:lo + P], start=True, stop=False,
                                     skip_group_check=True)
                nc.tensor.matmul(out[:, lo:lo + P], ident_bf, m.bconst[:, diag_k, :], start=False, stop=True,
                                 skip_group_check=True).then_inc(k_scores, 1)

            def times_v(b, pv):
                g, ki = pv // TPB, pv % TPB
                n = b * UNITS + pv * GH
                first = ki * P if causal else 0
                pe.wait_ge(probs_ready, n + GH)
                if ki == 0 and b * NG + g:
                    pe.wait_ge(o_read, b * NG + g)
                for j in range(GH):
                    last = nc.tensor.matmul(bank_o[32 * j:32 * j + 32, first:], v_ext[:, b % 3, ki, g * GH + j, :],
                                            probs[:, (n + j) % 8, first:], start=(ki == 0), stop=(ki == TPB - 1),
                                            skip_group_check=True)
                last.then_inc(pv_done, 1)

            def spread_sums(b, g):
                pe.wait_ge(o_read, b * NG + g + 1)
                free(b_read, nth_b, ("sum", b, g))
                nc.tensor.matmul(bank_b[:, :], m.fconst[:, FC_SEL:FC_SEL + P], o_raw[:, g, :], start=True,
                                 stop=True).then_inc(b_filled, 1)

            def project_out(b):
                pe.wait_ge(o_normed, (b + 1) * NG)
                free(c_read, nth_c, ("y", b))
                for t in range(TPB):
                    for g in range(NG):
                        last = nc.tensor.matmul(bank_c[:, t * P:(t + 1) * P], o_norm[:, g, t * P:(t + 1) * P],
                                                m.w_o[:, layer, g, :], start=(g == 0), stop=(g == NG - 1))
                last.then_inc(c_filled, 1)

            if layer == 0:
                pe.wait_ge(m.attn_w_in, 16 * 9)
                pe.wait_ge(m.bconst_in, 16)
            turn_x(0)
            project(0)
            for s in range(STEPS):
                for u in range(UNITS):
                    if u == 2 and 0 <= s - 1 < BATCH:
                        turn_max(s - 1, 1)
                    if u == 3 and 0 <= s - 2:
                        spread_sums(s - 2, 1)
                    if u == 4 and s + 1 < BATCH:
                        turn_x(s + 1)
                    if u == 5 and 0 <= s - 2:
                        project_out(s - 2)
                    if u == 7 and s + 1 < BATCH:
                        project(s + 1)
                    if u == 18 and s < BATCH:
                        turn_max(s, 0)
                    if u == 20 and 0 <= s - 1 < BATCH:
                        spread_sums(s - 1, 0)
                    if s < BATCH:
                        score_q(s, u)
                    if 0 <= s - 1 < BATCH:
                        score_k(s - 1, u)
                        if u % GH == 1 and u > GH:
                            times_v(s - 1, u // GH - 1)
                if 0 <= s - 1 < BATCH:
                    times_v(s - 1, UNITS // GH - 1)


def ring(off, n=4):
    return off % n, off // n


def moe_phase(nc, m, layer):
    first = layer == 0
    width = DFF if first else 2 * I1
    with ExitStack() as ctx:
        def sb(name, shape, dt=F32):
            return ctx.enter_context(nc.sbuf_tensor(f"{name}_m{layer}", shape, dt))

        sems = []

        def sem(name):
            sems.append(ctx.enter_context(nc.semaphore(f"m{layer}_{name}")))
            return sems[-1]

        stats, moments = sb("stats", [P, TPB, 6]), sb("moments", [P, TPB, 2])
        var_eps, inv_std = sb("var_eps", [P, TPB]), sb("inv_std", [P, TPB])
        xn, x_t = sb("xn", [P, 2, TPB, D]), sb("x_t", [P, 2, SEQ])
        logits, lower = sb("logits", [P, NT, E]), sb("lower", [P, NT, E])
        weighed, expd = sb("weighed", [P, NT, E]), sb("expd", [P, NT, E])
        chosen = sb("chosen", [P, 2, NT, E])
        top, rank = sb("top", [P, 2, NT]), sb("rank", [P, NT])
        gap, gap_exp, total = sb("gap", [P, NT]), sb("gap_exp", [P, NT]), sb("total", [P, NT])
        gate = sb("gate", [P, 2, NT])
        marks = sb("marks", [P, 2 * NT + 1, E], BF16)
        ranks = sb("ranks", [P, NT, E])
        over = sb("over", [P, E, NT])
        n_tiles, zeros_e, ends, starts = sb("n_tiles", [P, E]), sb("zeros_e", [P, E]), sb("ends", [P, E]), sb("starts", [P, E])
        pos, pos_i, row_i = sb("pos", [P, 2 * NT]), sb("pos_i", [P, 2 * NT], I32), sb("row_i", [P, 2 * NT], I32)
        row, tile128 = sb("row", [P, 2 * NT]), sb("tile128", [P, 2 * NT])
        row_hot = sb("row_hot", [P, 2 * NT, P], BF16)
        tile_hot = sb("tile_hot", [P, 2 * NT, 3, TILES], BF16)
        pair, wrap, pad = sb("pair", [P, TILES]), sb("wrap", [P, TILES]), sb("pad", [P, TILES])
        src_row, dst_row = sb("src_row", [P, TILES], I32), sb("dst_row", [P, TILES], I32)
        before, tile_expert = sb("before", [P, TILES, E]), sb("tile_expert", [P, TILES], I32)
        expert_f = sb("expert_f", [P, TILES])
        src_idx, dst_idx = sb("src_idx", [P, 4], I32), sb("dst_idx", [P, 4], I32)
        x_rows, y_rows = sb("x_rows", [P, 4, D]), sb("y_rows", [P, 4, D])
        xt = sb("xt", [P, 2, P])
        y_sel = sb("y_sel", [P, 2, 2, TPB, D])
        if first:
            h_pre, h_act = sb("h_pre", [P, 2, DFF]), sb("h_act", [P, 2, DFF])
            b1_now, b2_now = sb("b1_now", [P, 2, FC]), sb("b2_now", [P, 4, D])
        else:
            h_pre = sb("h_pre", [P, 2, I1, 2])
            g_cl, u_cl, g_al, sig = [sb(n, [P, 2, I1]) for n in ("g_cl", "u_cl", "g_al", "sig")]
            gu, te, te_t = sb("gu", [P, 2, I1]), sb("te", [P, 2, I1]), sb("te_t", [I1, 2, P])
            b2_now = sb("b2_now", [P, 4, D])
            soft = sb("soft", [P, 4, NE1, 2])
            s_g, s_u, s_sig = sb("s_g", [I1, 2, SEQ]), sb("s_u", [I1, 2, SEQ]), sb("s_sig", [I1, 2, SEQ])
            s_te = sb("s_te", [I1 + 1, 2, SEQ])

        bank_turn = m.bank[0:2]
        bank_logits, bank_rank, bank_pairs = m.bank[2], m.bank[3], m.bank[2]
        bank_up, bank_mid, bank_down = m.bank[2:4], m.bank[4:6], m.bank[6:8]

        dve_chain, pool_chain = sem("dve_chain"), sem("pool_chain")
        moments_ready, var_eps_ready, inv_std_ready = sem("moments_ready"), sem("var_eps_ready"), sem("inv_std_ready")
        xn_ready, xn_turned, x_t_ready = sem("xn_ready"), sem("xn_turned"), sem("x_t_ready")
        rows_out = [sem("rows_out_even"), sem("rows_out_odd")]
        logits_done, weighed_ready, expd_ready = sem("logits_done"), sem("weighed_ready"), sem("expd_ready")
        marks_ready, ranks_done = sem("marks_ready"), sem("ranks_done")
        pos_ready, row_hot_ready, tile_hot_ready = sem("pos_ready"), sem("row_hot_ready"), sem("tile_hot_ready")
        pairs_done, order_ready = sem("pairs_done"), sem("order_ready")
        idx_copied, x_in, y_out = sem("idx_copied"), m.x_in[layer], m.y_out[layer]
        turned, xt_ready, up_done = sem("turned"), sem("xt_ready"), sem("up_done")
        pre_ready, mid_turned, act_ready = sem("pre_ready"), sem("mid_turned"), sem("act_ready")
        bias_ready, down_done, y_ready = sem("bias_ready"), sem("down_done"), sem("y_ready")
        y_in, added, out_done = [sem("y_in_even"), sem("y_in_odd")], sem("added"), sem("out_done")
        if not first:
            soft_in, soft_ready = sem("soft_in"), sem("soft_ready")
            s_up, s_capped, s_clipped, s_sig_ready = sem("s_up"), sem("s_capped"), sem("s_clipped"), sem("s_sig_ready")
            s_te_ready, s_down, s_added, s_sum = sem("s_te_ready"), sem("s_down"), sem("s_added"), sem("s_sum")
            sig_asked, g_kept = sem("sig_asked"), sem("g_kept")
        if first:
            ctx.callback(clear_semaphores, nc, sems)
        block = ctx.enter_context(nc.Block())
        LOOPS = (TILES - 4) // 4

        @block.sync
        def _(sp):
            for b in range(BATCH):
                sp.wait_ge(xn_ready, b + 1)
                sp.dma_start(m.x_rows_d[b * SEQ:(b + 1) * SEQ, :].rearrange("(t p) d -> p t d", p=P),
                             xn[:, b % 2, :, :]).then_inc(rows_out[b % 2], 16)
            for r in range(4):
                sp.wait_ge(y_out[r], 16 * (TILES // 4))
            for b in range(BATCH):
                if b >= 2:
                    sp.wait_ge(added, b - 1)
                for k in range(2):
                    sp.dma_start(y_sel[:, b % 2, k, :, :],
                                 m.y_rows_d[k * TOK + b * SEQ:k * TOK + (b + 1) * SEQ, :].rearrange(
                                     "(t p) d -> p t d", p=P)).then_inc(y_in[b % 2], 16)
            if not first:
                for b in range(BATCH):
                    sp.wait_ge(added, b + 1)
                    sp.dma_start(m.out[b].rearrange("(t p) d -> p t d", p=P),
                                 m.h[:, b * TPB:(b + 1) * TPB, :]).then_inc(out_done, 16)
                sp.wait_ge(out_done, 16 * BATCH)

        @block.gpsimd
        def _(pool):
            chain = [0]

            def link(ins):
                chain[0] += 1
                ins.then_inc(pool_chain, 1)
                pool.wait_ge(pool_chain, chain[0])

            for b in range(BATCH):
                pool.wait_ge(moments_ready, b + 1)
                inverse_std(nc, pool, m, moments, var_eps, inv_std, var_eps_ready, b).then_inc(inv_std_ready, 1)
                if not first:
                    pool.wait_ge(s_capped, 2 * b + 2)
                    if b >= 2:
                        pool.wait_ge(s_te_ready, 2 * (b - 1))
                    for dest in (s_g, s_u):
                        last = nc.gpsimd.tensor_scalar(dest[:, b % 2, :], dest[:, b % 2, :],
                                                       soft[0:I1, 3, E, (0 if dest is s_g else 1):(1 if dest is s_g else 2)],
                                                       None, ALU.max)
                    last.then_inc(s_clipped, 1)

            def gather(i, off):
                r, rounds = ring(off)
                tile = i * 4 + off
                if off >= 4:
                    pool.wait_ge(turned, tile - 3)
                    pool.nop(nofuse=True)
                nc.gpsimd.tensor_copy(src_idx[:, r:r + 1], src_row[:, bass.ds(tile, 1)]).then_inc(idx_copied, 1)
                pool.wait_ge(idx_copied, tile + 1 if off < 4 else 2 * tile - 3)
                pool.nop(nofuse=True)
                pool.indirect_dma_start(x_rows[:, r, :], None, m.x_rows_d,
                                        bass.IndirectOffsetOnAxis(ap=src_idx[:, r:r + 1], axis=0)
                                        ).then_inc(x_in[r], 16)

            def scatter(i, off, last=False):
                r, rounds = ring(off)
                tile = i * 4 + off
                pool.wait_ge(y_ready, tile + 1)
                pool.nop(nofuse=True)
                nc.gpsimd.tensor_copy(dst_idx[:, r:r + 1], dst_row[:, bass.ds(tile, 1)]).then_inc(idx_copied, 1)
                pool.wait_ge(idx_copied, TILES + tile + 1 if last else 2 * tile + 6)
                pool.nop(nofuse=True)
                pool.indirect_dma_start(m.y_rows_d, bass.IndirectOffsetOnAxis(ap=dst_idx[:, r:r + 1], axis=0),
                                        y_rows[:, r, :], None).then_inc(y_out[r], 16)

            pool.wait_ge(order_ready, 3)
            for b in range(BATCH):
                pool.wait_ge(rows_out[b % 2], 16 * (b // 2 + 1))
            for off in range(4):
                gather(0, off)
            with pool.Fori(0, LOOPS) as i:
                for u in range(4):
                    gather(i, 4 + u)
                    scatter(i, u)
            for off in range(4):
                scatter(LOOPS, off, last=True)

        @block.scalar
        def _(act):
            if not first:
                act.wait_ge(soft_in, 1)
                nc.scalar.activation(soft[:, 1, :, :], soft[:, 0, :, :], ACT.Exp, scale=-1.0).then_inc(soft_ready, 1)
                act.wait_ge(soft_ready, 1)
                nc.scalar.activation(soft[:, 2, :, :], soft[:, 1, :, :], ACT.Ln, bias=1.0).then_inc(soft_ready, 1)
            for b in range(BATCH):
                act.wait_ge(xn_turned, b + 1)
                if b >= 2:
                    act.wait_ge(logits_done, b - 1)
                    if not first:
                        act.wait_ge(s_up, b - 1)
                nc.scalar.activation(x_t[:, b % 2, :], bank_turn[b % 2][:, :], ACT.Copy).then_inc(x_t_ready, 1)
                if not first:
                    act.wait_ge(s_clipped, b + 1)
                    if b >= 2:
                        act.wait_ge(s_te_ready, 2 * (b - 1))
                    nc.scalar.activation(s_sig[:, b % 2, :], s_g[:, b % 2, :], ACT.Sigmoid,
                                         scale=m.e_act[0:I1, E, 0:1]).then_inc(s_sig_ready, 1)
            act.wait_ge(weighed_ready, 1)
            nc.scalar.activation(expd[:, :, :], weighed[:, :, :], ACT.Exp).then_inc(expd_ready, 1)
            nc.scalar.activation(gap_exp[:, :], gap[:, :], ACT.Exp).then_inc(expd_ready, 1)
            act.wait_ge(order_ready, 3)
            nc.scalar.activation(gap[0:1, 0:1], gap_exp[0:1, 0:1], ACT.Gelu if first else ACT.Sigmoid)

            def hidden(i, off):
                tile = i * 4 + off
                act.wait_ge(mid_turned, tile + 1)
                act.wait_ge(bias_ready, tile + 1)
                for c in range(FC):
                    last = nc.scalar.activation(h_act[:, off % 2, c * P:(c + 1) * P],
                                                bank_mid[off % 2][:, c * P:(c + 1) * P], ACT.Gelu,
                                                bias=b1_now[:, off % 2, c:c + 1])
                last.then_inc(act_ready, 1)

            def take_x(i, off):
                tile = i * 4 + off
                act.wait_ge(turned, tile + 1)
                if off >= 2:
                    act.wait_ge(up_done, tile - 1)
                nc.scalar.activation(xt[:, off % 2, :], bank_turn[off % 2][:, 0:P], ACT.Copy).then_inc(xt_ready, 1)

            def take_mid(i, off):
                tile = i * 4 + off
                act.wait_ge(mid_turned, tile + 1)
                if off >= 2:
                    act.wait_ge(down_done, tile - 1)
                nc.scalar.activation(te_t[:, off % 2, :], bank_mid[off % 2][0:I1, 0:P], ACT.Copy).then_inc(act_ready, 1)

            def sigmoid(i, off):
                tile = i * 4 + off
                act.wait_ge(sig_asked, tile + 1)
                if off >= 2:
                    act.wait_ge(pre_ready, tile - 1)
                nc.scalar.activation(sig[:, off % 2, :], g_al[:, off % 2, :], ACT.Sigmoid).then_inc(g_kept, 1)

            if first:
                with act.Fori(0, TILES // 4) as i:
                    for u in range(4):
                        hidden(i, u)
            else:
                def step(i, off, x=True, mid=True, sg=True):
                    if x:
                        take_x(i, off + 1)
                    if mid:
                        take_mid(i, off - 1)
                    if sg:
                        sigmoid(i, off)

                take_x(0, 0)
                step(0, 0, mid=False)
                step(0, 1)
                with act.Fori(0, LOOPS) as i:
                    for u in range(4):
                        step(i, 2 + u)
                step(LOOPS, 2)
                step(LOOPS, 3, x=False)
                step(LOOPS, 4, x=False, sg=False)

        @block.vector
        def _(dve):
            chain = [0]

            def link(ins):
                chain[0] += 1
                ins.then_inc(dve_chain, 1)
                dve.wait_ge(dve_chain, chain[0])

            def over_tiles(ap):
                return ap.unsqueeze(2).to_broadcast([P, NT, E])

            def over_experts(ap):
                return ap.unsqueeze(1).to_broadcast([P, NT, E])

            def shared_front(b):
                dve.wait_ge(s_up, b + 1)
                if b >= 2:
                    dve.wait_ge(s_te_ready, 2 * (b - 1))
                for n, dest in enumerate((s_g, s_u)):
                    nc.vector.tensor_scalar(dest[:, b % 2, :], (bank_mid[n])[0:I1, :], m.s_b1[:, n:n + 1],
                                            soft[0:I1, 1, E, n:n + 1], ALU.add, ALU.min).then_inc(s_capped, 1)

            def shared_back(b):
                dve.wait_ge(s_sig_ready, b + 1)
                if b >= 2:
                    dve.wait_ge(s_down, b - 1)
                nc.vector.scalar_tensor_tensor(s_te[0:I1, b % 2, :], s_u[:, b % 2, :], m.e_act[0:I1, E, 2:3],
                                               s_g[:, b % 2, :], ALU.add, ALU.mult).then_inc(s_te_ready, 1)
                dve.wait_ge(s_te_ready, 2 * b + 1)
                nc.vector.scalar_tensor_tensor(s_te[0:I1, b % 2, :], s_te[0:I1, b % 2, :], m.e_act[0:I1, E, 1:2],
                                               s_sig[:, b % 2, :], ALU.mult, ALU.mult).then_inc(s_te_ready, 1)

            def shared_add(b):
                dve.wait_ge(s_down, b + 1)
                h = m.h[:, b * TPB:(b + 1) * TPB, :]
                nc.vector.tensor_tensor(h, h, bank_down[b % 2][:, :].rearrange("p (t d) -> p t d", t=TPB), ALU.add
                                        ).then_inc(s_added, 1)

            if not first:
                dve.wait_ge(m.experts_now, m.e_waits)
                link(nc.vector.tensor_scalar(soft[:, 3, :, :], m.e_act[:, :, 3:5], -1.0, None, ALU.mult))
                nc.vector.tensor_tensor(soft[:, 0, :, :], m.e_act[:, :, 3:5], soft[:, 3, :, :], ALU.max).then_inc(soft_in, 1)
                dve.wait_ge(soft_ready, 2)
                link(nc.vector.scalar_tensor_tensor(soft[:, 1, :, :], m.e_act[:, :, 3:5], 0.0, soft[:, 2, :, :],
                                                    ALU.max, ALU.add))
                link(nc.vector.tensor_scalar(soft[:, 3, :, :], soft[:, 1, :, :], -1.0, None, ALU.mult))
                for buf in range(2):
                    link(nc.vector.memset(s_te[I1:I1 + 1, buf, :], 1.0))

            for b in range(BATCH):
                h = m.h[:, b * TPB:(b + 1) * TPB, :]
                if b:
                    dve.wait_ge(xn_ready, b)
                layer_norm_stats(nc, link, h, stats, moments).then_inc(moments_ready, 1)
                dve.wait_ge(inv_std_ready, b + 1)
                if b >= 2:
                    dve.wait_ge(xn_turned, b - 1)
                    dve.wait_ge(rows_out[b % 2], 16)
                layer_norm_apply(nc, h, moments, inv_std, xn[:, b % 2, :, :]).then_inc(xn_ready, 1)
                if not first:
                    shared_front(b)
                    if b:
                        shared_back(b - 1)
                    if b >= 2:
                        shared_add(b - 2)
            if not first:
                shared_back(BATCH - 1)

            dve.wait_ge(logits_done, BATCH)
            link(nc.vector.tensor_tensor(logits[:, :, :], bank_logits[:, 0:NT * E].rearrange("p (t e) -> p t e", e=E),
                                         over_experts(m.router_b[:, layer, :]), ALU.add))
            rank_e = over_experts(m.fconst[:, FC_RANK:FC_RANK + E])
            values = logits
            for k in range(2):
                link(nc.vector.tensor_reduce(top[:, k, :], values[:, :, :], AX.X, ALU.max))
                link(nc.vector.tensor_tensor(chosen[:, k, :, :], values[:, :, :], over_tiles(top[:, k, :]), ALU.is_equal))
                link(nc.vector.tensor_tensor(chosen[:, k, :, :], chosen[:, k, :, :], rank_e, ALU.mult))
                link(nc.vector.tensor_reduce(rank[:, :], chosen[:, k, :, :], AX.X, ALU.max))
                link(nc.vector.tensor_tensor(chosen[:, k, :, :], rank_e, over_tiles(rank[:, :]), ALU.is_equal))
                if k == 0:
                    link(nc.vector.scalar_tensor_tensor(lower[:, :, :], chosen[:, 0, :, :], MASKED, logits[:, :, :],
                                                        ALU.mult, ALU.add))
                    values = lower
            link(nc.vector.memset(marks[:, 0:NT, :], 0.0))
            link(nc.vector.memset(marks[:, 2 * NT, :], 0.0))
            nc.vector.tensor_tensor(marks[:, NT:2 * NT, :], chosen[:, 0, :, :], chosen[:, 1, :, :], ALU.add).then_inc(marks_ready, 1)
            link(nc.vector.tensor_tensor(gap[:, :], top[:, 1, :], top[:, 0, :], ALU.subtract))
            nc.vector.tensor_tensor(weighed[:, :, :], logits[:, :, :], over_tiles(top[:, 0, :]), ALU.subtract
                                    ).then_inc(weighed_ready, 1)
            link(nc.vector.memset(zeros_e[:, :], 0.0))

            dve.wait_ge(ranks_done, 1)
            rank_bank = bank_rank[:, 0:(NT + 1) * E].rearrange("p (t e) -> p t e", e=E)
            link(nc.vector.tensor_tensor(over[:, :, :], rank_bank[:, NT, :].unsqueeze(2).to_broadcast([P, E, NT]),
                                         m.fconst[:, FC_J128:FC_J128 + NT].unsqueeze(1).to_broadcast([P, E, NT]),
                                         ALU.is_gt))
            link(nc.vector.tensor_reduce(n_tiles[:, :], over[:, :, :], AX.X, ALU.add))
            link(nc.vector.tensor_tensor_scan(ends[:, :], n_tiles[:, :], zeros_e[:, :], 0.0, ALU.add, ALU.add))
            link(nc.vector.tensor_tensor(starts[:, :], ends[:, :], n_tiles[:, :], ALU.subtract))
            link(nc.vector.scalar_tensor_tensor(ranks[:, :, :], over_experts(starts[:, :]), float(P),
                                                rank_bank[:, 0:NT, :], ALU.mult, ALU.add))
            for k in range(2):
                link(nc.vector.tensor_tensor(chosen[:, k, :, :], chosen[:, k, :, :], ranks[:, :, :], ALU.mult))
                link(nc.vector.tensor_reduce(pos[:, k * NT:(k + 1) * NT], chosen[:, k, :, :], AX.X, ALU.add))
            link(nc.vector.tensor_copy(pos_i[:, :], pos[:, :]))
            link(nc.vector.tensor_single_scalar(row_i[:, :], pos_i[:, :], P - 1, ALU.bitwise_and))
            link(nc.vector.tensor_copy(row[:, :], row_i[:, :]))
            nc.vector.tensor_tensor(tile128[:, :], pos[:, :], row[:, :], ALU.subtract).then_inc(pos_ready, 1)
            dve.wait_ge(pos_ready, 1)
            hot = tile_hot[:, :, 0, :]
            link(nc.vector.tensor_tensor(
                hot, tile128[:, :].unsqueeze(2).to_broadcast([P, 2 * NT, TILES]),
                m.fconst[:, FC_A128:FC_A128 + TILES].unsqueeze(1).to_broadcast([P, 2 * NT, TILES]), ALU.is_equal))
            nc.vector.tensor_scalar(tile_hot[:, :, 1, :], hot, m.fconst[:, FC_PART:FC_PART + 1], None, ALU.mult
                                    ).then_inc(tile_hot_ready, 1)
            nc.vector.tensor_tensor(
                tile_hot[:, :, 2, :], hot,
                m.fconst[:, FC_KT:FC_KT + 2 * NT].unsqueeze(2).to_broadcast([P, 2 * NT, TILES]), ALU.mult
            ).then_inc(tile_hot_ready, 1)
            nc.vector.tensor_tensor(
                row_hot[:, :, :], row[:, :].unsqueeze(2).to_broadcast([P, 2 * NT, P]),
                m.fconst[:, FC_IOTA:FC_IOTA + P].unsqueeze(1).to_broadcast([P, 2 * NT, P]), ALU.is_equal
            ).then_inc(row_hot_ready, 1)
            link(nc.vector.tensor_tensor(
                before[:, :, :], ends[:, :].unsqueeze(1).to_broadcast([P, TILES, E]),
                m.fconst[:, FC_TILE:FC_TILE + TILES].unsqueeze(2).to_broadcast([P, TILES, E]), ALU.is_le))
            link(nc.vector.tensor_reduce(expert_f[:, :], before[:, :, :], AX.X, ALU.add))
            nc.vector.tensor_scalar(tile_expert[:, :], expert_f[:, :], float(E - 1), None, ALU.min).then_inc(order_ready, 1)
            dve.wait_ge(expd_ready, 2)
            link(nc.vector.tensor_reduce(total[:, :], expd[:, :, :], AX.X, ALU.add))
            link(nc.vector.reciprocal(gate[:, 0, :], total[:, :]))
            link(nc.vector.tensor_tensor(gate[:, 1, :], gap_exp[:, :], gate[:, 0, :], ALU.mult))
            if not first:
                link(nc.vector.tensor_tensor(total[:, :], gate[:, 0, :], gate[:, 1, :], ALU.add))
                link(nc.vector.reciprocal(rank[:, :], total[:, :]))
                for k in range(2):
                    link(nc.vector.tensor_tensor(gate[:, k, :], gate[:, k, :], rank[:, :], ALU.mult))
                for b in range(BATCH - 2, BATCH):
                    shared_add(b)
            dve.wait_ge(pairs_done, 1)
            counted, part, kt = [bank_pairs[:, n * TILES:(n + 1) * TILES] for n in range(3)]
            link(nc.vector.tensor_scalar(wrap[:, :], kt, float(NT), -float(TOK), ALU.is_ge, ALU.mult))
            link(nc.vector.tensor_scalar(pad[:, :], counted, -1.0, 1.0, ALU.mult, ALU.add))
            link(nc.vector.tensor_scalar(pair[:, :], kt, float(P), None, ALU.mult))
            link(nc.vector.tensor_tensor(pair[:, :], pair[:, :], part, ALU.add))
            link(nc.vector.tensor_tensor(pad[:, :], pad[:, :], m.fconst[:, FC_TRASH:FC_TRASH + TILES], ALU.mult))
            nc.vector.tensor_tensor(src_row[:, :], pair[:, :], wrap[:, :], ALU.add).then_inc(order_ready, 1)
            nc.vector.tensor_tensor(dst_row[:, :], pair[:, :], pad[:, :], ALU.add).then_inc(order_ready, 1)
            dve.wait_ge(order_ready, 3)

            def expert(tile):
                return dve.value_load(tile_expert[0:1, bass.ds(tile, 1)], min_val=0, max_val=E - 1)

            def take_x(i, off):
                tile = i * 4 + off
                dve.wait_ge(turned, tile + 1)
                if off >= 2:
                    dve.wait_ge(up_done, tile - 1)
                nc.vector.tensor_copy(xt[:, off % 2, :], bank_turn[off % 2][:, 0:P]).then_inc(xt_ready, 1)

            def keep_b2(i, off, e):
                tile = i * 4 + off
                if off >= 3:
                    dve.wait_ge(y_ready, tile - 2)
                return nc.vector.tensor_scalar(b2_now[:, off % 4, :], m.b2_all[:, bass.ds(e * D, D)], 1.0, None, ALU.mult)

            def take_y(i, off):
                tile = i * 4 + off
                r, rounds = ring(off)
                dve.wait_ge(down_done, tile + 1)
                dve.wait_ge(bias_ready, tile + 1)
                if not (isinstance(i, int) and i + rounds == 0):
                    dve.wait_ge(y_out[r], (i + rounds) * 16)
                nc.vector.tensor_tensor(y_rows[:, r, :], bank_down[off % 2][:, 0:D], b2_now[:, r, :], ALU.add
                                        ).then_inc(y_ready, 1)

            def front_0(i, off):
                tile = i * 4 + off
                e = expert(tile)
                keep_b2(i, off, e)
                if off >= 2:
                    dve.wait_ge(act_ready, tile - 1)
                nc.vector.tensor_scalar(b1_now[:, off % 2, :], m.b1[:, bass.ds(e * FC, FC)], 1.0, None, ALU.mult).then_inc(bias_ready, 1)
                dve.wait_ge(up_done, tile + 1)
                if off >= 2:
                    dve.wait_ge(mid_turned, tile - 1)
                nc.vector.tensor_copy(h_pre[:, off % 2, :], bank_up[off % 2][:, :]).then_inc(pre_ready, 1)

            def front_1(i, off):
                tile = i * 4 + off
                p = off % 2
                e = expert(tile)
                keep_b2(i, off, e).then_inc(bias_ready, 1)
                dve.wait_ge(up_done, tile + 1)
                nc.vector.tensor_tensor(h_pre[:, p, :, :].rearrange("p i c -> p (i c)"), bank_up[p][:, 0:2 * I1],
                                        m.e_b1[:, bass.ds(e * 2 * I1, 2 * I1)], ALU.add).then_inc(s_sum, 1)
                dve.wait_ge(s_sum, tile * 4 + 1)
                bound = lambda which, n: soft[:, which, bass.ds(e, 1), n:n + 1].rearrange("p a b -> p (a b)")
                scalar = lambda n: m.e_act[:, bass.ds(e, 1), n:n + 1].rearrange("p a b -> p (a b)")
                nc.vector.tensor_scalar(g_cl[:, p, :], h_pre[:, p, :, 0], bound(1, 0), bound(3, 0), ALU.min, ALU.max
                                        ).then_inc(s_sum, 1)
                nc.vector.tensor_scalar(u_cl[:, p, :], h_pre[:, p, :, 1], bound(1, 1), bound(3, 1), ALU.min, ALU.max
                                        ).then_inc(s_sum, 1)
                dve.wait_ge(s_sum, tile * 4 + 3)
                if off >= 2:
                    dve.wait_ge(g_kept, tile - 1)
                nc.vector.tensor_scalar(g_al[:, p, :], g_cl[:, p, :], scalar(0), None, ALU.mult).then_inc(sig_asked, 1)
                nc.vector.scalar_tensor_tensor(gu[:, p, :], u_cl[:, p, :], scalar(2), g_cl[:, p, :], ALU.add, ALU.mult
                                               ).then_inc(s_sum, 1)
                return e

            def back_1(i, off, e):
                tile = i * 4 + off
                p = off % 2
                dve.wait_ge(g_kept, tile + 1)
                dve.wait_ge(s_sum, tile * 4 + 4)
                if off >= 2:
                    dve.wait_ge(mid_turned, tile - 1)
                scalar = m.e_act[:, bass.ds(e, 1), 1:2].rearrange("p a b -> p (a b)")
                nc.vector.scalar_tensor_tensor(te[:, p, :], gu[:, p, :], scalar, sig[:, p, :], ALU.mult, ALU.mult
                                               ).then_inc(pre_ready, 1)

            def step(i, off, front=True, x=True, y=True):
                if first:
                    if front:
                        front_0(i, off)
                    if x:
                        take_x(i, off + 1)
                    if y:
                        take_y(i, off - 2)
                else:
                    if front:
                        e = front_1(i, off)
                    if y:
                        take_y(i, off - 2)
                    if front:
                        back_1(i, off, e)

            if first:
                take_x(0, 0)
            step(0, 0, y=False)
            step(0, 1, y=False)
            for off in range(2, 6):
                step(0, off)
            with dve.Fori(0, LOOPS - 1) as i:
                for u in range(4):
                    step(i, 6 + u)
            step(LOOPS, 2)
            step(LOOPS, 3, x=False)
            for off in (4, 5):
                step(LOOPS, off, front=False, x=False)

            for b in range(BATCH):
                dve.wait_ge(y_in[b % 2], 32 * (b // 2 + 1))
                for k in range(2):
                    for t in range(TPB):
                        n = b * TPB + t
                        last = nc.vector.scalar_tensor_tensor(m.h[:, n, :], y_sel[:, b % 2, k, t, :], gate[:, k, n:n + 1],
                                                              m.h[:, n, :], ALU.mult, ALU.add)
                    if k == 0:
                        link(last)
                last.then_inc(added, 1)

        @block.tensor
        def _(pe):
            ident = m.fconst[:, FC_IDENT:FC_IDENT + P]
            if first:
                pe.wait_ge(m.experts_now, m.e_waits)

            def shared_down(b):
                pe.wait_ge(s_te_ready, 2 * b + 2)
                if b >= 2:
                    pe.wait_ge(s_added, b - 1)
                for t in range(TPB):
                    last = nc.tensor.matmul(bank_down[b % 2][:, t * P:(t + 1) * P], s_te[:, b % 2, t * P:(t + 1) * P],
                                            m.s_w2[:, :], start=True, stop=True)
                last.then_inc(s_down, 1)

            for b in range(BATCH):
                pe.wait_ge(xn_ready, b + 1)
                if b >= 2:
                    pe.wait_ge(x_t_ready, b - 1)
                for t in range(TPB):
                    last = nc.tensor.transpose(bank_turn[b % 2][:, t * P:(t + 1) * P], xn[:, b % 2, t, :], ident)
                last.then_inc(xn_turned, 1)
                pe.wait_ge(x_t_ready, b + 1)
                for t in range(TPB):
                    n = b * TPB + t
                    last = nc.tensor.matmul(bank_logits[:, n * E:(n + 1) * E], x_t[:, b % 2, t * P:(t + 1) * P],
                                            m.router_w[:, layer, :], start=True, stop=True)
                last.then_inc(logits_done, 1)
                if not first:
                    if b:
                        pe.wait_ge(s_capped, 2 * b)
                    elif not first:
                        pe.wait_ge(m.experts_now, m.e_waits)
                    for n in range(2):
                        w = m.s_w1[:, :].rearrange("p (i c) -> p c i", c=2)[:, n, :]
                        last = nc.tensor.matmul(bank_mid[n][0:I1, :], w, x_t[:, b % 2, :], start=True, stop=True)
                    last.then_inc(s_up, 1)
                    if b:
                        shared_down(b - 1)
            if not first:
                shared_down(BATCH - 1)
            pe.wait_ge(marks_ready, 1)
            for s in range(NT + 1):
                last = nc.tensor.matmul(bank_rank[:, 0:(NT + 1) * E], m.bconst[:, BC_ONES if s else BC_TRI, :],
                                        marks[:, NT - s:2 * NT + 1 - s, :].rearrange("p t e -> p (t e)"),
                                        start=(s == 0), stop=(s == NT))
            last.then_inc(ranks_done, 1)
            pe.wait_ge(tile_hot_ready, 2)
            pe.wait_ge(row_hot_ready, 1)
            for g in range(2 * NT):
                last = nc.tensor.matmul(bank_pairs[:, 0:3 * TILES], row_hot[:, g, :],
                                        tile_hot[:, g, :, :].rearrange("p s a -> p (s a)"),
                                        start=(g == 0), stop=(g == 2 * NT - 1))
            last.then_inc(pairs_done, 1)
            pe.wait_ge(order_ready, 3)

            def expert(tile):
                return pe.value_load(tile_expert[0:1, bass.ds(tile, 1)], min_val=0, max_val=E - 1)

            def turn(i, off):
                tile = i * 4 + off
                r, rounds = ring(off)
                pe.wait_ge(x_in[r], (i + rounds + 1) * 16)
                if off >= 2:
                    pe.wait_ge(xt_ready, tile - 1)
                nc.tensor.transpose(bank_turn[off % 2][:, 0:P], x_rows[:, r, :], ident).then_inc(turned, 1)

            def up(i, off):
                tile = i * 4 + off
                e = expert(tile)
                pe.wait_ge(xt_ready, tile + 1)
                if off >= 2:
                    pe.wait_ge(pre_ready if first else s_sum, tile - 1 if first else (tile - 2) * 4 + 1)
                w = m.w1 if first else m.e_w1
                nc.tensor.matmul(bank_up[off % 2][:, 0:width], xt[:, off % 2, :], w[:, bass.ds(e * width, width)],
                                 start=True, stop=True).then_inc(up_done, 1)

            def mid(i, off):
                tile = i * 4 + off
                pe.wait_ge(pre_ready, tile + 1)
                if off >= 2:
                    pe.wait_ge(act_ready, tile - 1)
                if first:
                    for c in range(FC):
                        last = nc.tensor.transpose(bank_mid[off % 2][:, c * P:(c + 1) * P],
                                                   h_pre[:, off % 2, c * P:(c + 1) * P], ident)
                else:
                    last = nc.tensor.transpose(bank_mid[off % 2][0:I1, 0:P], te[:, off % 2, :], ident)
                last.then_inc(mid_turned, 1)

            def down(i, off):
                tile = i * 4 + off
                e = expert(tile)
                pe.wait_ge(act_ready, tile + 1)
                if off >= 2:
                    pe.wait_ge(y_ready, tile - 1)
                if first:
                    for c in range(FC):
                        last = nc.tensor.matmul(bank_down[off % 2][:, 0:D], h_act[:, off % 2, c * P:(c + 1) * P],
                                                m.w2[:, bass.ds(e * DFF + c * D, D)], start=(c == 0), stop=(c == FC - 1))
                else:
                    last = nc.tensor.matmul(bank_down[off % 2][:, 0:D], te_t[:, off % 2, :],
                                            m.e_w2[:, bass.ds(e * D, D)], start=True, stop=True)
                last.then_inc(down_done, 1)

            def step(i, off, front=True, x=True, y=True):
                if front:
                    up(i, off)
                if x:
                    turn(i, off + 1)
                if first:
                    if y:
                        down(i, off - 2)
                    if front:
                        mid(i, off)
                else:
                    if off >= 1:
                        mid(i, off - 1)
                    if y:
                        down(i, off - 2)

            turn(0, 0)
            step(0, 0, y=False)
            step(0, 1, y=False)
            with pe.Fori(0, LOOPS) as i:
                for u in range(4):
                    step(i, 2 + u)
            step(LOOPS, 2)
            step(LOOPS, 3, x=False)
            step(LOOPS, 4, front=False, x=False)
            if first:
                step(LOOPS, 5, front=False, x=False)
            else:
                down(LOOPS, 3)


def program(nc, io):
    with ExitStack() as ctx:
        def sb(name, shape, dt=F32):
            return ctx.enter_context(nc.sbuf_tensor(name, shape, dt))

        def dram(name, shape, dt=F32):
            return nc.dram_tensor(name, shape, dt, kind="Internal").ap()

        def sem(name):
            return ctx.enter_context(nc.semaphore(name))

        m = Memory()
        m.x, m.table, m.out, m.w_qkv_d = io["x"], io["table"], io["out"], io["w_qkv_d"]
        m.w_o_d, m.router_w_d, m.router_b_d, m.w1_d = io["w_o_d"], io["router_w_d"], io["router_b_d"], io["w1_d"]
        m.w2_d, m.b1_d, m.b2_d, m.e_w1_d = io["w2_d"], io["b1_d"], io["b2_d"], io["e_w1_d"]
        m.e_b1_d, m.e_w2_d, m.e_b2_d, m.e_act_d = io["e_b1_d"], io["e_w2_d"], io["e_b2_d"], io["e_act_d"]
        m.s_w1_d, m.s_b1_d, m.s_w2_d, m.s_b2_d = io["s_w1_d"], io["s_b1_d"], io["s_w2_d"], io["s_b2_d"]
        m.s_act_d, m.fconst_d, m.bconst_d, m.q_rows_d = io["s_act_d"], io["fconst_d"], io["bconst_d"], io["q_rows_d"]
        m.k_rows_d = io["k_rows_d"]
        m.h = sb("h", [P, NT, D])
        m.fconst = sb("fconst", [P, FC_END])
        m.bconst = sb("bconst", [P, BC_END, P], BF16)
        m.w_qkv = sb("w_qkv", [P, 2, 3 * D])
        m.w_o = sb("w_o", [P, 2, NG, D])
        m.router_w = sb("router_w", [P, 2, E])
        m.router_b = sb("router_b", [P, 2, E])
        m.parts_d = dram("parts_d", [BATCH, 2, 3, H, HD, SEQ], BF16)
        m.x_rows_d = dram("x_rows_d", [TOK, D])
        m.y_rows_d = dram("y_rows_d", [PAIRS + SLOTS, D])
        m.bank = [ctx.enter_context(nc.psum_tensor(f"bank{i}", [P, 512], F32)) for i in range(8)]
        m.bconst_in, m.attn_w_in = sem("bconst_in"), sem("attn_w_in")
        m.experts_in, m.experts2_in = sem("experts_in"), sem("experts2_in")

        m.rows_in = sem("rows_in")
        m.x_in = [[sem(f"x_in_{layer}_{r}") for r in range(4)] for layer in range(2)]
        m.y_out = [[sem(f"y_out_{layer}_{r}") for r in range(4)] for layer in range(2)]

        with ExitStack() as experts:
            def esb(name, shape):
                return experts.enter_context(nc.sbuf_tensor(name, shape, F32))

            m.w1, m.w2 = esb("w1", [P, E * DFF]), esb("w2", [P, E * DFF])
            m.b1, m.b2 = esb("b1", [P, E * FC]), esb("b2", [P, E * D])
            embed_phase(nc, m)
            attention_phase(nc, m, 0)
            m.b2_all, m.experts_now, m.e_waits = m.b2, m.experts_in, 16 * 10
            moe_phase(nc, m, 0)
        m.e_w1, m.e_w2 = sb("e_w1", [P, E * 2 * I1]), sb("e_w2", [I1, E * D])
        m.e_b1, m.e_b2 = sb("e_b1", [P, E * 2 * I1]), sb("e_b2", [P, E * D])
        m.e_act = sb("e_act", [P, NE1, 5])
        m.s_w1, m.s_w2, m.s_b1 = sb("s_w1", [P, 2 * I1]), sb("s_w2", [I1 + 1, D]), sb("s_b1", [I1, 2])
        m.second_experts = [
            (m.e_w1[:, :].rearrange("p (e f) -> p e f", e=E), m.e_w1_d.rearrange("e d f -> d e f")),
            (m.e_w2[:, :].rearrange("p (e d) -> p e d", e=E), m.e_w2_d.rearrange("e i d -> i e d")),
            (m.e_b1[:, :], m.e_b1_d.partition_broadcast(P)),
            (m.e_b2[:, :], m.e_b2_d.partition_broadcast(P)),
            (m.e_act[:, 0:E, :].rearrange("p e c -> p (e c)"), m.e_act_d.partition_broadcast(P)),
            (m.e_act[:, E, :], m.s_act_d.partition_broadcast(P)),
            (m.s_w1[:, :], m.s_w1_d),
            (m.s_w2[0:I1, :], m.s_w2_d),
            (m.s_w2[I1:I1 + 1, :], m.s_b2_d.unsqueeze(0)),
            (m.s_b1[:, :], m.s_b1_d.rearrange("(i c) -> i c", c=2)),
        ]
        attention_phase(nc, m, 1)
        m.b2_all, m.experts_now, m.e_waits = m.e_b2, m.experts2_in, 16 * 10
        moe_phase(nc, m, 1)


def constants():
    p = np.arange(P)
    f = np.zeros((P, FC_END), np.float32)
    f[:, FC_IDENT:FC_IDENT + P] = np.eye(P)
    f[32 * (p // 32) + HD, FC_SEL + p] = 1.0
    f[:, FC_RANK:FC_RANK + E] = E - np.arange(E)
    f[:, FC_J128:FC_J128 + NT] = P * np.arange(NT)
    f[:, FC_IOTA:FC_IOTA + P] = p
    f[:, FC_A128:FC_A128 + TILES] = P * np.arange(TILES)
    f[:, FC_TILE:FC_TILE + TILES] = np.arange(TILES)
    f[:, FC_TRASH:FC_TRASH + TILES] = PAIRS + P * np.arange(TILES)[None] + p[:, None]
    f[:, FC_KT:FC_KT + 2 * NT] = np.arange(2 * NT)
    f[:, FC_PART] = p
    f[:, FC_POW:FC_POW + TPB] = -0.5
    b = np.zeros((P, BC_END, P), np.float32)
    past = p[:, None] - p[None]
    b[:, BC_IDENT] = np.eye(P)
    b[:, BC_CAUSAL_Q] = np.where(past < 0, MASKED, 0.0)
    b[:, BC_CAUSAL_K] = b[:, BC_CAUSAL_Q].T
    b[:, BC_PAST_Q] = np.maximum(past, 0)
    b[:, BC_PAST_K] = b[:, BC_PAST_Q].T
    b[:, BC_TRI] = past < 0
    b[:, BC_ONES] = 1.0
    t = np.arange(SEQ)
    high, low = t // 256 * 256, t % 256
    one = np.ones(SEQ)
    q_rows = np.stack([0 * one, 0 * one, 0 * one, high, low, one, one])
    k_rows = np.stack([one, one, one, one, one, -high, -low])
    bf = np.dtype("bfloat16")
    return {"fconst_d": f, "bconst_d": b.astype(bf), "q_rows_d": q_rows.astype(bf), "k_rows_d": k_rows.astype(bf)}


def padded_out(w, bias):
    w = w.T.reshape(NG, GH, HD, D)
    out = np.zeros((NG, GH, 2 * HD, D), w.dtype)
    out[:, :, :HD] = w
    out[0, 0, HD] = bias
    return out.reshape(NG, GH * 2 * HD, D)


def layout(a):
    c = np.ascontiguousarray
    return {
        "x": a["x"],
        "table": a["L0_tok_table"],
        "w_qkv_d": c(np.stack([a["L0_attn_w_qkv"].T, a["L1_attn_w_qkv"].T])),
        "w_o_d": c(np.stack([padded_out(a["L0_attn_w_proj"], a["L0_attn_b_proj"]),
                             padded_out(a["L1_attn_w_out"], a["L1_attn_b_out"])])),
        "router_w_d": c(np.stack([a["L0_ffn_router_w"].T, a["L1_ffn_gate_w"]], axis=1)),
        "router_b_d": c(np.stack([a["L0_ffn_router_b"], a["L1_ffn_gate_b"]])),
        "w1_d": c(a["L0_ffn_w1"].transpose(2, 0, 1).reshape(D, E * DFF)),
        "w2_d": c(a["L0_ffn_w2"].reshape(E, D, FC, P).transpose(3, 0, 2, 1).reshape(P, E * FC * D)),
        "b1_d": c(a["L0_ffn_b1"].reshape(E, FC, P).transpose(2, 0, 1).reshape(P, E * FC)),
        "b2_d": c(a["L0_ffn_b2"].reshape(E * D)),
        "e_w1_d": a["L1_ffn_expert_w1"], "e_b1_d": c(a["L1_ffn_expert_b1"].reshape(-1)),
        "e_w2_d": a["L1_ffn_expert_w2"], "e_b2_d": c(a["L1_ffn_expert_b2"].reshape(-1)),
        "e_act_d": c(a["L1_ffn_expert_act"].reshape(-1)),
        "s_w1_d": a["L1_ffn_shared_w1"], "s_b1_d": a["L1_ffn_shared_b1"],
        "s_w2_d": a["L1_ffn_shared_w2"], "s_b2_d": a["L1_ffn_shared_b2"], "s_act_d": a["L1_ffn_shared_act"],
    }


def kernel(**inputs):
    import concourse.bacc as bacc
    from concourse.bass_utils import run_bass_kernel_spmd

    nc = bacc.Bacc("TRN2", target_bir_lowering=False, num_devices=1)
    data = layout({name: np.asarray(a) for name, a in inputs.items()})
    data.update(constants())
    arrays, io = {}, {}
    for name, a in data.items():
        arrays[f"in_{name}"] = a
        io[name] = nc.dram_tensor(f"in_{name}", list(a.shape), mybir.dt.from_np(a.dtype), kind="ExternalInput").ap()
    io["out"] = nc.dram_tensor("out_0_dram", [BATCH, SEQ, D], F32, kind="ExternalOutput").ap()
    program(nc, io)
    r = run_bass_kernel_spmd(nc, [arrays], core_ids=[0])
    return r.results[0]["out_0_dram"]
```

```python
from contextlib import ExitStack
import math

import numpy as np

import concourse.bass as bass
from concourse import mybir

F32 = mybir.dt.float32
BF16 = mybir.dt.bfloat16
I32 = mybir.dt.int32
ALU = mybir.AluOpType
ACT = mybir.ActivationFunctionType
AX = mybir.AxisListType
ENGINE = mybir.EngineType

P = 128
D = 128
BATCH, SEQ = 4, 512
TPB = SEQ // P
NT = BATCH * TPB
TOK = BATCH * SEQ
H, HD = 8, 16
GH = 4
NG = H // GH
E = 16
NE1 = E + 1
DFF = 512
FC = DFF // P
I1 = 96
KMER, VOCAB = 6, 5
EPS = 1e-5
UNITS = H * TPB
TILES = 47
RING = 8
SHARED_FIRST, SHARED_EVERY = 2, 10
PAIRS = 2 * TOK
SLOTS = TILES * P
DECAY = -math.log(0.9)
MASKED = -1.0e30

BLOCKS_Q = (0, 0, 0, 1, 1, 2)
BLOCKS_K = (0, 1, 2, 0, 1, 0)
R_DOT = len(BLOCKS_Q) * HD
R_MAX = R_DOT + 3
R_ALL = R_MAX + 4

FC_IDENT, FC_RANK, FC_J128, FC_IOTA = 0, 128, 144, 160
FC_A128, FC_TILE, FC_TRASH = 288, 336, 384
FC_KT, FC_PART, FC_POW, FC_END = 432, 464, 465, 469
BC_IDENT, BC_CAUSAL_Q, BC_CAUSAL_K, BC_PAST_Q, BC_PAST_K, BC_TRI, BC_ONES, BC_END = range(8)


class Memory:
    pass


def clear_semaphores(nc, sems):
    for s in sems:
        nc.gpsimd.sem_clear(s)
    nc.all_engine_barrier()


def embed_phase(nc, m):
    with ExitStack() as ctx:
        ids = ctx.enter_context(nc.sbuf_tensor("ids", [BATCH, SEQ + KMER - 1], I32))
        idx = ctx.enter_context(nc.sbuf_tensor("idx", [BATCH, KMER, SEQ], F32))
        idx_col = ctx.enter_context(nc.sbuf_tensor("idx_col", [P, BATCH, TPB], I32))
        sems = []

        def sem(name):
            sems.append(ctx.enter_context(nc.semaphore(name)))
            return sems[-1]

        consts_in, ids_in = sem("e_consts_in"), sem("e_ids_in")
        ids_zero, horner = sem("e_ids_zero"), sem("e_horner")
        idx_turned, idx_ready, rows_in = sem("e_idx_turned"), sem("e_idx_ready"), m.rows_in
        turned = m.bank[0]
        ctx.callback(clear_semaphores, nc, sems)
        block = ctx.enter_context(nc.Block())

        @block.sync
        def _(sp):
            sp.wait_ge(ids_zero, 1)
            sp.dma_start(ids[:, 2:2 + SEQ], m.x).then_inc(ids_in, 16)
            sp.dma_start(m.fconst[:, :], m.fconst_d).then_inc(consts_in, 16)
            sp.dma_start(m.bconst[:, :, :], m.bconst_d).then_inc(m.bconst_in, 16)
            for layer in range(2):
                for g in range(NG):
                    sp.dma_start(m.w_o[:, layer, g, :], m.w_o_d[layer][g]).then_inc(m.attn_w_in, 16)
                sp.dma_start(m.w_qkv[:, layer, :], m.w_qkv_d[layer]).then_inc(m.attn_w_in, 16)
            sp.dma_start(m.router_w[:, :, :], m.router_w_d).then_inc(m.attn_w_in, 16)
            for layer in range(2):
                sp.dma_start(m.router_b[:, layer, :],
                             m.router_b_d[layer].partition_broadcast(P)).then_inc(m.attn_w_in, 16)

        @block.gpsimd
        def _(pool):
            pool.wait_ge(idx_ready, 1)
            for t in range(NT):
                pool.indirect_dma_start(
                    m.h[:, t, :], None, m.table,
                    bass.IndirectOffsetOnAxis(ap=idx_col[:, t // TPB, t % TPB:t % TPB + 1], axis=0)
                ).then_inc(rows_in, 16)
            pool.wait_ge(rows_in, 16 * NT)

        @block.vector
        def _(dve):
            nc.vector.memset(ids[:, :], 0).then_inc(ids_zero, 1)
            dve.wait_ge(ids_in, 16)
            nc.vector.scalar_tensor_tensor(idx[:, 1, :], ids[:, 0:SEQ], float(VOCAB), ids[:, 1:1 + SEQ],
                                           ALU.mult, ALU.add).then_inc(horner, 1)
            for j in range(2, KMER):
                dve.wait_ge(horner, j - 1)
                nc.vector.scalar_tensor_tensor(idx[:, j, :], idx[:, j - 1, :], float(VOCAB), ids[:, j:j + SEQ],
                                               ALU.mult, ALU.add).then_inc(horner, 1)
            dve.wait_ge(idx_turned, 1)
            nc.vector.tensor_copy(idx_col[:, :, :],
                                  turned[:, 0:NT].rearrange("p (c b) -> p b c", b=BATCH)).then_inc(idx_ready, 1)

        @block.tensor
        def _(pe):
            pe.wait_ge(consts_in, 16)
            pe.wait_ge(horner, KMER - 1)
            for c in range(TPB):
                last = nc.tensor.transpose(turned[:, c * BATCH:(c + 1) * BATCH],
                                           idx[:, KMER - 1, c * P:(c + 1) * P],
                                           m.fconst[0:BATCH, FC_IDENT:FC_IDENT + BATCH])
            last.then_inc(idx_turned, 1)


def layer_norm_stats(nc, link, h, stats, moments):
    for t in range(TPB):
        last = nc.vector.bn_stats(stats[:, t, :], h[:, t, :])
    link(last)
    for t in range(TPB):
        last = nc.vector.bn_aggr(moments[:, t, :], stats[:, t, :])
    return last


def inverse_std(nc, pool, m, moments, var_eps, inv_std, var_eps_ready, b):
    nc.gpsimd.tensor_scalar(var_eps[:, :], moments[:, :, 1], EPS, None, ALU.add).then_inc(var_eps_ready, 1)
    pool.wait_ge(var_eps_ready, b + 1)
    return nc.gpsimd.tensor_tensor(inv_std[:, :], var_eps[:, :], m.fconst[:, FC_POW:FC_POW + TPB], ALU.pow)


def layer_norm_apply(nc, h, moments, inv_std, out):
    for t in range(TPB):
        last = nc.vector.tensor_scalar(out[:, t, :], h[:, t, :], moments[:, t, 0:1], inv_std[:, t:t + 1],
                                       ALU.subtract, ALU.mult)
    return last


def attention_phase(nc, m, layer):
    causal = layer == 0
    q_scale = 1.0 if causal else HD ** -0.5 / DECAY
    exp_scale = HD ** -0.5 if causal else DECAY
    diag_q, diag_k = (BC_CAUSAL_Q, BC_CAUSAL_K) if causal else (BC_PAST_Q, BC_PAST_K)
    n_loads = 2 * len(BLOCKS_Q) + 1
    STEPS = BATCH + 2

    uses_a = [("x", 0), ("v", 0)]
    uses_b = [("q", 0)]
    uses_c = [("k", 0)]
    for s in range(STEPS):
        if 0 <= s - 1 < BATCH:
            uses_a.append(("max", s - 1, 1))
        if 0 <= s - 2:
            uses_b += [("turn", s - 2, 1), ("back", s - 2, 1)]
        if s + 1 < BATCH:
            uses_a += [("x", s + 1), ("v", s + 1)]
            uses_b.append(("q", s + 1))
            uses_c.append(("k", s + 1))
        if s < BATCH:
            uses_a.append(("max", s, 0))
        if 0 <= s - 1 < BATCH:
            uses_b += [("turn", s - 1, 0), ("back", s - 1, 0)]
        if 0 <= s - 2:
            uses_a.append(("x2", s - 2))
            uses_c += [("y", s - 2), ("logits", s - 2)]
    nth_a = {key: n for n, key in enumerate(uses_a)}
    nth_b = {key: n for n, key in enumerate(uses_b)}
    nth_c = {key: n for n, key in enumerate(uses_c)}

    with ExitStack() as ctx:
        def sb(name, shape, dt=F32):
            return ctx.enter_context(nc.sbuf_tensor(f"{name}_{layer}", shape, dt))

        sems = []

        def sem(name):
            sems.append(ctx.enter_context(nc.semaphore(f"a{layer}_{name}")))
            return sems[-1]

        stats, moments = sb("stats", [P, TPB, 6]), sb("moments", [P, TPB, 2])
        var_eps, inv_std = sb("var_eps", [P, TPB]), sb("inv_std", [P, TPB])
        xn, x_t = sb("xn", [P, TPB, D]), sb("x_t", [P, SEQ])
        q_pack, k_pack = sb("q_pack", [P, 3, H, SEQ], BF16), sb("k_pack", [P, 3, H, SEQ], BF16)
        v_ext = sb("v_ext", [P, 3, TPB, H, 2 * HD])
        parts = {"q": sb("q_parts", [P, 3, SEQ], BF16), "k": sb("k_parts", [P, 3, SEQ], BF16)}
        rest = {"q": sb("q_rest", [P, SEQ]), "k": sb("k_rest", [P, SEQ])}
        neg_max, max_rest = sb("neg_max", [P, NG, UNITS // NG]), sb("max_rest", [P, NG, UNITS // NG])
        max_parts = sb("max_parts", [P, NG, 3, UNITS // NG], BF16)
        max_rows = sb("max_rows", [3 * UNITS // NG, NG, P], BF16)
        probs = sb("probs", [P, 8, SEQ])
        o_tok, inv_sums = sb("o_tok", [P, TPB * GH, 2 * HD]), sb("inv_sums", [P, TPB * GH])
        stats2, moments2 = sb("stats2", [P, TPB, 6]), sb("moments2", [P, TPB, 2])
        var_eps2, inv_std2 = sb("var_eps2", [P, TPB]), sb("inv_std2", [P, TPB])
        xn2 = sb("xn2", [P, TPB, D])
        o_raw, o_norm = sb("o_raw", [P, NG, SEQ]), sb("o_norm", [P, NG, SEQ])

        bank_q = m.bank[0:2]
        bank_k = m.bank[2:4]
        bank_o = m.bank[4]
        bank_a, bank_b, bank_c = m.bank[5:8]

        dve_chain = sem("dve_chain")
        pack_rows_in, v_ext_zero = sem("pack_rows_in"), sem("v_ext_zero")
        var_eps_ready = sem("var_eps_ready")
        moments_ready, inv_std_ready, xn_ready = sem("moments_ready"), sem("inv_std_ready"), sem("xn_ready")
        a_filled, b_filled, c_filled = sem("a_filled"), sem("b_filled"), sem("c_filled")
        a_read, b_read, c_read = sem("a_read"), sem("b_read"), sem("c_read")
        high_ready, mid_ready, low_ready = sem("high_ready"), sem("mid_ready"), sem("low_ready")
        parts_out = sem("parts_out")
        pack_in = [sem("pack_in_even"), sem("pack_in_odd")]
        q_scores, q_scores_read = sem("q_scores"), sem("q_scores_read")
        max_parts_ready, max_in = sem("max_parts_ready"), [sem("max_in_0"), sem("max_in_1")]
        k_scores, probs_ready, pv_done = sem("k_scores"), sem("probs_ready"), sem("pv_done")
        o_read, inverted = sem("o_read"), sem("inverted")
        moments2_ready, var_eps2_ready, inv_std2_ready = sem("moments2_ready"), sem("var_eps2_ready"), sem("inv_std2_ready")
        xn2_ready, rows_out = sem("xn2_ready"), sem("rows_out")
        ctx.callback(clear_semaphores, nc, sems)
        block = ctx.enter_context(nc.Block())

        @block.sync
        def _(sp):
            def pack(b):
                for n, name in enumerate("qk"):
                    sp.wait_ge(high_ready, 2 * b + n + 1)
                    sp.wait_ge(mid_ready, 2 * b + n + 1)
                    sp.wait_ge(low_ready, 2 * b + n + 1)
                    sp.dma_start(m.parts_d[b, n].rearrange("s h d t -> (h d) s t"),
                                 parts[name][:, :, :]).then_inc(parts_out, 16)
                if b == 0:
                    sp.wait_ge(pack_rows_in, 16 * 6)
                if b >= 3:
                    sp.wait_ge(pv_done, (b - 2) * UNITS // GH)
                sp.wait_ge(parts_out, 32 * (b + 1))
                for n, (dest, blocks) in enumerate(((q_pack, BLOCKS_Q), (k_pack, BLOCKS_K))):
                    for i, part in enumerate(blocks):
                        sp.dma_start(dest[i * HD:(i + 1) * HD, b % 3, :, :],
                                     m.parts_d[b, n, part].rearrange("h d t -> d h t")
                                     ).then_inc(pack_in[b % 2], 16)
                sp.dma_start(q_pack[R_DOT:R_MAX, b % 3, :, :],
                             m.q_rows_d[0:3].unsqueeze(1).to_broadcast([3, H, SEQ])).then_inc(pack_in[b % 2], 16)

            def max_to_rows(b, g):
                sp.wait_ge(a_read, nth_a["max", b, g] + 1)
                sp.wait_ge(q_scores, b * UNITS + (g + 1) * UNITS // NG)
                for s in range(3):
                    sp.dma_start(q_pack[R_DOT + s:R_DOT + s + 1, b % 3, g * GH:(g + 1) * GH, :],
                                 max_rows[s * 16:(s + 1) * 16, g, :]).then_inc(max_in[g], 16)

            for buf in range(3):
                for pack_buf, rows in ((k_pack, m.k_rows_d), (q_pack, m.q_rows_d)):
                    sp.dma_start(pack_buf[R_DOT:R_ALL, buf, :, :],
                                 rows.unsqueeze(1).to_broadcast([R_ALL - R_DOT, H, SEQ])
                                 ).then_inc(pack_rows_in, 16)
            pack(0)
            for s in range(STEPS):
                if 0 <= s - 1 < BATCH:
                    max_to_rows(s - 1, 1)
                if s + 1 < BATCH:
                    pack(s + 1)
                if s < BATCH:
                    for dest, src in m.expert_loads[s::BATCH]:
                        sp.dma_start(dest, src).then_inc(m.experts_now, 16)
                    max_to_rows(s, 0)
                if 0 <= s - 2:
                    sp.wait_ge(xn2_ready, s - 1)
                    sp.dma_start(m.x_rows_d[(s - 2) * SEQ:(s - 1) * SEQ, :].rearrange("(t p) d -> p t d", p=P),
                                 xn2[:, :, :]).then_inc(rows_out, 16)
            sp.wait_ge(rows_out, 16 * BATCH)

        @block.gpsimd
        def _(pool):
            def low_parts(b):
                pool.wait_ge(moments_ready, b + 1)
                inverse_std(nc, pool, m, moments, var_eps, inv_std, var_eps_ready, b).then_inc(inv_std_ready, 1)
                for n, name in enumerate("qk"):
                    pool.wait_ge(mid_ready, 2 * b + n + 1)
                    nc.gpsimd.tensor_tensor(parts[name][:, 2, :], rest[name][:, :], parts[name][:, 1, :],
                                            ALU.subtract).then_inc(low_ready, 1)

            low_parts(0)
            for s in range(STEPS):
                if s + 1 < BATCH:
                    low_parts(s + 1)
                if 0 <= s - 2:
                    pool.wait_ge(moments2_ready, s - 1)
                    inverse_std(nc, pool, m, moments2, var_eps2, inv_std2, var_eps2_ready, s - 2).then_inc(inv_std2_ready, 1)

        @block.scalar
        def _(act):
            def take_x(b):
                act.wait_ge(a_filled, nth_a["x", b] + 1)
                if b:
                    act.wait_ge(c_filled, nth_c["k", b - 1] + 1)
                    act.wait_ge(a_filled, nth_a["v", b - 1] + 1)
                nc.scalar.activation(x_t[:, :], bank_a[:, :], ACT.Copy).then_inc(a_read, 1)

            def take_projections(b):
                for n, (name, bank, filled, nth) in enumerate((("q", bank_b, b_filled, nth_b),
                                                               ("k", bank_c, c_filled, nth_c))):
                    act.wait_ge(filled, nth[name, b] + 1)
                    if b:
                        act.wait_ge(parts_out, 32 * b)
                    nc.scalar.activation(parts[name][:, 0, :], bank[:, :], ACT.Copy,
                                         scale=q_scale if name == "q" else 1.0).then_inc(high_ready, 1)
                for n, (name, read, nth) in enumerate((("q", b_read, nth_b), ("k", c_read, nth_c))):
                    act.wait_ge(read, nth[name, b] + 1)
                    nc.scalar.activation(parts[name][:, 1, :], rest[name][:, :], ACT.Copy).then_inc(mid_ready, 1)
                act.wait_ge(a_filled, nth_a["v", b] + 1)
                if b == 0:
                    act.wait_ge(v_ext_zero, 6)
                if b >= 3:
                    act.wait_ge(pv_done, (b - 2) * UNITS // GH)
                nc.scalar.activation(v_ext[:, b % 3, :, :, 0:HD],
                                     bank_a[:, :].rearrange("p (t h d) -> p t h d", t=TPB, h=H),
                                     ACT.Copy).then_inc(a_read, 1)

            def take_max_rows(b, g):
                act.wait_ge(a_filled, nth_a["max", b, g] + 1)
                if b:
                    act.wait_ge(max_in[g], 48 * b)
                nc.scalar.activation(max_rows[:, g, :], bank_a[0:48, 0:P // 2].bitcast(BF16),
                                     ACT.Copy).then_inc(a_read, 1)

            def exponential(b, u):
                n = b * UNITS + u
                ki = (u // GH) % TPB
                first = ki * P if causal else 0
                act.wait_ge(k_scores, n + 1)
                if n >= 8:
                    act.wait_ge(pv_done, (n - 8) // GH + 1)
                nc.scalar.activation(probs[:, n % 8, first:], bank_k[n % 2][:, first:], ACT.Exp,
                                     scale=exp_scale).then_inc(probs_ready, 1)

            def take_output(b, g):
                act.wait_ge(pv_done, (b * NG + g + 1) * TPB)
                if b:
                    act.wait_ge(b_filled, nth_b["turn", b - 1, g] + 1)
                nc.scalar.activation(o_raw[:, g, :], bank_o[:, :], ACT.Copy).then_inc(o_read, 1)

            def take_normalized(b, g):
                act.wait_ge(b_filled, nth_b["back", b, g] + 1)
                if b:
                    act.wait_ge(c_filled, nth_c["y", b - 1] + 1)
                nc.scalar.activation(o_norm[:, g, :], bank_b[:, :], ACT.Copy).then_inc(b_read, 1)

            def take_x2(b):
                act.wait_ge(a_filled, nth_a["x2", b] + 1)
                if layer == 0 and b >= 2:
                    act.wait_ge(c_filled, nth_c["logits", b - 2] + 1)
                nc.scalar.activation(m.x2_t[:, b % m.x2_t.shape[1], :], bank_a[:, :], ACT.Copy).then_inc(a_read, 1)

            take_x(0)
            take_projections(0)
            for s in range(STEPS):
                for u in range(UNITS):
                    if u == 3 and 0 <= s - 1 < BATCH:
                        take_max_rows(s - 1, 1)
                    if u == 5 and s + 1 < BATCH:
                        take_x(s + 1)
                    if u == 7 and 0 <= s - 2:
                        take_normalized(s - 2, 1)
                    if u == 11 and s + 1 < BATCH:
                        take_projections(s + 1)
                    if u == 19 and s < BATCH:
                        take_max_rows(s, 0)
                    if u == 18 and 0 <= s - 1 < BATCH:
                        take_output(s - 1, 0)
                    if u == 24 and 0 <= s - 1 < BATCH:
                        take_normalized(s - 1, 0)
                    if u == 26 and 0 <= s - 2:
                        take_x2(s - 2)
                    if 0 <= s - 1 < BATCH:
                        exponential(s - 1, u)
                if 0 <= s - 1 < BATCH:
                    take_output(s - 1, 1)

        @block.vector
        def _(dve):
            chain = [0]

            def link(ins):
                chain[0] += 1
                ins.then_inc(dve_chain, 1)
                dve.wait_ge(dve_chain, chain[0])

            def norm(b):
                if b:
                    dve.wait_ge(a_filled, nth_a["x", b - 1] + 1)
                h = m.h[:, b * TPB:(b + 1) * TPB, :]
                layer_norm_stats(nc, link, h, stats, moments).then_inc(moments_ready, 1)
                dve.wait_ge(inv_std_ready, b + 1)
                layer_norm_apply(nc, h, moments, inv_std, xn).then_inc(xn_ready, 1)

            def split(b):
                for n, (name, bank, read) in enumerate((("q", bank_b, b_read), ("k", bank_c, c_read))):
                    dve.wait_ge(high_ready, 2 * b + n + 1)
                    if b:
                        dve.wait_ge(low_ready, 2 * (b - 1) + n + 1)
                    nc.vector.scalar_tensor_tensor(rest[name][:, :], bank[:, :], q_scale if name == "q" else 1.0,
                                                   parts[name][:, 0, :], ALU.mult, ALU.subtract
                                                   ).then_inc(read, 1)

            def row_max(b, u):
                n = b * UNITS + u
                width = (u % TPB + 1) * P if causal else SEQ
                g, col = u // (UNITS // NG), u % (UNITS // NG)
                dve.wait_ge(q_scores, n + 1)
                if u == 0 and b:
                    dve.wait_ge(max_parts_ready, 2 * b)
                nc.vector.tensor_reduce(neg_max[:, g, col:col + 1], bank_q[n % 2][:, 0:width], AX.X, ALU.max,
                                        negate=True).then_inc(q_scores_read, 1)

            def split_max(b, g):
                dve.wait_ge(q_scores_read, b * UNITS + (g + 1) * UNITS // NG)
                if b:
                    dve.wait_ge(a_filled, nth_a["max", b - 1, g] + 1)
                link(nc.vector.tensor_copy(max_parts[:, g, 0, :], neg_max[:, g, :]))
                link(nc.vector.tensor_tensor(max_rest[:, g, :], neg_max[:, g, :], max_parts[:, g, 0, :], ALU.subtract))
                link(nc.vector.tensor_copy(max_parts[:, g, 1, :], max_rest[:, g, :]))
                nc.vector.tensor_tensor(max_parts[:, g, 2, :], max_rest[:, g, :], max_parts[:, g, 1, :],
                                        ALU.subtract).then_inc(max_parts_ready, 1)

            def normalize(b, g):
                dve.wait_ge(b_filled, nth_b["turn", b, g] + 1)
                if b + g:
                    before = (b, 0) if g else (b - 1, 1)
                    dve.wait_ge(b_filled, nth_b[("back",) + before] + 1)
                turned = bank_b[:, :].rearrange("p (q d) -> p q d", d=2 * HD)
                nc.vector.reciprocal(inv_sums[:, :].unsqueeze(2), turned[:, :, HD:HD + 1]).then_inc(inverted, 1)
                dve.wait_ge(inverted, b * NG + g + 1)
                nc.vector.tensor_tensor(o_tok[:, :, :], turned,
                                        inv_sums[:, :].unsqueeze(2).to_broadcast([P, TPB * GH, 2 * HD]), ALU.mult
                                        ).then_inc(b_read, 1)

            def add_output(b):
                dve.wait_ge(c_filled, nth_c["y", b] + 1)
                rows = m.h[:, b * TPB:(b + 1) * TPB, :]
                nc.vector.tensor_tensor(rows, rows, bank_c[:, :].rearrange("p (t d) -> p t d", t=TPB),
                                        ALU.add).then_inc(c_read, 1)

            def stats_2(b):
                dve.wait_ge(c_read, nth_c["y", b] + 1)
                if b:
                    dve.wait_ge(xn2_ready, b)
                layer_norm_stats(nc, link, m.h[:, b * TPB:(b + 1) * TPB, :], stats2, moments2).then_inc(moments2_ready, 1)

            def norm_2(b):
                dve.wait_ge(inv_std2_ready, b + 1)
                if b:
                    dve.wait_ge(a_filled, nth_a["x2", b - 1] + 1)
                    dve.wait_ge(rows_out, 16 * b)
                layer_norm_apply(nc, m.h[:, b * TPB:(b + 1) * TPB, :], moments2, inv_std2, xn2).then_inc(xn2_ready, 1)

            def take_logits(b):
                dve.wait_ge(c_filled, nth_c["logits", b] + 1)
                nc.vector.tensor_tensor(m.logits[:, b * TPB:(b + 1) * TPB, :],
                                        bank_c[:, 0:TPB * E].rearrange("p (t e) -> p t e", e=E),
                                        m.router_b[:, layer, :].unsqueeze(1).to_broadcast([P, TPB, E]), ALU.add
                                        ).then_inc(c_read, 1)

            norm(0)
            for buf in range(3):
                nc.vector.memset(v_ext[:, buf, :, :, HD:2 * HD], 0.0).then_inc(v_ext_zero, 1)
            for buf in range(3):
                dve.wait_ge(v_ext_zero, buf + 1)
                nc.vector.memset(v_ext[:, buf, :, :, HD:HD + 1], 1.0).then_inc(v_ext_zero, 1)
            split(0)
            for s in range(STEPS):
                for u in range(UNITS):
                    if u == 1 and s + 1 < BATCH:
                        norm(s + 1)
                    if u == 4 and 0 <= s - 2:
                        normalize(s - 2, 1)
                    if u == 11 and s + 1 < BATCH:
                        split(s + 1)
                    if u == 14 and 0 <= s - 2:
                        add_output(s - 2)
                        stats_2(s - 2)
                    if u == 16 and 0 <= s - 2:
                        norm_2(s - 2)
                    if u == 30 and 0 <= s - 2:
                        take_logits(s - 2)
                    if u == 17 and s < BATCH:
                        split_max(s, 0)
                    if u == 21 and 0 <= s - 1 < BATCH:
                        normalize(s - 1, 0)
                    if s < BATCH:
                        row_max(s, u)
                if s < BATCH:
                    split_max(s, 1)

        @block.tensor
        def _(pe):
            ident = m.fconst[:, FC_IDENT:FC_IDENT + P]
            ident_bf = m.bconst[:, BC_IDENT, :]

            def free(read, nth, key):
                if nth[key]:
                    pe.wait_ge(read, nth[key])

            def turn_x(b):
                pe.wait_ge(xn_ready, b + 1)
                free(a_read, nth_a, ("x", b))
                for t in range(TPB):
                    last = nc.tensor.transpose(bank_a[:, t * P:(t + 1) * P], xn[:, t, :], ident)
                last.then_inc(a_filled, 1)

            def project(b):
                pe.wait_ge(a_read, nth_a["x", b] + 1)
                w = m.w_qkv[:, layer, :]
                free(b_read, nth_b, ("q", b))
                nc.tensor.matmul(bank_b[:, :], w[:, 0:D], x_t[:, :], start=True, stop=True).then_inc(b_filled, 1)
                free(c_read, nth_c, ("k", b))
                nc.tensor.matmul(bank_c[:, :], w[:, D:2 * D], x_t[:, :], start=True, stop=True).then_inc(c_filled, 1)
                for t in range(TPB):
                    last = nc.tensor.matmul(bank_a[:, t * P:(t + 1) * P], x_t[:, t * P:(t + 1) * P],
                                            w[:, 2 * D:3 * D], start=True, stop=True)
                last.then_inc(a_filled, 1)

            def score_q(b, u):
                n, h, qi = b * UNITS + u, u // TPB, u % TPB
                if u == 0:
                    pe.wait_ge(pack_in[b % 2], 16 * n_loads * (b // 2 + 1))
                if n >= 2:
                    pe.wait_ge(q_scores_read, n - 1)
                q = q_pack[:, b % 3, h, qi * P:(qi + 1) * P]
                k = k_pack[:, b % 3, h, :]
                out = bank_q[n % 2]
                lo = qi * P
                if causal:
                    nc.tensor.matmul(out[:, 0:lo + P], q[0:R_DOT], k[0:R_DOT, 0:lo + P], start=True, stop=False,
                                     skip_group_check=True)
                else:
                    if qi:
                        nc.tensor.matmul(out[:, 0:lo], q[0:R_ALL], k[0:R_ALL, 0:lo], start=True, stop=True,
                                         skip_group_check=True)
                    nc.tensor.matmul(out[:, lo:], q[0:R_DOT], k[0:R_DOT, lo:], start=True, stop=False,
                                     skip_group_check=True)
                nc.tensor.matmul(out[:, lo:lo + P], ident_bf, m.bconst[:, diag_q, :], start=False, stop=True,
                                 skip_group_check=True).then_inc(q_scores, 1)

            def turn_max(b, g):
                pe.wait_ge(max_parts_ready, b * NG + g + 1)
                free(a_read, nth_a, ("max", b, g))
                nc.tensor.transpose(bank_a[0:48, 0:P // 2].bitcast(BF16),
                                    max_parts[:, g, :, :].rearrange("p s c -> p (s c)"), ident_bf).then_inc(a_filled, 1)

            def score_k(b, u):
                n, h, ki = b * UNITS + u, (u // (GH * TPB)) * GH + u % GH, (u // GH) % TPB
                if u % (UNITS // NG) == 0:
                    pe.wait_ge(max_in[u // (UNITS // NG)], 48 * (b + 1))
                if n >= 2:
                    pe.wait_ge(probs_ready, n - 1)
                k = k_pack[:, b % 3, h, ki * P:(ki + 1) * P]
                q = q_pack[:, b % 3, h, :]
                out = bank_k[n % 2]
                lo = ki * P
                if causal:
                    nc.tensor.matmul(out[:, lo:], k[0:R_MAX], q[0:R_MAX, lo:], start=True, stop=False,
                                     skip_group_check=True)
                else:
                    if lo + P < SEQ:
                        nc.tensor.matmul(out[:, lo + P:], k[0:R_ALL], q[0:R_ALL, lo + P:], start=True, stop=True,
                                         skip_group_check=True)
                    nc.tensor.matmul(out[:, 0:lo + P], k[0:R_MAX], q[0:R_MAX, 0:lo + P], start=True, stop=False,
                                     skip_group_check=True)
                nc.tensor.matmul(out[:, lo:lo + P], ident_bf, m.bconst[:, diag_k, :], start=False, stop=True,
                                 skip_group_check=True).then_inc(k_scores, 1)

            def times_v(b, pv):
                g, ki = pv // TPB, pv % TPB
                n = b * UNITS + pv * GH
                first = ki * P if causal else 0
                pe.wait_ge(probs_ready, n + GH)
                if ki == 0 and b * NG + g:
                    pe.wait_ge(o_read, b * NG + g)
                for j in range(GH):
                    last = nc.tensor.matmul(bank_o[32 * j:32 * j + 32, first:], v_ext[:, b % 3, ki, g * GH + j, :],
                                            probs[:, (n + j) % 8, first:], start=(ki == 0), stop=(ki == TPB - 1),
                                            skip_group_check=True)
                last.then_inc(pv_done, 1)

            def turn_output(b, g):
                pe.wait_ge(o_read, b * NG + g + 1)
                free(b_read, nth_b, ("turn", b, g))
                for t in range(TPB):
                    last = nc.tensor.transpose(bank_b[:, t * P:(t + 1) * P], o_raw[:, g, t * P:(t + 1) * P], ident)
                last.then_inc(b_filled, 1)

            def turn_back(b, g):
                free(b_read, nth_b, ("back", b, g))
                for t in range(TPB):
                    last = nc.tensor.transpose(bank_b[:, t * P:(t + 1) * P],
                                               o_tok[:, t * GH:(t + 1) * GH, :].rearrange("p j d -> p (j d)"), ident)
                last.then_inc(b_filled, 1)

            def project_out(b):
                pe.wait_ge(b_read, nth_b["back", b, 1] + 1)
                free(c_read, nth_c, ("y", b))
                for t in range(TPB):
                    for g in range(NG):
                        last = nc.tensor.matmul(bank_c[:, t * P:(t + 1) * P], o_norm[:, g, t * P:(t + 1) * P],
                                                m.w_o[:, layer, g, :], start=(g == 0), stop=(g == NG - 1))
                last.then_inc(c_filled, 1)

            def turn_x2(b):
                pe.wait_ge(xn2_ready, b + 1)
                free(a_read, nth_a, ("x2", b))
                for t in range(TPB):
                    last = nc.tensor.transpose(bank_a[:, t * P:(t + 1) * P], xn2[:, t, :], ident)
                last.then_inc(a_filled, 1)

            def route(b):
                pe.wait_ge(a_read, nth_a["x2", b] + 1)
                free(c_read, nth_c, ("logits", b))
                for t in range(TPB):
                    last = nc.tensor.matmul(bank_c[:, t * E:(t + 1) * E],
                                            m.x2_t[:, b % m.x2_t.shape[1], t * P:(t + 1) * P],
                                            m.router_w[:, layer, :], start=True, stop=True)
                last.then_inc(c_filled, 1)

            if layer == 0:
                pe.wait_ge(m.attn_w_in, 16 * 9)
                pe.wait_ge(m.bconst_in, 16)
            turn_x(0)
            project(0)
            for s in range(STEPS):
                for u in range(UNITS):
                    if u == 2 and 0 <= s - 1 < BATCH:
                        turn_max(s - 1, 1)
                    if u == 3 and 0 <= s - 2:
                        turn_output(s - 2, 1)
                    if u == 4 and s + 1 < BATCH:
                        turn_x(s + 1)
                    if u == 6 and 0 <= s - 2:
                        turn_back(s - 2, 1)
                    if u == 9 and s + 1 < BATCH:
                        project(s + 1)
                    if u == 18 and s < BATCH:
                        turn_max(s, 0)
                    if u == 20 and 0 <= s - 1 < BATCH:
                        turn_output(s - 1, 0)
                    if u == 23 and 0 <= s - 1 < BATCH:
                        turn_back(s - 1, 0)
                    if u == 12 and 0 <= s - 2:
                        project_out(s - 2)
                    if u == 25 and 0 <= s - 2:
                        turn_x2(s - 2)
                    if u == 28 and 0 <= s - 2:
                        route(s - 2)
                    if s < BATCH:
                        score_q(s, u)
                    if 0 <= s - 1 < BATCH:
                        score_k(s - 1, u)
                        if u % GH == 1 and u > GH:
                            times_v(s - 1, u // GH - 1)
                if 0 <= s - 1 < BATCH:
                    times_v(s - 1, UNITS // GH - 1)


def expert_of(nc, engine, tile_expert, tile):
    return nc.values_load(tile_expert[0:1, tile:tile + 1], engines=[engine], min_val=0, max_val=E - 1,
                          skip_runtime_bounds_check_because="a minimum on the chip bounds it")


def moe_phase(nc, m, layer):
    first = layer == 0
    width = DFF if first else 2 * I1
    with ExitStack() as ctx:
        def sb(name, shape, dt=F32):
            return ctx.enter_context(nc.sbuf_tensor(f"{name}_m{layer}", shape, dt))

        sems = []

        def sem(name):
            sems.append(ctx.enter_context(nc.semaphore(f"m{layer}_{name}")))
            return sems[-1]

        logits, lower = m.logits, sb("lower", [P, NT, E])
        weighed, expd = sb("weighed", [P, NT, E]), sb("expd", [P, NT, E])
        chosen = sb("chosen", [P, 2, NT, E])
        top, rank = sb("top", [P, 2, NT]), sb("rank", [P, NT])
        gap, gap_exp, total = sb("gap", [P, NT]), sb("gap_exp", [P, NT]), sb("total", [P, NT])
        gate = sb("gate", [P, 2, NT])
        marks = sb("marks", [P, 2 * NT + 1, E], BF16)
        ranks = sb("ranks", [P, NT, E])
        over = sb("over", [P, E, NT])
        n_tiles, zeros_e, ends, starts = sb("n_tiles", [P, E]), sb("zeros_e", [P, E]), sb("ends", [P, E]), sb("starts", [P, E])
        pos, pos_i, row_i = sb("pos", [P, 2 * NT]), sb("pos_i", [P, 2 * NT], I32), sb("row_i", [P, 2 * NT], I32)
        row, tile128 = sb("row", [P, 2 * NT]), sb("tile128", [P, 2 * NT])
        row_hot = sb("row_hot", [P, 2 * NT, P], BF16)
        tile_hot = sb("tile_hot", [P, 2 * NT, 3, TILES], BF16)
        pair, wrap, pad = sb("pair", [P, TILES]), sb("wrap", [P, TILES]), sb("pad", [P, TILES])
        src_row, dst_row = sb("src_row", [P, TILES], I32), sb("dst_row", [P, TILES], I32)
        before, tile_expert = sb("before", [P, TILES, E]), sb("tile_expert", [P, TILES], I32)
        expert_f = sb("expert_f", [P, TILES])
        x_rows, y_rows = sb("x_rows", [P, RING, D]), sb("y_rows", [P, RING, D])
        xt = sb("xt", [P, 2, P])
        y_sel = sb("y_sel", [P, 2, 2, TPB, D])
        if first:
            h_pre, h_act = sb("h_pre", [P, 2, DFF]), sb("h_act", [P, 2, DFF])
        else:
            h_pre = sb("h_pre", [P, 2, I1, 2])
            g_cl, u_cl, g_al, sig = [sb(n, [P, 2, I1]) for n in ("g_cl", "u_cl", "g_al", "sig")]
            gu, te, te_t = sb("gu", [P, 2, I1]), sb("te", [P, 2, I1]), sb("te_t", [I1, 2, P])
            soft = sb("soft", [P, 4, NE1, 2])
            s_pre, s_sig, s_te = sb("s_pre", [I1, 2, SEQ]), sb("s_sig", [I1, SEQ]), sb("s_te", [I1 + 1, SEQ])

        bank_rank, bank_pairs = m.bank[3], m.bank[2]
        bank_up, bank_down = m.bank[2:4], m.bank[6:8]
        bank_turn = m.bank[0:2] if first else [m.bank[0]] * 2
        bank_mid = m.bank[4:6] if first else [m.bank[4]] * 2
        bank_shared = [m.bank[1], m.bank[5]]

        dve_chain = sem("dve_chain")
        weighed_ready, expd_ready = sem("weighed_ready"), sem("expd_ready")
        marks_ready, ranks_done = sem("marks_ready"), sem("ranks_done")
        pos_ready, row_hot_ready, tile_hot_ready = sem("pos_ready"), sem("row_hot_ready"), sem("tile_hot_ready")
        pairs_done, order_ready = sem("pairs_done"), sem("order_ready")
        x_in, y_out = m.x_in[layer], m.y_out[layer]
        turned, xt_ready, up_done = sem("turned"), sem("xt_ready"), sem("up_done")
        pre_ready, mid_turned, act_ready = sem("pre_ready"), sem("mid_turned"), sem("act_ready")
        down_done, y_ready = sem("down_done"), sem("y_ready")
        y_in, added = [sem("y_in_even"), sem("y_in_odd")], sem("added")
        if not first:
            soft_in, soft_ready = sem("soft_in"), sem("soft_ready")
            s_up, s_biased, s_clipped, s_sig_ready = sem("s_up"), sem("s_biased"), sem("s_clipped"), sem("s_sig_ready")
            s_te_ready, s_down, s_added, s_sum = sem("s_te_ready"), sem("s_down"), sem("s_added"), sem("s_sum")
            sig_asked, g_kept = sem("sig_asked"), sem("g_kept")
        shared_at = {SHARED_FIRST + SHARED_EVERY * b: b for b in range(0 if first else BATCH)}
        if first:
            ctx.callback(clear_semaphores, nc, sems)
        block = ctx.enter_context(nc.Block())

        @block.sync
        def _(sp):
            for r in range(RING):
                sp.wait_ge(y_out[r], 16 * len(range(r, TILES, RING)))
            for b in range(BATCH):
                if b >= 2:
                    sp.wait_ge(added, b - 1)
                for k in range(2):
                    sp.dma_start(y_sel[:, b % 2, k, :, :],
                                 m.y_rows_d[k * TOK + b * SEQ:k * TOK + (b + 1) * SEQ, :].rearrange(
                                     "(t p) d -> p t d", p=P)).then_inc(y_in[b % 2], 16)
            if not first:
                for b in range(BATCH):
                    sp.wait_ge(added, b + 1)
                    sp.dma_start(m.out[b].rearrange("(t p) d -> p t d", p=P),
                                 m.h[:, b * TPB:(b + 1) * TPB, :]).then_inc(m.out_done, 16)
                sp.wait_ge(m.out_done, 16 * BATCH)

        @block.gpsimd
        def _(pool):
            def gather(tile):
                if tile >= RING:
                    pool.wait_ge(turned, tile - RING + 1)
                    pool.nop(nofuse=True)
                pool.indirect_dma_start(x_rows[:, tile % RING, :], None, m.x_rows_d,
                                        bass.IndirectOffsetOnAxis(ap=src_row[:, tile:tile + 1], axis=0)
                                        ).then_inc(x_in[tile % RING], 16)

            def scatter(tile):
                pool.wait_ge(y_ready, tile + 1)
                pool.nop(nofuse=True)
                pool.indirect_dma_start(m.y_rows_d, bass.IndirectOffsetOnAxis(ap=dst_row[:, tile:tile + 1], axis=0),
                                        y_rows[:, tile % RING, :], None).then_inc(y_out[tile % RING], 16)

            pool.wait_ge(order_ready, 3)
            for tile in range(RING):
                gather(tile)
            for tile in range(TILES):
                if tile + RING < TILES:
                    gather(tile + RING)
                scatter(tile)

        @block.scalar
        def _(act):
            if not first:
                act.wait_ge(soft_in, 1)
                nc.scalar.activation(soft[:, 1, :, :], soft[:, 0, :, :], ACT.Exp, scale=-1.0).then_inc(soft_ready, 1)
                act.wait_ge(soft_ready, 1)
                nc.scalar.activation(soft[:, 2, :, :], soft[:, 1, :, :], ACT.Ln, bias=1.0).then_inc(soft_ready, 1)
            act.wait_ge(weighed_ready, 1)
            nc.scalar.activation(expd[:, :, :], weighed[:, :, :], ACT.Exp).then_inc(expd_ready, 1)
            nc.scalar.activation(gap_exp[:, :], gap[:, :], ACT.Exp).then_inc(expd_ready, 1)
            act.wait_ge(order_ready, 3)
            nc.scalar.activation(gap[0:1, 0:1], gap_exp[0:1, 0:1], ACT.Gelu if first else ACT.Sigmoid)

            def hidden(tile):
                e = expert_of(nc, ENGINE.Activation, tile_expert, tile)
                act.wait_ge(mid_turned, tile + 1)
                if tile >= 2:
                    act.wait_ge(down_done, tile - 1)
                for c in range(FC):
                    last = nc.scalar.activation(h_act[:, tile % 2, c * P:(c + 1) * P],
                                                bank_mid[tile % 2][:, c * P:(c + 1) * P], ACT.Gelu,
                                                bias=m.b1[:, bass.ds(e * FC + c, 1)])
                last.then_inc(act_ready, 1)

            def take_x(tile):
                act.wait_ge(turned, tile + 1)
                if tile >= 2:
                    act.wait_ge(up_done, tile - 1)
                nc.scalar.activation(xt[:, tile % 2, :], bank_turn[tile % 2][:, 0:P], ACT.Copy).then_inc(xt_ready, 1)

            def take_mid(tile):
                act.wait_ge(mid_turned, tile + 1)
                if tile >= 2:
                    act.wait_ge(down_done, tile - 1)
                nc.scalar.activation(te_t[:, tile % 2, :], bank_mid[tile % 2][0:I1, 0:P], ACT.Copy).then_inc(act_ready, 1)

            def shared_bias(b):
                act.wait_ge(s_up, b + 1)
                if b:
                    act.wait_ge(s_te_ready, 2 * b)
                for n in range(2):
                    nc.scalar.activation(s_pre[:, n, :], bank_shared[n][0:I1, :], ACT.Identity,
                                         bias=m.s_b1[:, n:n + 1]).then_inc(s_biased, 1)

            def shared_sigmoid(b):
                act.wait_ge(s_clipped, 2 * b + 1)
                nc.scalar.activation(s_sig[:, :], s_pre[:, 0, :], ACT.Sigmoid,
                                     scale=m.e_act[0:I1, E, 0:1]).then_inc(s_sig_ready, 1)

            def sigmoid(tile):
                act.wait_ge(sig_asked, tile + 1)
                if tile >= 2:
                    act.wait_ge(pre_ready, tile - 1)
                nc.scalar.activation(sig[:, tile % 2, :], g_al[:, tile % 2, :], ACT.Sigmoid).then_inc(g_kept, 1)

            if first:
                for tile in range(TILES):
                    hidden(tile)
            else:
                take_x(0)
                for tile in range(TILES + 1):
                    if tile + 1 < TILES:
                        take_x(tile + 1)
                    if tile >= 1:
                        take_mid(tile - 1)
                    if tile < TILES:
                        sigmoid(tile)
                    if tile - 1 in shared_at:
                        shared_bias(shared_at[tile - 1])
                    if tile - 3 in shared_at:
                        shared_sigmoid(shared_at[tile - 3])

        @block.vector
        def _(dve):
            chain = [0]

            def link(ins):
                chain[0] += 1
                ins.then_inc(dve_chain, 1)
                dve.wait_ge(dve_chain, chain[0])

            def over_tiles(ap):
                return ap.unsqueeze(2).to_broadcast([P, NT, E])

            def over_experts(ap):
                return ap.unsqueeze(1).to_broadcast([P, NT, E])

            def shared_clip(b):
                for n in range(2):
                    dve.wait_ge(s_biased, 2 * b + n + 1)
                    nc.vector.tensor_scalar(s_pre[:, n, :], s_pre[:, n, :], soft[0:I1, 1, E, n:n + 1],
                                            soft[0:I1, 3, E, n:n + 1], ALU.min, ALU.max).then_inc(s_clipped, 1)

            def shared_product(b):
                dve.wait_ge(s_sig_ready, b + 1)
                dve.wait_ge(s_clipped, 2 * b + 2)
                if b:
                    dve.wait_ge(s_down, b)
                nc.vector.scalar_tensor_tensor(s_te[0:I1, :], s_pre[:, 1, :], m.e_act[0:I1, E, 2:3],
                                               s_pre[:, 0, :], ALU.add, ALU.mult).then_inc(s_te_ready, 1)

            def shared_gate(b):
                dve.wait_ge(s_te_ready, 2 * b + 1)
                nc.vector.scalar_tensor_tensor(s_te[0:I1, :], s_te[0:I1, :], m.e_act[0:I1, E, 1:2],
                                               s_sig[:, :], ALU.mult, ALU.mult).then_inc(s_te_ready, 1)

            def shared_add(b):
                dve.wait_ge(s_down, b + 1)
                h = m.h[:, b * TPB:(b + 1) * TPB, :]
                nc.vector.tensor_tensor(h, h, bank_shared[0][:, :].rearrange("p (t d) -> p t d", t=TPB), ALU.add
                                        ).then_inc(s_added, 1)

            if not first:
                dve.wait_ge(m.experts_now, 16 * len(m.expert_loads))
                link(nc.vector.tensor_scalar(soft[:, 3, :, :], m.e_act[:, :, 3:5], -1.0, None, ALU.mult))
                nc.vector.tensor_tensor(soft[:, 0, :, :], m.e_act[:, :, 3:5], soft[:, 3, :, :], ALU.max).then_inc(soft_in, 1)
                dve.wait_ge(soft_ready, 2)
                link(nc.vector.scalar_tensor_tensor(soft[:, 1, :, :], m.e_act[:, :, 3:5], 0.0, soft[:, 2, :, :],
                                                    ALU.max, ALU.add))
                link(nc.vector.tensor_scalar(soft[:, 3, :, :], soft[:, 1, :, :], -1.0, None, ALU.mult))
                link(nc.vector.memset(s_te[I1:I1 + 1, :], 1.0))

            rank_e = over_experts(m.fconst[:, FC_RANK:FC_RANK + E])
            values = logits
            for k in range(2):
                link(nc.vector.tensor_reduce(top[:, k, :], values[:, :, :], AX.X, ALU.max))
                link(nc.vector.tensor_tensor(chosen[:, k, :, :], values[:, :, :], over_tiles(top[:, k, :]), ALU.is_equal))
                link(nc.vector.tensor_tensor(chosen[:, k, :, :], chosen[:, k, :, :], rank_e, ALU.mult))
                link(nc.vector.tensor_reduce(rank[:, :], chosen[:, k, :, :], AX.X, ALU.max))
                link(nc.vector.tensor_tensor(chosen[:, k, :, :], rank_e, over_tiles(rank[:, :]), ALU.is_equal))
                if k == 0:
                    link(nc.vector.scalar_tensor_tensor(lower[:, :, :], chosen[:, 0, :, :], MASKED, logits[:, :, :],
                                                        ALU.mult, ALU.add))
                    values = lower
            link(nc.vector.memset(marks[:, 0:NT, :], 0.0))
            link(nc.vector.memset(marks[:, 2 * NT, :], 0.0))
            nc.vector.tensor_tensor(marks[:, NT:2 * NT, :], chosen[:, 0, :, :], chosen[:, 1, :, :], ALU.add).then_inc(marks_ready, 1)
            link(nc.vector.tensor_tensor(gap[:, :], top[:, 1, :], top[:, 0, :], ALU.subtract))
            nc.vector.tensor_tensor(weighed[:, :, :], logits[:, :, :], over_tiles(top[:, 0, :]), ALU.subtract
                                    ).then_inc(weighed_ready, 1)
            link(nc.vector.memset(zeros_e[:, :], 0.0))

            dve.wait_ge(ranks_done, 1)
            rank_bank = bank_rank[:, 0:(NT + 1) * E].rearrange("p (t e) -> p t e", e=E)
            link(nc.vector.tensor_tensor(over[:, :, :], rank_bank[:, NT, :].unsqueeze(2).to_broadcast([P, E, NT]),
                                         m.fconst[:, FC_J128:FC_J128 + NT].unsqueeze(1).to_broadcast([P, E, NT]),
                                         ALU.is_gt))
            link(nc.vector.tensor_reduce(n_tiles[:, :], over[:, :, :], AX.X, ALU.add))
            link(nc.vector.tensor_tensor_scan(ends[:, :], n_tiles[:, :], zeros_e[:, :], 0.0, ALU.add, ALU.add))
            link(nc.vector.tensor_tensor(starts[:, :], ends[:, :], n_tiles[:, :], ALU.subtract))
            link(nc.vector.scalar_tensor_tensor(ranks[:, :, :], over_experts(starts[:, :]), float(P),
                                                rank_bank[:, 0:NT, :], ALU.mult, ALU.add))
            for k in range(2):
                link(nc.vector.tensor_tensor(chosen[:, k, :, :], chosen[:, k, :, :], ranks[:, :, :], ALU.mult))
                link(nc.vector.tensor_reduce(pos[:, k * NT:(k + 1) * NT], chosen[:, k, :, :], AX.X, ALU.add))
            link(nc.vector.tensor_copy(pos_i[:, :], pos[:, :]))
            link(nc.vector.tensor_single_scalar(row_i[:, :], pos_i[:, :], P - 1, ALU.bitwise_and))
            link(nc.vector.tensor_copy(row[:, :], row_i[:, :]))
            nc.vector.tensor_tensor(tile128[:, :], pos[:, :], row[:, :], ALU.subtract).then_inc(pos_ready, 1)
            dve.wait_ge(pos_ready, 1)
            hot = tile_hot[:, :, 0, :]
            link(nc.vector.tensor_tensor(
                hot, tile128[:, :].unsqueeze(2).to_broadcast([P, 2 * NT, TILES]),
                m.fconst[:, FC_A128:FC_A128 + TILES].unsqueeze(1).to_broadcast([P, 2 * NT, TILES]), ALU.is_equal))
            nc.vector.tensor_scalar(tile_hot[:, :, 1, :], hot, m.fconst[:, FC_PART:FC_PART + 1], None, ALU.mult
                                    ).then_inc(tile_hot_ready, 1)
            nc.vector.tensor_tensor(
                tile_hot[:, :, 2, :], hot,
                m.fconst[:, FC_KT:FC_KT + 2 * NT].unsqueeze(2).to_broadcast([P, 2 * NT, TILES]), ALU.mult
            ).then_inc(tile_hot_ready, 1)
            nc.vector.tensor_tensor(
                row_hot[:, :, :], row[:, :].unsqueeze(2).to_broadcast([P, 2 * NT, P]),
                m.fconst[:, FC_IOTA:FC_IOTA + P].unsqueeze(1).to_broadcast([P, 2 * NT, P]), ALU.is_equal
            ).then_inc(row_hot_ready, 1)
            link(nc.vector.tensor_tensor(
                before[:, :, :], ends[:, :].unsqueeze(1).to_broadcast([P, TILES, E]),
                m.fconst[:, FC_TILE:FC_TILE + TILES].unsqueeze(2).to_broadcast([P, TILES, E]), ALU.is_le))
            link(nc.vector.tensor_reduce(expert_f[:, :], before[:, :, :], AX.X, ALU.add))
            nc.vector.tensor_scalar(tile_expert[:, :], expert_f[:, :], float(E - 1), None, ALU.min).then_inc(order_ready, 1)
            dve.wait_ge(expd_ready, 2)
            link(nc.vector.tensor_reduce(total[:, :], expd[:, :, :], AX.X, ALU.add))
            link(nc.vector.reciprocal(gate[:, 0, :], total[:, :]))
            link(nc.vector.tensor_tensor(gate[:, 1, :], gap_exp[:, :], gate[:, 0, :], ALU.mult))
            if not first:
                link(nc.vector.tensor_tensor(total[:, :], gate[:, 0, :], gate[:, 1, :], ALU.add))
                link(nc.vector.reciprocal(rank[:, :], total[:, :]))
                for k in range(2):
                    link(nc.vector.tensor_tensor(gate[:, k, :], gate[:, k, :], rank[:, :], ALU.mult))
            dve.wait_ge(pairs_done, 1)
            counted, part, kt = [bank_pairs[:, n * TILES:(n + 1) * TILES] for n in range(3)]
            link(nc.vector.tensor_scalar(wrap[:, :], kt, float(NT), -float(TOK), ALU.is_ge, ALU.mult))
            link(nc.vector.tensor_scalar(pad[:, :], counted, -1.0, 1.0, ALU.mult, ALU.add))
            link(nc.vector.tensor_scalar(pair[:, :], kt, float(P), None, ALU.mult))
            link(nc.vector.tensor_tensor(pair[:, :], pair[:, :], part, ALU.add))
            link(nc.vector.tensor_tensor(pad[:, :], pad[:, :], m.fconst[:, FC_TRASH:FC_TRASH + TILES], ALU.mult))
            nc.vector.tensor_tensor(src_row[:, :], pair[:, :], wrap[:, :], ALU.add).then_inc(order_ready, 1)
            nc.vector.tensor_tensor(dst_row[:, :], pair[:, :], pad[:, :], ALU.add).then_inc(order_ready, 1)
            dve.wait_ge(order_ready, 3)

            def take_x(tile):
                dve.wait_ge(turned, tile + 1)
                if tile >= 2:
                    dve.wait_ge(up_done, tile - 1)
                nc.vector.tensor_copy(xt[:, tile % 2, :], bank_turn[tile % 2][:, 0:P]).then_inc(xt_ready, 1)

            def take_up(tile):
                dve.wait_ge(up_done, tile + 1)
                if tile >= 2:
                    dve.wait_ge(mid_turned, tile - 1)
                nc.vector.tensor_copy(h_pre[:, tile % 2, :], bank_up[tile % 2][:, :]).then_inc(pre_ready, 1)

            def take_y(tile, e):
                r = tile % RING
                dve.wait_ge(down_done, tile + 1)
                if tile >= RING:
                    dve.wait_ge(y_out[r], 16 * (tile // RING))
                nc.vector.tensor_tensor(y_rows[:, r, :], bank_down[tile % 2][:, 0:D], m.b2_all[:, bass.ds(e * D, D)], ALU.add
                                        ).then_inc(y_ready, 1)

            def front_1(tile, e):
                p = tile % 2
                dve.wait_ge(up_done, tile + 1)
                nc.vector.tensor_tensor(h_pre[:, p, :, :].rearrange("p i c -> p (i c)"), bank_up[p][:, 0:2 * I1],
                                        m.e_b1[:, bass.ds(e * 2 * I1, 2 * I1)], ALU.add).then_inc(s_sum, 1)
                dve.wait_ge(s_sum, tile * 4 + 1)
                bound = lambda which, n: soft[:, which, bass.ds(e, 1), n:n + 1].rearrange("p a b -> p (a b)")
                scalar = lambda n: m.e_act[:, bass.ds(e, 1), n:n + 1].rearrange("p a b -> p (a b)")
                nc.vector.tensor_scalar(g_cl[:, p, :], h_pre[:, p, :, 0], bound(1, 0), bound(3, 0), ALU.min, ALU.max
                                        ).then_inc(s_sum, 1)
                nc.vector.tensor_scalar(u_cl[:, p, :], h_pre[:, p, :, 1], bound(1, 1), bound(3, 1), ALU.min, ALU.max
                                        ).then_inc(s_sum, 1)
                if tile >= 2:
                    dve.wait_ge(g_kept, tile - 1)
                dve.wait_ge(s_sum, tile * 4 + 2)
                nc.vector.tensor_scalar(g_al[:, p, :], g_cl[:, p, :], scalar(0), None, ALU.mult).then_inc(sig_asked, 1)
                dve.wait_ge(s_sum, tile * 4 + 3)
                nc.vector.scalar_tensor_tensor(gu[:, p, :], u_cl[:, p, :], scalar(2), g_cl[:, p, :], ALU.add, ALU.mult
                                               ).then_inc(s_sum, 1)

            def back_1(tile, e):
                p = tile % 2
                dve.wait_ge(g_kept, tile + 1)
                dve.wait_ge(s_sum, tile * 4 + 4)
                if tile >= 2:
                    dve.wait_ge(mid_turned, tile - 1)
                scalar = m.e_act[:, bass.ds(e, 1), 1:2].rearrange("p a b -> p (a b)")
                nc.vector.scalar_tensor_tensor(te[:, p, :], gu[:, p, :], scalar, sig[:, p, :], ALU.mult, ALU.mult
                                               ).then_inc(pre_ready, 1)

            experts = {}
            if first:
                take_x(0)
            for tile in range(TILES + 2):
                if tile < TILES:
                    experts[tile] = expert_of(nc, ENGINE.DVE, tile_expert, tile)
                    if first:
                        take_up(tile)
                    else:
                        front_1(tile, experts[tile])
                if first and tile + 1 < TILES:
                    take_x(tile + 1)
                if tile >= 2:
                    take_y(tile - 2, experts.pop(tile - 2))
                if tile < TILES and not first:
                    back_1(tile, experts[tile])
                for late, stage in ((2, shared_clip), (4, shared_product), (5, shared_gate), (7, shared_add)):
                    if tile - late in shared_at:
                        stage(shared_at[tile - late])

            for b in range(BATCH):
                dve.wait_ge(y_in[b % 2], 32 * (b // 2 + 1))
                for k in range(2):
                    for t in range(TPB):
                        n = b * TPB + t
                        last = nc.vector.scalar_tensor_tensor(m.h[:, n, :], y_sel[:, b % 2, k, t, :], gate[:, k, n:n + 1],
                                                              m.h[:, n, :], ALU.mult, ALU.add)
                    if k == 0:
                        link(last)
                last.then_inc(added, 1)

        @block.tensor
        def _(pe):
            ident = m.fconst[:, FC_IDENT:FC_IDENT + P]
            pe.wait_ge(m.experts_now, 16 * len(m.expert_loads))

            def shared_up(b):
                if b:
                    pe.wait_ge(s_added, b)
                    pe.wait_ge(s_biased, 2 * b)
                for n in range(2):
                    w = m.s_w1[:, :].rearrange("p (i c) -> p c i", c=2)[:, n, :]
                    last = nc.tensor.matmul(bank_shared[n][0:I1, :], w, m.x2_t[:, b, :], start=True, stop=True)
                last.then_inc(s_up, 1)

            def shared_down(b):
                pe.wait_ge(s_te_ready, 2 * b + 2)
                for t in range(TPB):
                    last = nc.tensor.matmul(bank_shared[0][:, t * P:(t + 1) * P], s_te[:, t * P:(t + 1) * P],
                                            m.s_w2[:, :], start=True, stop=True)
                last.then_inc(s_down, 1)

            pe.wait_ge(marks_ready, 1)
            for s in range(NT + 1):
                last = nc.tensor.matmul(bank_rank[:, 0:(NT + 1) * E], m.bconst[:, BC_ONES if s else BC_TRI, :],
                                        marks[:, NT - s:2 * NT + 1 - s, :].rearrange("p t e -> p (t e)"),
                                        start=(s == 0), stop=(s == NT))
            last.then_inc(ranks_done, 1)
            pe.wait_ge(tile_hot_ready, 2)
            pe.wait_ge(row_hot_ready, 1)
            for g in range(2 * NT):
                last = nc.tensor.matmul(bank_pairs[:, 0:3 * TILES], row_hot[:, g, :],
                                        tile_hot[:, g, :, :].rearrange("p s a -> p (s a)"),
                                        start=(g == 0), stop=(g == 2 * NT - 1))
            last.then_inc(pairs_done, 1)
            pe.wait_ge(order_ready, 3)

            def turn(tile):
                pe.wait_ge(x_in[tile % RING], 16 * (tile // RING + 1))
                before = tile - (2 if first else 1)
                if before >= 0:
                    pe.wait_ge(xt_ready, before + 1)
                nc.tensor.transpose(bank_turn[tile % 2][:, 0:P], x_rows[:, tile % RING, :], ident).then_inc(turned, 1)

            def up(tile, e):
                pe.wait_ge(xt_ready, tile + 1)
                if tile >= 2:
                    if first:
                        pe.wait_ge(pre_ready, tile - 1)
                    else:
                        pe.wait_ge(s_sum, (tile - 2) * 4 + 1)
                w = m.w1 if first else m.e_w1
                nc.tensor.matmul(bank_up[tile % 2][:, 0:width], xt[:, tile % 2, :], w[:, bass.ds(e * width, width)],
                                 start=True, stop=True).then_inc(up_done, 1)

            def mid(tile):
                pe.wait_ge(pre_ready, tile + 1)
                before = tile - (2 if first else 1)
                if before >= 0:
                    pe.wait_ge(act_ready, before + 1)
                if first:
                    for c in range(FC):
                        last = nc.tensor.transpose(bank_mid[tile % 2][:, c * P:(c + 1) * P],
                                                   h_pre[:, tile % 2, c * P:(c + 1) * P], ident)
                else:
                    last = nc.tensor.transpose(bank_mid[tile % 2][0:I1, 0:P], te[:, tile % 2, :], ident)
                last.then_inc(mid_turned, 1)

            def down(tile, e):
                pe.wait_ge(act_ready, tile + 1)
                if tile >= 2:
                    pe.wait_ge(y_ready, tile - 1)
                if first:
                    for c in range(FC):
                        last = nc.tensor.matmul(bank_down[tile % 2][:, 0:D], h_act[:, tile % 2, c * P:(c + 1) * P],
                                                m.w2[:, bass.ds(e * DFF + c * D, D)], start=(c == 0), stop=(c == FC - 1))
                else:
                    last = nc.tensor.matmul(bank_down[tile % 2][:, 0:D], te_t[:, tile % 2, :],
                                            m.e_w2[:, bass.ds(e * D, D)], start=True, stop=True)
                last.then_inc(down_done, 1)

            experts = {}
            turn(0)
            for tile in range(TILES + 2):
                if tile < TILES:
                    experts[tile] = expert_of(nc, ENGINE.PE, tile_expert, tile)
                    up(tile, experts[tile])
                if tile + 1 < TILES:
                    turn(tile + 1)
                if not first and 1 <= tile <= TILES:
                    mid(tile - 1)
                if tile >= 2:
                    down(tile - 2, experts.pop(tile - 2))
                if first and tile < TILES:
                    mid(tile)
                if tile in shared_at:
                    shared_up(shared_at[tile])
                if tile - 6 in shared_at:
                    shared_down(shared_at[tile - 6])


def program(nc, io):
    with ExitStack() as ctx:
        def sb(name, shape, dt=F32):
            return ctx.enter_context(nc.sbuf_tensor(name, shape, dt))

        def dram(name, shape, dt=F32):
            return nc.dram_tensor(name, shape, dt, kind="Internal").ap()

        def sem(name):
            return ctx.enter_context(nc.semaphore(name))

        m = Memory()
        m.x, m.table, m.out, m.w_qkv_d = io["x"], io["table"], io["out"], io["w_qkv_d"]
        m.w_o_d, m.router_w_d, m.router_b_d, m.w1_d = io["w_o_d"], io["router_w_d"], io["router_b_d"], io["w1_d"]
        m.w2_d, m.b1_d, m.b2_d, m.e_w1_d = io["w2_d"], io["b1_d"], io["b2_d"], io["e_w1_d"]
        m.e_b1_d, m.e_w2_d, m.e_b2_d, m.e_act_d = io["e_b1_d"], io["e_w2_d"], io["e_b2_d"], io["e_act_d"]
        m.s_w1_d, m.s_b1_d, m.s_w2_d, m.s_b2_d = io["s_w1_d"], io["s_b1_d"], io["s_w2_d"], io["s_b2_d"]
        m.s_act_d, m.fconst_d, m.bconst_d, m.q_rows_d = io["s_act_d"], io["fconst_d"], io["bconst_d"], io["q_rows_d"]
        m.k_rows_d = io["k_rows_d"]
        m.h = sb("h", [P, NT, D])
        m.fconst = sb("fconst", [P, FC_END])
        m.bconst = sb("bconst", [P, BC_END, P], BF16)
        m.w_qkv = sb("w_qkv", [P, 2, 3 * D])
        m.w_o = sb("w_o", [P, 2, NG, D])
        m.router_w = sb("router_w", [P, 2, E])
        m.router_b = sb("router_b", [P, 2, E])
        m.parts_d = dram("parts_d", [BATCH, 2, 3, H, HD, SEQ], BF16)
        m.logits = sb("logits", [P, NT, E])
        m.x_rows_d = dram("x_rows_d", [TOK, D])
        m.y_rows_d = dram("y_rows_d", [PAIRS + SLOTS, D])
        m.bank = [ctx.enter_context(nc.psum_tensor(f"bank{i}", [P, 512], F32)) for i in range(8)]
        m.bconst_in, m.attn_w_in = sem("bconst_in"), sem("attn_w_in")
        m.out_done = sem("out_done")
        m.experts_in, m.experts2_in = sem("experts_in"), sem("experts2_in")

        m.rows_in = sem("rows_in")
        m.x_in = [[sem(f"x_in_{layer}_{r}") for r in range(RING)] for layer in range(2)]
        m.y_out = [[sem(f"y_out_{layer}_{r}") for r in range(RING)] for layer in range(2)]

        with ExitStack() as experts:
            def esb(name, shape):
                return experts.enter_context(nc.sbuf_tensor(name, shape, F32))

            m.w1, m.w2 = esb("w1", [P, E * DFF]), esb("w2", [P, E * DFF])
            m.b1, m.b2 = esb("b1", [P, E * FC]), esb("b2", [P, E * D])
            m.x2_t = esb("x2_t_0", [P, 2, SEQ])
            m.b2_all, m.experts_now = m.b2, m.experts_in
            m.expert_loads = [(m.b1[:, :], m.b1_d), (m.b2[:, :], m.b2_d.partition_broadcast(P))]
            for e in range(0, E, 4):
                for dest, src in ((m.w1, m.w1_d), (m.w2, m.w2_d)):
                    m.expert_loads.append((dest[:, e * DFF:(e + 4) * DFF], src[:, e * DFF:(e + 4) * DFF]))
            embed_phase(nc, m)
            attention_phase(nc, m, 0)
            moe_phase(nc, m, 0)
        m.e_w1, m.e_w2 = sb("e_w1", [P, E * 2 * I1]), sb("e_w2", [I1, E * D])
        m.e_b1, m.e_b2 = sb("e_b1", [P, E * 2 * I1]), sb("e_b2", [P, E * D])
        m.e_act = sb("e_act", [P, NE1, 5])
        m.s_w1, m.s_w2, m.s_b1 = sb("s_w1", [P, 2 * I1]), sb("s_w2", [I1 + 1, D]), sb("s_b1", [I1, 2])
        m.x2_t = sb("x2_t_1", [P, BATCH, SEQ])
        m.b2_all, m.experts_now = m.e_b2, m.experts2_in
        m.expert_loads = [
            (m.e_w1[:, :].rearrange("p (e f) -> p e f", e=E), m.e_w1_d.rearrange("e d f -> d e f")),
            (m.e_w2[:, :].rearrange("p (e d) -> p e d", e=E), m.e_w2_d.rearrange("e i d -> i e d")),
            (m.e_b1[:, :], m.e_b1_d.partition_broadcast(P)),
            (m.e_b2[:, :], m.e_b2_d.partition_broadcast(P)),
            (m.e_act[:, 0:E, :].rearrange("p e c -> p (e c)"), m.e_act_d.partition_broadcast(P)),
            (m.e_act[:, E, :], m.s_act_d.partition_broadcast(P)),
            (m.s_w1[:, :], m.s_w1_d),
            (m.s_w2[0:I1, :], m.s_w2_d),
            (m.s_w2[I1:I1 + 1, :], m.s_b2_d.unsqueeze(0)),
            (m.s_b1[:, :], m.s_b1_d.rearrange("(i c) -> i c", c=2)),
        ]
        attention_phase(nc, m, 1)
        moe_phase(nc, m, 1)


def constants():
    p = np.arange(P)
    f = np.zeros((P, FC_END), np.float32)
    f[:, FC_IDENT:FC_IDENT + P] = np.eye(P)
    f[:, FC_RANK:FC_RANK + E] = E - np.arange(E)
    f[:, FC_J128:FC_J128 + NT] = P * np.arange(NT)
    f[:, FC_IOTA:FC_IOTA + P] = p
    f[:, FC_A128:FC_A128 + TILES] = P * np.arange(TILES)
    f[:, FC_TILE:FC_TILE + TILES] = np.arange(TILES)
    f[:, FC_TRASH:FC_TRASH + TILES] = PAIRS + P * np.arange(TILES)[None] + p[:, None]
    f[:, FC_KT:FC_KT + 2 * NT] = np.arange(2 * NT)
    f[:, FC_PART] = p
    f[:, FC_POW:FC_POW + TPB] = -0.5
    b = np.zeros((P, BC_END, P), np.float32)
    past = p[:, None] - p[None]
    b[:, BC_IDENT] = np.eye(P)
    b[:, BC_CAUSAL_Q] = np.where(past < 0, MASKED, 0.0)
    b[:, BC_CAUSAL_K] = b[:, BC_CAUSAL_Q].T
    b[:, BC_PAST_Q] = np.maximum(past, 0)
    b[:, BC_PAST_K] = b[:, BC_PAST_Q].T
    b[:, BC_TRI] = past < 0
    b[:, BC_ONES] = 1.0
    t = np.arange(SEQ)
    high, low = t // 256 * 256, t % 256
    one = np.ones(SEQ)
    q_rows = np.stack([0 * one, 0 * one, 0 * one, high, low, one, one])
    k_rows = np.stack([one, one, one, one, one, -high, -low])
    bf = np.dtype("bfloat16")
    return {"fconst_d": f, "bconst_d": b.astype(bf), "q_rows_d": q_rows.astype(bf), "k_rows_d": k_rows.astype(bf)}


def padded_out(w, bias):
    w = w.T.reshape(NG, GH, HD, D)
    out = np.zeros((NG, GH, 2 * HD, D), w.dtype)
    out[:, :, :HD] = w
    out[0, 0, HD] = bias
    return out.reshape(NG, GH * 2 * HD, D)


def layout(a):
    c = np.ascontiguousarray
    return {
        "x": a["x"],
        "table": a["L0_tok_table"],
        "w_qkv_d": c(np.stack([a["L0_attn_w_qkv"].T, a["L1_attn_w_qkv"].T])),
        "w_o_d": c(np.stack([padded_out(a["L0_attn_w_proj"], a["L0_attn_b_proj"]),
                             padded_out(a["L1_attn_w_out"], a["L1_attn_b_out"])])),
        "router_w_d": c(np.stack([a["L0_ffn_router_w"].T, a["L1_ffn_gate_w"]], axis=1)),
        "router_b_d": c(np.stack([a["L0_ffn_router_b"], a["L1_ffn_gate_b"]])),
        "w1_d": c(a["L0_ffn_w1"].transpose(2, 0, 1).reshape(D, E * DFF)),
        "w2_d": c(a["L0_ffn_w2"].reshape(E, D, FC, P).transpose(3, 0, 2, 1).reshape(P, E * FC * D)),
        "b1_d": c(a["L0_ffn_b1"].reshape(E, FC, P).transpose(2, 0, 1).reshape(P, E * FC)),
        "b2_d": c(a["L0_ffn_b2"].reshape(E * D)),
        "e_w1_d": a["L1_ffn_expert_w1"], "e_b1_d": c(a["L1_ffn_expert_b1"].reshape(-1)),
        "e_w2_d": a["L1_ffn_expert_w2"], "e_b2_d": c(a["L1_ffn_expert_b2"].reshape(-1)),
        "e_act_d": c(a["L1_ffn_expert_act"].reshape(-1)),
        "s_w1_d": a["L1_ffn_shared_w1"], "s_b1_d": a["L1_ffn_shared_b1"],
        "s_w2_d": a["L1_ffn_shared_w2"], "s_b2_d": a["L1_ffn_shared_b2"], "s_act_d": a["L1_ffn_shared_act"],
    }


def kernel(**inputs):
    import concourse.bacc as bacc
    from concourse.bass_utils import run_bass_kernel_spmd

    nc = bacc.Bacc("TRN2", target_bir_lowering=False, num_devices=1)
    data = layout({name: np.asarray(a) for name, a in inputs.items()})
    data.update(constants())
    arrays, io = {}, {}
    for name, a in data.items():
        arrays[f"in_{name}"] = a
        io[name] = nc.dram_tensor(f"in_{name}", list(a.shape), mybir.dt.from_np(a.dtype), kind="ExternalInput").ap()
    io["out"] = nc.dram_tensor("out_0_dram", [BATCH, SEQ, D], F32, kind="ExternalOutput").ap()
    program(nc, io)
    r = run_bass_kernel_spmd(nc, [arrays], core_ids=[0])
    return r.results[0]["out_0_dram"]
```

```python
from contextlib import ExitStack
import math

import numpy as np

import concourse.bass as bass
from concourse import mybir

F32 = mybir.dt.float32
BF16 = mybir.dt.bfloat16
I32 = mybir.dt.int32
ALU = mybir.AluOpType
ACT = mybir.ActivationFunctionType
AX = mybir.AxisListType
ENGINE = mybir.EngineType

P = 128
D = 128
BATCH, SEQ = 4, 512
TPB = SEQ // P
NT = BATCH * TPB
TOK = BATCH * SEQ
H, HD = 8, 16
GH = 4
NG = H // GH
E = 16
DFF = 512
FC = DFF // P
I1 = 96
KMER, VOCAB = 6, 5
EPS = 1e-5
UNITS = H * TPB
TILES = 47
TILES_USUAL = 42
RING = 8
HOT_PARTS = 16
SHARED_FIRST, SHARED_EVERY = 3, 8
PAIRS = 2 * TOK
SLOTS = TILES * P
DECAY = -math.log(0.9)
MASKED = -1.0e30
PACK_LOADS = (2 * 6 + 1,) + (2 * 3 + 1,) * (BATCH - 1)
LAG = 25
AT_PAIRS, AT_STATS, AT_NORM, AT_X = (-41, -39), -35, -32, -28
AT_PROJECT, AT_SPLIT, AT_PACK = -25, -23, -13
AT_MAX = (18, 34)
AT_OUTPUT, AT_TURN, AT_BACK = (LAG + 18, LAG + 34), (LAG + 24, LAG + 36), (LAG + 27, LAG + 39)
AT_Y, AT_NORM2, AT_X2, AT_LOGITS = LAG + 42, LAG + 48, LAG + 54, LAG + 57
AT_STATS2 = LAG + 45
TIME_END = (BATCH - 1) * UNITS + LAG + 60
PAR_ALPHA, PAR_SCALE, PAR_SHIFT, PAR_HIGH, PAR_LOW, N_PAR = 0, 1, 2, 3, 5, 7

BLOCKS_Q = (0, 0, 0, 1, 1, 2)
BLOCKS_K = (0, 1, 2, 0, 1, 0)
R_DOT = len(BLOCKS_Q) * HD
R_MAX = R_DOT + 3
R_ALL = R_MAX + 4

FC_IDENT, FC_RANK, FC_J128 = 0, 128, 144
FC_A128, FC_TILE, FC_TRASH = 160, 208, 256
FC_KT, FC_PART, FC_PART1, FC_POW, FC_ROW0, FC_END = 304, 336, 337, 338, 342, 470
BC_IDENT, BC_CAUSAL_Q, BC_CAUSAL_K, BC_PAST_Q, BC_PAST_K, BC_TRI, BC_ONES, BC_IOTA, BC_END = range(9)


class Memory:
    pass


def clear_semaphores(nc, sems):
    for s in sems:
        nc.gpsimd.sem_clear(s)


def embed_phase(nc, m):
    with ExitStack() as ctx:
        ids = ctx.enter_context(nc.sbuf_tensor("ids", [BATCH, SEQ + KMER - 1], I32))
        idx = ctx.enter_context(nc.sbuf_tensor("idx", [BATCH, KMER, SEQ], F32))
        sems = []

        def sem(name):
            sems.append(ctx.enter_context(nc.semaphore(name)))
            return sems[-1]

        consts_in, ids_in = sem("e_consts_in"), sem("e_ids_in")
        ids_zero, horner = sem("e_ids_zero"), sem("e_horner")
        idx_turned = sem("e_idx_turned")
        turned = m.bank[0]
        ctx.callback(clear_semaphores, nc, sems)
        block = ctx.enter_context(nc.Block())

        @block.sync
        def _(sp):
            sp.wait_ge(ids_zero, 1)
            sp.dma_start(ids[:, 2:2 + SEQ], m.x).then_inc(ids_in, 16)
            sp.dma_start(m.fconst[:, :], m.fconst_d).then_inc(consts_in, 16)
            sp.dma_start(m.bconst[:, :, :], m.bconst_d).then_inc(m.bconst_in, 16)
            for layer in range(2):
                for g in range(NG):
                    sp.dma_start(m.w_o[:, layer, g, :], m.w_o_d[layer][g]).then_inc(m.attn_w_in, 16)
                sp.dma_start(m.w_qkv[:, layer, :], m.w_qkv_d[layer]).then_inc(m.attn_w_in, 16)
            sp.dma_start(m.router_w[:, :, :], m.router_w_d).then_inc(m.attn_w_in, 16)
            for layer in range(2):
                sp.dma_start(m.router_b[:, layer, :],
                             m.router_b_d[layer].partition_broadcast(P)).then_inc(m.attn_w_in, 16)

        @block.vector
        def _(dve):
            nc.vector.memset(ids[:, :], 0).then_inc(ids_zero, 1)
            dve.wait_ge(ids_in, 16)
            nc.vector.scalar_tensor_tensor(idx[:, 1, :], ids[:, 0:SEQ], float(VOCAB), ids[:, 1:1 + SEQ],
                                           ALU.mult, ALU.add).then_inc(horner, 1)
            for j in range(2, KMER):
                dve.wait_ge(horner, j - 1)
                nc.vector.scalar_tensor_tensor(idx[:, j, :], idx[:, j - 1, :], float(VOCAB), ids[:, j:j + SEQ],
                                               ALU.mult, ALU.add).then_inc(horner, 1)
            dve.wait_ge(idx_turned, 1)
            nc.vector.tensor_copy(m.idx_col[:, :, :], turned[:, 0:NT].rearrange("p (c b) -> p b c", b=BATCH))

        @block.tensor
        def _(pe):
            pe.wait_ge(consts_in, 16)
            pe.wait_ge(horner, KMER - 1)
            for c in range(TPB):
                last = nc.tensor.transpose(turned[:, c * BATCH:(c + 1) * BATCH],
                                           idx[:, KMER - 1, c * P:(c + 1) * P],
                                           m.fconst[0:BATCH, FC_IDENT:FC_IDENT + BATCH])
            last.then_inc(idx_turned, 1)


def layer_norm_stats(nc, link, h, stats, moments):
    for t in range(TPB):
        last = nc.vector.bn_stats(stats[:, t, :], h[:, t, :])
    link(last)
    for t in range(TPB):
        last = nc.vector.bn_aggr(moments[:, t, :], stats[:, t, :])
    return last


def inverse_std(nc, pool, m, moments, var_eps, inv_std, var_eps_ready, b):
    nc.gpsimd.tensor_scalar(var_eps[:, :], moments[:, :, 1], EPS, None, ALU.add).then_inc(var_eps_ready, 1)
    pool.wait_ge(var_eps_ready, b + 1)
    return nc.gpsimd.tensor_tensor(inv_std[:, :], var_eps[:, :], m.fconst[:, FC_POW:FC_POW + TPB], ALU.pow)


def layer_norm_apply(engine, h, moments, inv_std, out):
    for t in range(TPB):
        last = engine.tensor_scalar(out[:, t, :], h[:, t, :], moments[:, t, 0:1], inv_std[:, t:t + 1],
                                       ALU.subtract, ALU.mult)
    return last


def due(time, at):
    b, off = divmod(time - at, UNITS)
    return [b] if off == 0 and 0 <= b < BATCH else []


def attention_phase(nc, m, layer):
    causal = layer == 0
    q_scale = 1.0 if causal else HD ** -0.5 / DECAY
    exp_scale = HD ** -0.5 if causal else DECAY
    diag_q, diag_k = (BC_CAUSAL_Q, BC_CAUSAL_K) if causal else (BC_PAST_Q, BC_PAST_K)

    uses_a, uses_b, uses_c = [], [], []
    for time in range(AT_X, TIME_END):
        for uses, kind, at in ((uses_a, ("x",), AT_X), (uses_a, ("v",), AT_PROJECT), (uses_b, ("q",), AT_PROJECT),
                               (uses_c, ("k",), AT_PROJECT), (uses_a, ("max", 0), AT_MAX[0]),
                               (uses_a, ("max", 1), AT_MAX[1]), (uses_b, ("turn", 0), AT_TURN[0]),
                               (uses_b, ("back", 0), AT_BACK[0]), (uses_b, ("turn", 1), AT_TURN[1]),
                               (uses_b, ("back", 1), AT_BACK[1]), (uses_c, ("y",), AT_Y), (uses_a, ("x2",), AT_X2),
                               (uses_c, ("logits",), AT_LOGITS)):
            for b in due(time, at):
                uses.append((kind[0], b) + kind[1:])
    nth_a = {key: n for n, key in enumerate(uses_a)}
    nth_b = {key: n for n, key in enumerate(uses_b)}
    nth_c = {key: n for n, key in enumerate(uses_c)}

    with ExitStack() as ctx:
        def sb(name, shape, dt=F32):
            return ctx.enter_context(nc.sbuf_tensor(f"{name}_{layer}", shape, dt))

        sems = []

        def sem(name):
            sems.append(ctx.enter_context(nc.semaphore(f"a{layer}_{name}")))
            return sems[-1]

        stats, moments = sb("stats", [P, TPB, 6]), sb("moments", [P, TPB, 2])
        var_eps, inv_std = sb("var_eps", [P, TPB]), sb("inv_std", [P, TPB])
        xn, x_t = sb("xn", [P, TPB, D]), sb("x_t", [P, SEQ])
        q_pack, k_pack = sb("q_pack", [P, 3, H, SEQ], BF16), sb("k_pack", [P, 3, H, SEQ], BF16)
        v_ext = sb("v_ext", [P, 3, TPB, H, 2 * HD])
        parts = {"q": sb("q_parts", [P, 3, SEQ], BF16), "k": sb("k_parts", [P, 3, SEQ], BF16)}
        rest = {"q": sb("q_rest", [P, SEQ]), "k": sb("k_rest", [P, SEQ])}
        neg_max, max_rest = sb("neg_max", [P, NG, UNITS // NG]), sb("max_rest", [P, NG, UNITS // NG])
        max_parts = sb("max_parts", [P, NG, 3, UNITS // NG], BF16)
        max_rows = sb("max_rows", [3 * UNITS // NG, NG, P], BF16)
        probs = sb("probs", [P, 8, SEQ])
        o_tok, inv_sums = sb("o_tok", [P, TPB * GH, 2 * HD]), sb("inv_sums", [P, TPB * GH])
        stats2, moments2 = sb("stats2", [P, TPB, 6]), sb("moments2", [P, TPB, 2])
        var_eps2, inv_std2 = sb("var_eps2", [P, TPB]), sb("inv_std2", [P, TPB])
        xn2 = sb("xn2", [P, TPB, D])
        o_raw, o_norm = sb("o_raw", [P, NG, SEQ]), sb("o_norm", [P, NG, SEQ])

        bank_q = m.bank[0:2]
        bank_k = m.bank[2:4]
        bank_o = m.bank[4]
        bank_a, bank_b, bank_c = m.bank[5:8]

        if layer:
            y_sel, y_in = sb("y_sel", [P, 2, TPB, D]), sem("y_in")
            pairs_added = sem("pairs_added")
        dve_chain = sem("dve_chain")
        pack_rows_in, v_ext_zero = sem("pack_rows_in"), sem("v_ext_zero")
        var_eps_ready = sem("var_eps_ready")
        moments_ready, inv_std_ready, xn_ready = sem("moments_ready"), sem("inv_std_ready"), sem("xn_ready")
        a_filled, b_filled, c_filled = sem("a_filled"), sem("b_filled"), sem("c_filled")
        a_read, b_read, c_read = sem("a_read"), sem("b_read"), sem("c_read")
        high_ready, mid_ready, low_ready = sem("high_ready"), sem("mid_ready"), sem("low_ready")
        parts_out = sem("parts_out")
        pack_in = [sem("pack_in_even"), sem("pack_in_odd")]
        q_scores, q_scores_read = sem("q_scores"), sem("q_scores_read")
        max_parts_ready, max_in = sem("max_parts_ready"), [sem("max_in_0"), sem("max_in_1")]
        k_scores, probs_ready, pv_done = sem("k_scores"), sem("probs_ready"), sem("pv_done")
        o_read, inverted = sem("o_read"), sem("inverted")
        moments2_ready, var_eps2_ready, inv_std2_ready = sem("moments2_ready"), sem("var_eps2_ready"), sem("inv_std2_ready")
        xn2_ready, rows_out = sem("xn2_ready"), m.rows_out[layer]
        ctx.callback(clear_semaphores, nc, sems)
        block = ctx.enter_context(nc.Block())

        @block.sync
        def _(sp):
            def clear_max(b):
                sp.dma_start(q_pack[R_DOT:R_MAX, b % 3, :, :],
                             m.q_rows_d[0:3].unsqueeze(1).to_broadcast([3, H, SEQ])).then_inc(pack_in[b % 2], 16)

            def pack_first():
                sp.wait_ge(pack_rows_in, 16 * 6)
                clear_max(0)
                for part, ready in enumerate((high_ready, mid_ready, low_ready)):
                    for n, (name, dest, blocks) in enumerate((("q", q_pack, BLOCKS_Q), ("k", k_pack, BLOCKS_K))):
                        sp.wait_ge(ready, n + 1)
                        for i in range(len(blocks)):
                            if blocks[i] == part:
                                sp.dma_start(dest[i * HD:(i + 1) * HD, 0, :, :], parts[name][:, part, :]
                                             ).then_inc(pack_in[0], 16)

            def parts_to_dram(b):
                for n, name in enumerate("qk"):
                    sp.wait_ge(high_ready, 2 * b + n + 1)
                    sp.wait_ge(mid_ready, 2 * b + n + 1)
                    sp.wait_ge(low_ready, 2 * b + n + 1)
                    sp.dma_start(m.parts_d[b, n].rearrange("s d h t -> (d h) s t"),
                                 parts[name][:, :, :]).then_inc(parts_out, 16)

            def pack(b):
                if b >= 3:
                    sp.wait_ge(pv_done, (b - 2) * UNITS // GH)
                clear_max(b)
                sp.wait_ge(parts_out, 32 * b)
                row = 0
                for part, times in enumerate((3, 2, 1)):
                    for dest, src in ((q_pack, m.parts_d[b, 0, part:part + 1].to_broadcast([times, HD, H, SEQ])),
                                      (k_pack, m.parts_d[b, 1, 0:times])):
                        sp.dma_start(dest[row:row + times * HD, b % 3, :, :], src.rearrange("s d h t -> s d (h t)")
                                     ).then_inc(pack_in[b % 2], 16)
                    row += times * HD

            def max_to_rows(b, g):
                sp.wait_ge(a_read, nth_a["max", b, g] + 1)
                sp.wait_ge(q_scores, b * UNITS + (g + 1) * UNITS // NG)
                for s in range(3):
                    sp.dma_start(q_pack[R_DOT + s:R_DOT + s + 1, b % 3, g * GH:(g + 1) * GH, :],
                                 max_rows[s * 16:(s + 1) * 16, g, :]).then_inc(max_in[g], 16)

            if layer:
                load_pairs(sp, m, 0, y_sel, y_in)
            for buf in range(3):
                for pack_buf, rows in ((k_pack, m.k_rows_d), (q_pack, m.q_rows_d)):
                    sp.dma_start(pack_buf[R_DOT:R_ALL, buf, :, :],
                                 rows.unsqueeze(1).to_broadcast([R_ALL - R_DOT, H, SEQ])
                                 ).then_inc(pack_rows_in, 16)
            for time in range(AT_X, TIME_END):
                if layer:
                    for b in due(time, AT_PAIRS[0] - 16):
                        if b:
                            sp.wait_ge(pairs_added, 2 * b)
                            load_pairs(sp, m, b, y_sel, y_in)
                for b in due(time, AT_MAX[1] + 1):
                    max_to_rows(b, 1)
                for b in due(time, AT_NORM2 + 1):
                    sp.wait_ge(xn2_ready, b + 1)
                    sp.dma_start(m.x_rows_d[b * SEQ:(b + 1) * SEQ, :].rearrange("(t p) d -> p t d", p=P),
                                 xn2[:, :, :]).then_inc(rows_out, 16)
                if time == AT_SPLIT:
                    pack_first()
                for b in due(time, AT_SPLIT + 2):
                    if b:
                        parts_to_dram(b)
                for b in due(time, AT_MAX[0] + 1):
                    max_to_rows(b, 0)
                for b in due(time, AT_PACK):
                    if b:
                        pack(b)
                for b in due(time, AT_PACK + UNITS):
                    for dest, src in m.expert_loads[b::BATCH]:
                        sp.dma_start(dest, src).then_inc(m.experts_now, 16)
        @block.gpsimd
        def _(pool):
            def embed(b, first=0, end=TPB):
                for t in range(first, end):
                    pool.indirect_dma_start(m.h[:, b * TPB + t, :], None, m.table,
                                            bass.IndirectOffsetOnAxis(ap=m.idx_col[:, b, t:t + 1], axis=0)
                                            ).then_inc(m.rows_in[b], 16)

            def norm(b):
                pool.wait_ge(inv_std_ready, b + 1)
                if b:
                    pool.wait_ge(a_filled, nth_a["x", b - 1] + 1)
                layer_norm_apply(nc.gpsimd, m.h[:, b * TPB:(b + 1) * TPB, :], moments, inv_std, xn).then_inc(xn_ready, 1)

            def norm_2(b):
                pool.wait_ge(inv_std2_ready, b + 1)
                if b:
                    pool.wait_ge(a_filled, nth_a["x2", b - 1] + 1)
                    pool.wait_ge(rows_out, 16 * b)
                layer_norm_apply(nc.gpsimd, m.h[:, b * TPB:(b + 1) * TPB, :], moments2, inv_std2, xn2).then_inc(xn2_ready, 1)

            def low_parts(b):
                for n, name in enumerate("qk"):
                    pool.wait_ge(mid_ready, 2 * b + n + 1)
                    nc.gpsimd.tensor_tensor(parts[name][:, 2, :], rest[name][:, :], parts[name][:, 1, :],
                                            ALU.subtract).then_inc(low_ready, 1)

            if layer == 0:
                embed(0)
                embed(1, 0, TPB // 2)
            for time in range(AT_STATS, TIME_END):
                for b in due(time, AT_STATS):
                    pool.wait_ge(moments_ready, b + 1)
                    inverse_std(nc, pool, m, moments, var_eps, inv_std, var_eps_ready, b).then_inc(inv_std_ready, 1)
                    if layer == 0 and b == 0:
                        embed(1, TPB // 2)
                        for later in range(2, BATCH):
                            embed(later)
                    if b:
                        norm(b)
                for b in due(time, AT_NORM2):
                    pool.wait_ge(moments2_ready, b + 1)
                    inverse_std(nc, pool, m, moments2, var_eps2, inv_std2, var_eps2_ready, b).then_inc(inv_std2_ready, 1)
                    if b < BATCH - 1:
                        norm_2(b)
                for b in due(time, AT_SPLIT):
                    low_parts(b)

        @block.scalar
        def _(act):
            def take_x(b):
                act.wait_ge(a_filled, nth_a["x", b] + 1)
                if b:
                    act.wait_ge(c_filled, nth_c["k", b - 1] + 1)
                    act.wait_ge(a_filled, nth_a["v", b - 1] + 1)
                nc.scalar.activation(x_t[:, :], bank_a[:, :], ACT.Copy).then_inc(a_read, 1)

            def take_projections(b):
                for n, (name, bank, filled, nth) in enumerate((("q", bank_b, b_filled, nth_b),
                                                               ("k", bank_c, c_filled, nth_c))):
                    act.wait_ge(filled, nth[name, b] + 1)
                    if b:
                        if b == 1:
                            act.wait_ge(pack_in[0], 16 * PACK_LOADS[0])
                        else:
                            act.wait_ge(parts_out, 32 * (b - 1))
                    nc.scalar.activation(parts[name][:, 0, :], bank[:, :], ACT.Copy,
                                         scale=q_scale if name == "q" else 1.0).then_inc(high_ready, 1)
                for n, (name, read, nth) in enumerate((("q", b_read, nth_b), ("k", c_read, nth_c))):
                    act.wait_ge(read, nth[name, b] + 1)
                    nc.scalar.activation(parts[name][:, 1, :], rest[name][:, :], ACT.Copy).then_inc(mid_ready, 1)
                act.wait_ge(a_filled, nth_a["v", b] + 1)
                if b == 0:
                    act.wait_ge(v_ext_zero, 6)
                if b >= 3:
                    act.wait_ge(pv_done, (b - 2) * UNITS // GH)
                nc.scalar.activation(v_ext[:, b % 3, :, :, 0:HD],
                                     bank_a[:, :].rearrange("p (t h d) -> p t h d", t=TPB, h=H),
                                     ACT.Copy).then_inc(a_read, 1)

            def take_max_rows(b, g):
                act.wait_ge(a_filled, nth_a["max", b, g] + 1)
                if b:
                    act.wait_ge(max_in[g], 48 * b)
                nc.scalar.activation(max_rows[:, g, :], bank_a[0:48, 0:P // 2].bitcast(BF16),
                                     ACT.Copy).then_inc(a_read, 1)

            def exponential(b, u):
                n = b * UNITS + u
                ki = (u // GH) % TPB
                first = ki * P if causal else 0
                act.wait_ge(k_scores, n + 1)
                if n >= 8:
                    act.wait_ge(pv_done, (n - 8) // GH + 1)
                nc.scalar.activation(probs[:, n % 8, first:], bank_k[n % 2][:, first:], ACT.Exp,
                                     scale=exp_scale).then_inc(probs_ready, 1)

            def take_output(b, g):
                act.wait_ge(pv_done, (b * NG + g + 1) * TPB)
                if b:
                    act.wait_ge(b_filled, nth_b["turn", b - 1, g] + 1)
                nc.scalar.activation(o_raw[:, g, :], bank_o[:, :], ACT.Copy).then_inc(o_read, 1)

            def take_normalized(b, g):
                act.wait_ge(b_filled, nth_b["back", b, g] + 1)
                if b:
                    act.wait_ge(c_filled, nth_c["y", b - 1] + 1)
                nc.scalar.activation(o_norm[:, g, :], bank_b[:, :], ACT.Copy).then_inc(b_read, 1)

            def take_x2(b):
                act.wait_ge(a_filled, nth_a["x2", b] + 1)
                if layer == 0 and b >= 2:
                    act.wait_ge(c_filled, nth_c["logits", b - 2] + 1)
                nc.scalar.activation(m.x2_t[:, b % m.x2_t.shape[1], :], bank_a[:, :], ACT.Copy).then_inc(a_read, 1)

            for time in range(AT_X, TIME_END):
                for b in due(time, AT_MAX[1] + 1):
                    take_max_rows(b, 1)
                for b in due(time, AT_X + 1):
                    take_x(b)
                for b in due(time, AT_SPLIT):
                    take_projections(b)
                for b in due(time, AT_MAX[0] + 1):
                    take_max_rows(b, 0)
                for g in range(NG):
                    for b in due(time, AT_OUTPUT[g]):
                        take_output(b, g)
                    for b in due(time, AT_BACK[g] + 1):
                        take_normalized(b, g)
                for b in due(time, AT_X2 + 1):
                    take_x2(b)
                if 0 <= time - LAG < BATCH * UNITS:
                    exponential(*divmod(time - LAG, UNITS))

        @block.vector
        def _(dve):
            chain = [0]

            def link(ins):
                chain[0] += 1
                ins.then_inc(dve_chain, 1)
                dve.wait_ge(dve_chain, chain[0])

            def norm_stats(b):
                if layer:
                    dve.wait_ge(pairs_added, NG * (b + 1))
                else:
                    dve.wait_ge(m.rows_in[b], 16 * TPB)
                if b:
                    dve.wait_ge(xn_ready, b)
                layer_norm_stats(nc, link, m.h[:, b * TPB:(b + 1) * TPB, :], stats, moments).then_inc(moments_ready, 1)

            def norm(b):
                dve.wait_ge(inv_std_ready, b + 1)
                if b:
                    dve.wait_ge(a_filled, nth_a["x", b - 1] + 1)
                layer_norm_apply(nc.vector, m.h[:, b * TPB:(b + 1) * TPB, :], moments, inv_std, xn).then_inc(xn_ready, 1)

            def norm_2(b):
                dve.wait_ge(inv_std2_ready, b + 1)
                if b:
                    dve.wait_ge(a_filled, nth_a["x2", b - 1] + 1)
                    dve.wait_ge(rows_out, 16 * b)
                layer_norm_apply(nc.vector, m.h[:, b * TPB:(b + 1) * TPB, :], moments2, inv_std2, xn2).then_inc(xn2_ready, 1)

            def split(b):
                for n, (name, bank, read) in enumerate((("q", bank_b, b_read), ("k", bank_c, c_read))):
                    dve.wait_ge(high_ready, 2 * b + n + 1)
                    if b:
                        dve.wait_ge(low_ready, 2 * (b - 1) + n + 1)
                    nc.vector.scalar_tensor_tensor(rest[name][:, :], bank[:, :], q_scale if name == "q" else 1.0,
                                                   parts[name][:, 0, :], ALU.mult, ALU.subtract
                                                   ).then_inc(read, 1)

            def row_max(b, u):
                n = b * UNITS + u
                width = (u % TPB + 1) * P if causal else SEQ
                g, col = u // (UNITS // NG), u % (UNITS // NG)
                dve.wait_ge(q_scores, n + 1)
                if u == 0 and b:
                    dve.wait_ge(max_parts_ready, 2 * b)
                nc.vector.tensor_reduce(neg_max[:, g, col:col + 1], bank_q[n % 2][:, 0:width], AX.X, ALU.max,
                                        negate=True).then_inc(q_scores_read, 1)

            def split_max(b, g):
                dve.wait_ge(q_scores_read, b * UNITS + (g + 1) * UNITS // NG)
                if b:
                    dve.wait_ge(a_filled, nth_a["max", b - 1, g] + 1)
                link(nc.vector.tensor_copy(max_parts[:, g, 0, :], neg_max[:, g, :]))
                link(nc.vector.tensor_tensor(max_rest[:, g, :], neg_max[:, g, :], max_parts[:, g, 0, :], ALU.subtract))
                link(nc.vector.tensor_copy(max_parts[:, g, 1, :], max_rest[:, g, :]))
                nc.vector.tensor_tensor(max_parts[:, g, 2, :], max_rest[:, g, :], max_parts[:, g, 1, :],
                                        ALU.subtract).then_inc(max_parts_ready, 1)

            def normalize(b, g):
                dve.wait_ge(b_filled, nth_b["turn", b, g] + 1)
                if b + g:
                    before = (b, 0) if g else (b - 1, 1)
                    dve.wait_ge(b_filled, nth_b[("back",) + before] + 1)
                turned = bank_b[:, :].rearrange("p (q d) -> p q d", d=2 * HD)
                nc.vector.reciprocal(inv_sums[:, :].unsqueeze(2), turned[:, :, HD:HD + 1]).then_inc(inverted, 1)
                dve.wait_ge(inverted, b * NG + g + 1)
                nc.vector.tensor_tensor(o_tok[:, :, :], turned,
                                        inv_sums[:, :].unsqueeze(2).to_broadcast([P, TPB * GH, 2 * HD]), ALU.mult
                                        ).then_inc(b_read, 1)

            def add_output(b):
                dve.wait_ge(c_filled, nth_c["y", b] + 1)
                rows = m.h[:, b * TPB:(b + 1) * TPB, :]
                nc.vector.tensor_tensor(rows, rows, bank_c[:, :].rearrange("p (t d) -> p t d", t=TPB),
                                        ALU.add).then_inc(c_read, 1)

            def stats_2(b):
                dve.wait_ge(c_read, nth_c["y", b] + 1)
                if b:
                    dve.wait_ge(xn2_ready, b)
                layer_norm_stats(nc, link, m.h[:, b * TPB:(b + 1) * TPB, :], stats2, moments2).then_inc(moments2_ready, 1)

            def take_logits(b):
                dve.wait_ge(c_filled, nth_c["logits", b] + 1)
                nc.vector.tensor_tensor(m.logits[:, b * TPB:(b + 1) * TPB, :],
                                        bank_c[:, 0:TPB * E].rearrange("p (t e) -> p t e", e=E),
                                        m.router_b[:, layer, :].unsqueeze(1).to_broadcast([P, TPB, E]), ALU.add
                                        ).then_inc(c_read, 1)

            def fill_v_ext():
                for buf in range(3):
                    nc.vector.memset(v_ext[:, buf, :, :, HD:2 * HD], 0.0).then_inc(v_ext_zero, 1)
                for buf in range(3):
                    dve.wait_ge(v_ext_zero, buf + 1)
                    nc.vector.memset(v_ext[:, buf, :, :, HD:HD + 1], 1.0).then_inc(v_ext_zero, 1)

            for time in range(AT_PAIRS[0], TIME_END):
                for b in due(time, AT_MAX[1] - 2):
                    split_max(b, 1)
                for k in range(2 if layer else 0):
                    for b in due(time, AT_PAIRS[k]):
                        if k == 0:
                            dve.wait_ge(y_in, 32 * (b + 1))
                        else:
                            dve.wait_ge(pairs_added, 2 * b + 1)
                        add_pairs(nc, m, b, k, y_sel).then_inc(pairs_added, 1)
                for b in due(time, AT_STATS):
                    norm_stats(b)
                if time == AT_NORM:
                    norm(0)
                    fill_v_ext()
                for b in due(time, AT_Y + 2):
                    add_output(b)
                for b in due(time, AT_STATS2):
                    stats_2(b)
                if time == AT_NORM2 + (BATCH - 1) * UNITS:
                    norm_2(BATCH - 1)
                for b in due(time, AT_SPLIT):
                    split(b)
                for g in range(NG):
                    for b in due(time, AT_TURN[g] + 1):
                        normalize(b, g)
                for b in due(time, AT_LOGITS + 2):
                    take_logits(b)
                for b in due(time, AT_MAX[0] - 1):
                    split_max(b, 0)
                if 0 <= time < BATCH * UNITS:
                    row_max(*divmod(time, UNITS))

        @block.tensor
        def _(pe):
            ident = m.fconst[:, FC_IDENT:FC_IDENT + P]
            ident_bf = m.bconst[:, BC_IDENT, :]

            def free(read, nth, key):
                if nth[key]:
                    pe.wait_ge(read, nth[key])

            def turn_x(b):
                pe.wait_ge(xn_ready, b + 1)
                free(a_read, nth_a, ("x", b))
                for t in range(TPB):
                    last = nc.tensor.transpose(bank_a[:, t * P:(t + 1) * P], xn[:, t, :], ident)
                last.then_inc(a_filled, 1)

            def project(b):
                pe.wait_ge(a_read, nth_a["x", b] + 1)
                w = m.w_qkv[:, layer, :]
                free(b_read, nth_b, ("q", b))
                nc.tensor.matmul(bank_b[:, :], w[:, 0:D], x_t[:, :], start=True, stop=True).then_inc(b_filled, 1)
                free(c_read, nth_c, ("k", b))
                nc.tensor.matmul(bank_c[:, :], w[:, D:2 * D], x_t[:, :], start=True, stop=True).then_inc(c_filled, 1)
                for t in range(TPB):
                    last = nc.tensor.matmul(bank_a[:, t * P:(t + 1) * P], x_t[:, t * P:(t + 1) * P],
                                            w[:, 2 * D:3 * D], start=True, stop=True)
                last.then_inc(a_filled, 1)

            def score_q(b, u):
                n, h, qi = b * UNITS + u, u // TPB, u % TPB
                if u == 0:
                    pe.wait_ge(pack_in[b % 2], 16 * sum(PACK_LOADS[b % 2:b + 1:2]))
                if n >= 2:
                    pe.wait_ge(q_scores_read, n - 1)
                q = q_pack[:, b % 3, h, qi * P:(qi + 1) * P]
                k = k_pack[:, b % 3, h, :]
                out = bank_q[n % 2]
                lo = qi * P
                if causal:
                    nc.tensor.matmul(out[:, 0:lo + P], q[0:R_DOT], k[0:R_DOT, 0:lo + P], start=True, stop=False,
                                     skip_group_check=True)
                else:
                    if qi:
                        nc.tensor.matmul(out[:, 0:lo], q[0:R_ALL], k[0:R_ALL, 0:lo], start=True, stop=True,
                                         skip_group_check=True)
                    nc.tensor.matmul(out[:, lo:], q[0:R_DOT], k[0:R_DOT, lo:], start=True, stop=False,
                                     skip_group_check=True)
                nc.tensor.matmul(out[:, lo:lo + P], ident_bf, m.bconst[:, diag_q, :], start=False, stop=True,
                                 skip_group_check=True).then_inc(q_scores, 1)

            def turn_max(b, g):
                pe.wait_ge(max_parts_ready, b * NG + g + 1)
                free(a_read, nth_a, ("max", b, g))
                nc.tensor.transpose(bank_a[0:48, 0:P // 2].bitcast(BF16),
                                    max_parts[:, g, :, :].rearrange("p s c -> p (s c)"), ident_bf).then_inc(a_filled, 1)

            def score_k(b, u):
                n, h, ki = b * UNITS + u, (u // (GH * TPB)) * GH + u % GH, (u // GH) % TPB
                if u % (UNITS // NG) == 0:
                    pe.wait_ge(max_in[u // (UNITS // NG)], 48 * (b + 1))
                if n >= 2:
                    pe.wait_ge(probs_ready, n - 1)
                k = k_pack[:, b % 3, h, ki * P:(ki + 1) * P]
                q = q_pack[:, b % 3, h, :]
                out = bank_k[n % 2]
                lo = ki * P
                if causal:
                    nc.tensor.matmul(out[:, lo:], k[0:R_MAX], q[0:R_MAX, lo:], start=True, stop=False,
                                     skip_group_check=True)
                else:
                    if lo + P < SEQ:
                        nc.tensor.matmul(out[:, lo + P:], k[0:R_ALL], q[0:R_ALL, lo + P:], start=True, stop=True,
                                         skip_group_check=True)
                    nc.tensor.matmul(out[:, 0:lo + P], k[0:R_MAX], q[0:R_MAX, 0:lo + P], start=True, stop=False,
                                     skip_group_check=True)
                nc.tensor.matmul(out[:, lo:lo + P], ident_bf, m.bconst[:, diag_k, :], start=False, stop=True,
                                 skip_group_check=True).then_inc(k_scores, 1)

            def times_v(b, pv):
                g, ki = pv // TPB, pv % TPB
                n = b * UNITS + pv * GH
                first = ki * P if causal else 0
                pe.wait_ge(probs_ready, n + GH)
                if ki == 0 and b * NG + g:
                    pe.wait_ge(o_read, b * NG + g)
                for j in range(GH):
                    last = nc.tensor.matmul(bank_o[32 * j:32 * j + 32, first:], v_ext[:, b % 3, ki, g * GH + j, :],
                                            probs[:, (n + j) % 8, first:], start=(ki == 0), stop=(ki == TPB - 1),
                                            skip_group_check=True)
                last.then_inc(pv_done, 1)

            def turn_output(b, g):
                pe.wait_ge(o_read, b * NG + g + 1)
                free(b_read, nth_b, ("turn", b, g))
                for t in range(TPB):
                    last = nc.tensor.transpose(bank_b[:, t * P:(t + 1) * P], o_raw[:, g, t * P:(t + 1) * P], ident)
                last.then_inc(b_filled, 1)

            def turn_back(b, g):
                free(b_read, nth_b, ("back", b, g))
                for t in range(TPB):
                    last = nc.tensor.transpose(bank_b[:, t * P:(t + 1) * P],
                                               o_tok[:, t * GH:(t + 1) * GH, :].rearrange("p j d -> p (j d)"), ident)
                last.then_inc(b_filled, 1)

            def project_out(b):
                pe.wait_ge(b_read, nth_b["back", b, 1] + 1)
                free(c_read, nth_c, ("y", b))
                for t in range(TPB):
                    for g in range(NG):
                        last = nc.tensor.matmul(bank_c[:, t * P:(t + 1) * P], o_norm[:, g, t * P:(t + 1) * P],
                                                m.w_o[:, layer, g, :], start=(g == 0), stop=(g == NG - 1))
                last.then_inc(c_filled, 1)

            def turn_x2(b):
                pe.wait_ge(xn2_ready, b + 1)
                free(a_read, nth_a, ("x2", b))
                for t in range(TPB):
                    last = nc.tensor.transpose(bank_a[:, t * P:(t + 1) * P], xn2[:, t, :], ident)
                last.then_inc(a_filled, 1)

            def route(b):
                pe.wait_ge(a_read, nth_a["x2", b] + 1)
                free(c_read, nth_c, ("logits", b))
                for t in range(TPB):
                    last = nc.tensor.matmul(bank_c[:, t * E:(t + 1) * E],
                                            m.x2_t[:, b % m.x2_t.shape[1], t * P:(t + 1) * P],
                                            m.router_w[:, layer, :], start=True, stop=True)
                last.then_inc(c_filled, 1)

            if layer == 0:
                pe.wait_ge(m.attn_w_in, 16 * 9)
                pe.wait_ge(m.bconst_in, 16)
            for time in range(AT_X, TIME_END):
                for b in due(time, AT_MAX[1]):
                    turn_max(b, 1)
                for b in due(time, AT_X):
                    turn_x(b)
                for b in due(time, AT_PROJECT):
                    project(b)
                for b in due(time, AT_MAX[0]):
                    turn_max(b, 0)
                for g in range(NG):
                    for b in due(time, AT_TURN[g]):
                        turn_output(b, g)
                    for b in due(time, AT_BACK[g]):
                        turn_back(b, g)
                for b in due(time, AT_Y):
                    project_out(b)
                for b in due(time, AT_X2):
                    turn_x2(b)
                for b in due(time, AT_LOGITS):
                    route(b)
                if 0 <= time < BATCH * UNITS:
                    score_q(*divmod(time, UNITS))
                n = time - LAG
                if 0 <= n < BATCH * UNITS:
                    score_k(*divmod(n, UNITS))
                if n % GH == 1 and GH < n < (BATCH * UNITS + GH):
                    times_v(*divmod(n // GH - 1, UNITS // GH))


def expert_of(nc, engine, tile_expert, tile):
    return nc.values_load(tile_expert[0:1, tile:tile + 1], engines=[engine], min_val=0, max_val=E - 1,
                          skip_runtime_bounds_check_because="a minimum on the chip bounds it")


def tiles_used(nc, engine, used):
    return nc.values_load(used[0:1, 0:1], engines=[engine], min_val=0, max_val=TILES,
                          skip_runtime_bounds_check_because="it only decides a branch")


def load_pairs(sp, m, b, dest, signal):
    for k in range(2):
        sp.dma_start(dest[:, k, :, :], m.y_rows_d[k * TOK + b * SEQ:k * TOK + (b + 1) * SEQ, :].rearrange(
            "(t p) d -> p t d", p=P)).then_inc(signal, 16)


def add_pairs(nc, m, b, k, pairs):
    for t in range(TPB):
        n = b * TPB + t
        last = nc.vector.scalar_tensor_tensor(m.h[:, n, :], pairs[:, k, t, :], m.gate[:, k, n:n + 1],
                                              m.h[:, n, :], ALU.mult, ALU.add)
    return last


def moe_phase(nc, m, layer):
    first = layer == 0
    with ExitStack() as ctx:
        def sb(name, shape, dt=F32):
            return ctx.enter_context(nc.sbuf_tensor(f"{name}_m{layer}", shape, dt))

        sems = []

        def sem(name):
            sems.append(ctx.enter_context(nc.semaphore(f"m{layer}_{name}")))
            return sems[-1]

        logits, lower = m.logits, sb("lower", [P, NT, E])
        weighed, expd = sb("weighed", [P, NT, E]), sb("expd", [P, NT, E])
        chosen = sb("chosen", [P, 2, NT, E])
        top, rank = sb("top", [P, 2, NT]), sb("rank", [P, NT])
        gap, gap_exp, total = sb("gap", [P, NT]), sb("gap_exp", [P, NT]), sb("total", [P, NT])
        gate = m.gate
        marks = sb("marks", [P, NT + 2, E], BF16)
        ranks = sb("ranks", [P, NT, E])
        over = sb("over", [P, E, NT])
        n_tiles, zeros_e, ends, starts = sb("n_tiles", [P, E]), sb("zeros_e", [P, E]), sb("ends", [P, E]), sb("starts", [P, E])
        pos, pos_i, row_i = sb("pos", [P, 2 * NT]), sb("pos_i", [P, 2 * NT], I32), sb("row_i", [P, 2 * NT], I32)
        row, tile128 = sb("row", [P, 2 * NT]), sb("tile128", [P, 2 * NT])
        row_hot = sb("row_hot", [P, 2 * NT, P], BF16)
        hot, tile_hot = sb("hot", [P, 2 * NT, TILES], BF16), sb("tile_hot", [P, 2 * NT, 2, TILES], BF16)
        pair, wrap, pad = sb("pair", [P, TILES]), sb("wrap", [P, TILES]), sb("pad", [P, TILES])
        src_row, dst_row = sb("src_row", [P, TILES], I32), sb("dst_row", [P, TILES], I32)
        used = sb("used", [P, 1], I32)
        before, tile_expert = sb("before", [P, TILES, E]), sb("tile_expert", [P, TILES], I32)
        expert_f = sb("expert_f", [P, TILES])
        x_rows, y_rows = sb("x_rows", [P, RING, D]), sb("y_rows", [P, RING, D])
        xt = sb("xt", [P, 2, P])
        if not first:
            y_sel = sb("y_sel", [P, BATCH, 2, TPB, D])
        if first:
            w1_now, h_act = sb("w1_now", [P, 2, DFF]), sb("h_act", [P, 2, DFF])
        else:
            g_cl, u_cl, sig = [sb(n, [P, 2, I1]) for n in ("g_cl", "u_cl", "sig")]
            gu, te, te_t = sb("gu", [P, 2, I1]), sb("te", [P, 2, I1]), sb("te_t", [I1 + 1, 2, P])
            soft, ones_e, expert_hot = sb("soft", [P, 4, 2, 2]), sb("ones_e", [E, P]), sb("expert_hot", [E, TILES])
            e_par, par_spread, par = sb("e_par", [E, N_PAR]), sb("par_spread", [E, TILES, N_PAR]), sb("par", [P, TILES, N_PAR])
            s_pre, s_sig, s_te = sb("s_pre", [I1, 2, SEQ]), sb("s_sig", [I1, SEQ]), sb("s_te", [I1 + 1, SEQ])

        bank_rank, bank_pairs = m.bank[3], m.bank[2]
        bank_up, bank_down = m.bank[2:4], m.bank[6:8]
        bank_turn = m.bank[0:2] if first else [m.bank[0]] * 2
        bank_mid = m.bank[4]
        bank_shared, bank_par = [m.bank[1], m.bank[5]], m.bank[7]

        dve_chain = sem("dve_chain")
        weighed_ready, expd_ready = sem("weighed_ready"), sem("expd_ready")
        marks_ready, ranks_done = sem("marks_ready"), sem("ranks_done")
        pos_ready, row_hot_ready, tile_hot_ready = sem("pos_ready"), sem("row_hot_ready"), sem("tile_hot_ready")
        hot_ready, tiles_done = sem("hot_ready"), sem("tiles_done")
        pairs_done, order_ready = sem("pairs_done"), sem("order_ready")
        x_in, y_out = m.x_in[layer], m.y_out[layer]
        turned, xt_ready, up_done = sem("turned"), sem("xt_ready"), sem("up_done")
        pre_ready, mid_turned, act_ready = sem("pre_ready"), sem("mid_turned"), sem("act_ready")
        w1_ready = sem("w1_ready")
        down_done, y_ready = sem("down_done"), sem("y_ready")
        y_in, added, half_added = [sem(f"y_in_{b}") for b in range(BATCH)], sem("added"), sem("half_added")
        if not first:
            soft_in, soft_ready = sem("soft_in"), sem("soft_ready")
            s_up, s_biased, s_clipped, s_sig_ready = sem("s_up"), sem("s_biased"), sem("s_clipped"), sem("s_sig_ready")
            s_te_ready, s_down, s_added, s_sum = sem("s_te_ready"), sem("s_down"), sem("s_added"), sem("s_sum")
            sig_ready, par_spread_ready, par_filled, par_ready = [
                sem(n) for n in ("sig_ready", "par_spread_ready", "par_filled", "par_ready")]
        shared_at = {SHARED_FIRST + SHARED_EVERY * b: b for b in range(0 if first else BATCH)}
        if first:
            ctx.callback(clear_semaphores, nc, sems)
        block = ctx.enter_context(nc.Block())

        @block.sync
        def _(sp):
            if not first:
                sp.wait_ge(tiles_done, 1)
                for b in range(BATCH):
                    load_pairs(sp, m, b, y_sel[:, b], y_in[b])
                for b in range(BATCH):
                    sp.wait_ge(added, b + 1)
                    sp.dma_start(m.out[b].rearrange("(t p) d -> p t d", p=P),
                                 m.h[:, b * TPB:(b + 1) * TPB, :]).then_inc(m.out_done, 16)
                sp.wait_ge(m.out_done, 16 * BATCH)

        @block.gpsimd
        def _(pool):
            def gather(tile):
                if tile >= RING:
                    pool.wait_ge(turned, tile - RING + 1)
                    pool.nop(nofuse=True)
                pool.indirect_dma_start(x_rows[:, tile % RING, :], None, m.x_rows_d,
                                        bass.IndirectOffsetOnAxis(ap=src_row[:, tile:tile + 1], axis=0)
                                        ).then_inc(x_in[tile % RING], 16)

            def scatter(tile):
                pool.wait_ge(y_ready, tile + 1)
                pool.nop(nofuse=True)
                pool.indirect_dma_start(m.y_rows_d, bass.IndirectOffsetOnAxis(ap=dst_row[:, tile:tile + 1], axis=0),
                                        y_rows[:, tile % RING, :], None).then_inc(y_out[tile % RING], 16)

            pool.wait_ge(hot_ready, 1)
            nc.gpsimd.tensor_tensor(
                tile_hot[:, :, 1, :], hot[:, :, :],
                m.fconst[:, FC_KT:FC_KT + 2 * NT].unsqueeze(2).to_broadcast([P, 2 * NT, TILES]), ALU.mult
            ).then_inc(tile_hot_ready, 1)
            pool.wait_ge(m.rows_out[layer], 16 * BATCH)
            pool.wait_ge(order_ready, 2)
            def move_tiles(lo, hi):
                for tile in range(lo, min(lo + RING, hi)):
                    gather(tile)
                pool.wait_ge(order_ready, 3)
                for tile in range(lo, hi):
                    if tile + RING < hi:
                        gather(tile + RING)
                    scatter(tile)
                for r in range(RING):
                    pool.wait_ge(y_out[r], 16 * len(range(r, hi, RING)))

            move_tiles(0, TILES_USUAL)
            with pool.If(tiles_used(nc, ENGINE.Pool, used) > TILES_USUAL):
                move_tiles(TILES_USUAL, TILES)
            pool.nop(nofuse=True).then_inc(tiles_done, 1)

        @block.scalar
        def _(act):
            act.wait_ge(weighed_ready, 1)
            nc.scalar.activation(expd[:, :, :], weighed[:, :, :], ACT.Exp).then_inc(expd_ready, 1)
            nc.scalar.activation(gap_exp[:, :], gap[:, :], ACT.Exp).then_inc(expd_ready, 1)
            if not first:
                act.wait_ge(soft_in, 1)
                nc.scalar.activation(soft[:, 1, :, :], soft[:, 0, :, :], ACT.Exp, scale=-1.0).then_inc(soft_ready, 1)
                act.wait_ge(soft_ready, 1)
                nc.scalar.activation(soft[:, 2, :, :], soft[:, 1, :, :], ACT.Ln, bias=1.0).then_inc(soft_ready, 1)
            act.wait_ge(expd_ready, 2)
            nc.scalar.activation(gap[0:1, 0:1], gap_exp[0:1, 0:1], ACT.Gelu if first else ACT.Sigmoid)
            if not first:
                act.wait_ge(par_filled, 1)
                nc.scalar.activation(par[:, :, :].rearrange("p a c -> p (a c)"), bank_par[:, 0:TILES * N_PAR],
                                     ACT.Copy).then_inc(par_ready, 1)

            def hidden(tile):
                e = expert_of(nc, ENGINE.Activation, tile_expert, tile)
                act.wait_ge(up_done, tile + 1)
                if tile >= 2:
                    act.wait_ge(down_done, tile - 1)
                for c in range(FC):
                    last = nc.scalar.activation(h_act[:, tile % 2, c * P:(c + 1) * P],
                                                bank_up[tile % 2][:, c * P:(c + 1) * P], ACT.Gelu,
                                                bias=m.b1[:, bass.ds(e * FC + c, 1)])
                last.then_inc(act_ready, 1)

            def take_x(tile):
                act.wait_ge(turned, tile + 1)
                if tile >= 2:
                    act.wait_ge(up_done, tile - 1)
                nc.scalar.activation(xt[:, tile % 2, :], bank_turn[tile % 2][:, 0:P], ACT.Copy).then_inc(xt_ready, 1)

            def take_mid(tile):
                act.wait_ge(mid_turned, tile + 1)
                if tile >= 2:
                    act.wait_ge(down_done, tile - 1)
                nc.scalar.activation(te_t[0:I1, tile % 2, :], bank_mid[0:I1, 0:P], ACT.Copy).then_inc(act_ready, 1)

            def shared_bias(b):
                act.wait_ge(s_up, b + 1)
                if b:
                    act.wait_ge(s_te_ready, 2 * b)
                for n in range(2):
                    nc.scalar.activation(s_pre[:, n, :], bank_shared[n][0:I1, :], ACT.Identity,
                                         bias=m.s_b1[:, n:n + 1]).then_inc(s_biased, 1)

            def shared_sigmoid(b):
                act.wait_ge(s_clipped, 2 * b + 1)
                nc.scalar.activation(s_sig[:, :], s_pre[:, 0, :], ACT.Sigmoid,
                                     scale=m.act[0:I1, 1, 0:1]).then_inc(s_sig_ready, 1)

            def sigmoid(tile):
                act.wait_ge(s_sum, tile * 3 + 1)
                if tile >= 2:
                    act.wait_ge(pre_ready, tile - 1)
                nc.scalar.activation(sig[:, tile % 2, :], g_cl[:, tile % 2, :], ACT.Sigmoid,
                                     scale=par[:, tile, PAR_ALPHA:PAR_ALPHA + 1]).then_inc(sig_ready, 1)

            def take_y(tile):
                r = tile % RING
                act.wait_ge(down_done, tile + 1)
                if tile >= RING:
                    act.wait_ge(y_out[r], 16 * (tile // RING))
                nc.scalar.activation(y_rows[:, r, :], bank_down[tile % 2][:, 0:D], ACT.Copy).then_inc(y_ready, 1)

            act.wait_ge(order_ready, 1)

            def run_tiles(lo, hi):
                if first:
                    for tile in range(lo, hi):
                        hidden(tile)
                    return
                take_x(lo)
                for tile in range(lo, hi + 3):
                    if tile + 1 < hi:
                        take_x(tile + 1)
                    if lo + 2 <= tile < hi + 2:
                        take_mid(tile - 2)
                    if tile < hi:
                        sigmoid(tile)
                    if tile >= lo + 3:
                        take_y(tile - 3)
                    if tile - 1 in shared_at:
                        shared_bias(shared_at[tile - 1])
                    if tile - 3 in shared_at:
                        shared_sigmoid(shared_at[tile - 3])

            if not first:
                act.wait_ge(par_ready, 1)
            run_tiles(0, TILES_USUAL)
            with act.If(tiles_used(nc, ENGINE.Activation, used) > TILES_USUAL):
                run_tiles(TILES_USUAL, TILES)

        @block.vector
        def _(dve):
            chain = [0]

            def link(ins):
                chain[0] += 1
                ins.then_inc(dve_chain, 1)
                dve.wait_ge(dve_chain, chain[0])

            def over_tiles(ap):
                return ap.unsqueeze(2).to_broadcast([P, NT, E])

            def over_experts(ap):
                return ap.unsqueeze(1).to_broadcast([P, NT, E])

            def shared_clip(b):
                for n in range(2):
                    dve.wait_ge(s_biased, 2 * b + n + 1)
                    nc.vector.tensor_scalar(s_pre[:, n, :], s_pre[:, n, :], soft[0:I1, 1, 1, n:n + 1],
                                            soft[0:I1, 3, 1, n:n + 1], ALU.min, ALU.max).then_inc(s_clipped, 1)

            def shared_product(b):
                dve.wait_ge(s_sig_ready, b + 1)
                dve.wait_ge(s_clipped, 2 * b + 2)
                if b:
                    dve.wait_ge(s_down, b)
                nc.vector.scalar_tensor_tensor(s_te[0:I1, :], s_pre[:, 1, :], m.act[0:I1, 1, 2:3],
                                               s_pre[:, 0, :], ALU.add, ALU.mult).then_inc(s_te_ready, 1)

            def shared_gate(b):
                dve.wait_ge(s_te_ready, 2 * b + 1)
                nc.vector.scalar_tensor_tensor(s_te[0:I1, :], s_te[0:I1, :], m.act[0:I1, 1, 1:2],
                                               s_sig[:, :], ALU.mult, ALU.mult).then_inc(s_te_ready, 1)

            def shared_add(b):
                dve.wait_ge(s_down, b + 1)
                h = m.h[:, b * TPB:(b + 1) * TPB, :]
                nc.vector.tensor_tensor(h, h, bank_shared[0][:, :].rearrange("p (t d) -> p t d", t=TPB), ALU.add
                                        ).then_inc(s_added, 1)

            rank_e = over_experts(m.fconst[:, FC_RANK:FC_RANK + E])
            values = logits
            for k in range(2):
                link(nc.vector.tensor_reduce(top[:, k, :], values[:, :, :], AX.X, ALU.max))
                link(nc.vector.tensor_tensor(chosen[:, k, :, :], values[:, :, :], over_tiles(top[:, k, :]), ALU.is_equal))
                link(nc.vector.tensor_tensor(chosen[:, k, :, :], chosen[:, k, :, :], rank_e, ALU.mult))
                link(nc.vector.tensor_reduce(rank[:, :], chosen[:, k, :, :], AX.X, ALU.max))
                link(nc.vector.tensor_tensor(chosen[:, k, :, :], rank_e, over_tiles(rank[:, :]), ALU.is_equal))
                if k == 0:
                    link(nc.vector.scalar_tensor_tensor(lower[:, :, :], chosen[:, 0, :, :], MASKED, logits[:, :, :],
                                                        ALU.mult, ALU.add))
                    values = lower
            link(nc.vector.memset(marks[:, 0:NT + 2:NT + 1, :], 0.0))
            nc.vector.tensor_tensor(marks[:, 1:NT + 1, :], chosen[:, 0, :, :], chosen[:, 1, :, :], ALU.add).then_inc(marks_ready, 1)
            link(nc.vector.tensor_tensor(gap[:, :], top[:, 1, :], top[:, 0, :], ALU.subtract))
            nc.vector.tensor_tensor(weighed[:, :, :], logits[:, :, :], over_tiles(top[:, 0, :]), ALU.subtract
                                    ).then_inc(weighed_ready, 1)
            link(nc.vector.memset(zeros_e[:, :], 0.0))
            if not first:
                dve.wait_ge(m.experts_now, 16 * len(m.expert_loads))
                link(nc.vector.tensor_scalar(soft[:, 3, :, :], m.act[:, :, 3:5], -1.0, None, ALU.mult))
                nc.vector.tensor_tensor(soft[:, 0, :, :], m.act[:, :, 3:5], soft[:, 3, :, :], ALU.max).then_inc(soft_in, 1)

            dve.wait_ge(ranks_done, 1)
            rank_bank = bank_rank[:, 0:(NT + 1) * E].rearrange("p (t e) -> p t e", e=E)
            link(nc.vector.tensor_tensor(over[:, :, :], rank_bank[:, NT, :].unsqueeze(2).to_broadcast([P, E, NT]),
                                         m.fconst[:, FC_J128:FC_J128 + NT].unsqueeze(1).to_broadcast([P, E, NT]),
                                         ALU.is_gt))
            link(nc.vector.tensor_reduce(n_tiles[:, :], over[:, :, :], AX.X, ALU.add))
            link(nc.vector.tensor_tensor_scan(ends[:, :], n_tiles[:, :], zeros_e[:, :], 0.0, ALU.add, ALU.add))
            link(nc.vector.tensor_tensor(starts[:, :], ends[:, :], n_tiles[:, :], ALU.subtract))
            link(nc.vector.scalar_tensor_tensor(ranks[:, :, :], over_experts(starts[:, :]), float(P),
                                                rank_bank[:, 0:NT, :], ALU.mult, ALU.add))
            link(nc.vector.tensor_tensor(chosen[:, :, :, :], chosen[:, :, :, :],
                                         ranks[:, :, :].unsqueeze(1).to_broadcast([P, 2, NT, E]), ALU.mult))
            link(nc.vector.tensor_reduce(pos[:, :], chosen[:, :, :, :].rearrange("p k t e -> p (k t) e"), AX.X, ALU.add))
            link(nc.vector.tensor_copy(pos_i[:, :], pos[:, :]))
            link(nc.vector.tensor_single_scalar(row_i[:, :], pos_i[:, :], P - 1, ALU.bitwise_and))
            link(nc.vector.tensor_copy(row[:, :], row_i[:, :]))
            nc.vector.tensor_tensor(tile128[:, :], pos[:, :], row[:, :], ALU.subtract).then_inc(pos_ready, 1)
            dve.wait_ge(pos_ready, 1)
            nc.vector.tensor_tensor(
                hot[:, :, :], tile128[:, :].unsqueeze(2).to_broadcast([P, 2 * NT, TILES]),
                m.fconst[:, FC_A128:FC_A128 + TILES].unsqueeze(1).to_broadcast([P, 2 * NT, TILES]), ALU.is_equal
            ).then_inc(hot_ready, 1)
            dve.wait_ge(hot_ready, 1)
            nc.vector.tensor_scalar(tile_hot[:, :, 0, :], hot[:, :, :], m.fconst[:, FC_PART1:FC_PART1 + 1], None, ALU.mult
                                    ).then_inc(tile_hot_ready, 1)
            for q in range(HOT_PARTS):
                part = slice(q * 2 * NT // HOT_PARTS, (q + 1) * 2 * NT // HOT_PARTS)
                shape = [P, 2 * NT // HOT_PARTS, P]
                nc.vector.tensor_tensor(
                    row_hot[:, part, :], row[:, part].unsqueeze(2).to_broadcast(shape),
                    m.bconst[:, BC_IOTA, :].unsqueeze(1).to_broadcast(shape), ALU.is_equal
                ).then_inc(row_hot_ready, 1)
            nc.vector.tensor_copy(used[:, :], ends[:, E - 1:E])
            link(nc.vector.tensor_tensor(
                before[:, :, :], ends[:, :].unsqueeze(1).to_broadcast([P, TILES, E]),
                m.fconst[:, FC_TILE:FC_TILE + TILES].unsqueeze(2).to_broadcast([P, TILES, E]), ALU.is_le))
            link(nc.vector.tensor_reduce(expert_f[:, :], before[:, :, :], AX.X, ALU.add))
            nc.vector.tensor_scalar(tile_expert[:, :], expert_f[:, :], float(E - 1), None, ALU.min).then_inc(order_ready, 1)
            dve.wait_ge(pairs_done, 1)
            part, kt = [bank_pairs[:, n * TILES:(n + 1) * TILES] for n in range(2)]
            link(nc.vector.tensor_scalar(pair[:, :], part, -1.0, 0.0, ALU.add, ALU.max))
            link(nc.vector.scalar_tensor_tensor(pair[:, :], kt, float(P), pair[:, :], ALU.mult, ALU.add))
            link(nc.vector.tensor_scalar(wrap[:, :], kt, float(NT), -float(TOK), ALU.is_ge, ALU.mult))
            nc.vector.tensor_tensor(src_row[:, :], pair[:, :], wrap[:, :], ALU.add).then_inc(order_ready, 1)
            link(nc.vector.tensor_scalar(pad[:, :], part, 0.0, None, ALU.is_equal))
            link(nc.vector.tensor_tensor(pad[:, :], pad[:, :], m.fconst[:, FC_TRASH:FC_TRASH + TILES], ALU.mult))
            nc.vector.tensor_tensor(dst_row[:, :], pair[:, :], pad[:, :], ALU.add).then_inc(order_ready, 1)
            dve.wait_ge(order_ready, 3)
            if not first:
                dve.wait_ge(soft_ready, 2)
                link(nc.vector.scalar_tensor_tensor(soft[:, 1, :, :], m.act[:, :, 3:5], 0.0, soft[:, 2, :, :],
                                                    ALU.max, ALU.add))
                link(nc.vector.tensor_scalar(soft[:, 3, :, :], soft[:, 1, :, :], -1.0, None, ALU.mult))
                link(nc.vector.memset(s_te[I1:I1 + 1, :], 1.0))
                link(nc.vector.memset(te_t[I1:I1 + 1, :, :], 1.0))
                link(nc.vector.memset(ones_e[:, :], 1.0))
                for n in range(2):
                    for which, col in ((1, PAR_HIGH), (3, PAR_LOW)):
                        nc.vector.tensor_copy(e_par[:, col + n:col + n + 1], soft[0:E, which, 0, n:n + 1])
                link(nc.vector.tensor_copy(e_par[:, PAR_ALPHA:PAR_ALPHA + 3], m.act[0:E, 0, 0:3]))

            if not first:
                link(nc.vector.tensor_scalar(expert_hot[:, :], tile_expert[0:E, :], m.fconst[0:E, FC_PART:FC_PART + 1],
                                             None, ALU.is_equal))
                nc.vector.tensor_tensor(par_spread[:, :, :], expert_hot[:, :].unsqueeze(2).to_broadcast([E, TILES, N_PAR]),
                                        e_par[:, :].unsqueeze(1).to_broadcast([E, TILES, N_PAR]), ALU.mult
                                        ).then_inc(par_spread_ready, 1)
            dve.wait_ge(expd_ready, 2)
            link(nc.vector.tensor_reduce(total[:, :], expd[:, :, :], AX.X, ALU.add))
            link(nc.vector.reciprocal(gate[:, 0, :], total[:, :]))
            link(nc.vector.tensor_tensor(gate[:, 1, :], gap_exp[:, :], gate[:, 0, :], ALU.mult))
            if not first:
                link(nc.vector.tensor_tensor(total[:, :], gate[:, 0, :], gate[:, 1, :], ALU.add))
                link(nc.vector.reciprocal(rank[:, :], total[:, :]))
                for k in range(2):
                    link(nc.vector.tensor_tensor(gate[:, k, :], gate[:, k, :], rank[:, :], ALU.mult))

            def take_x(tile):
                dve.wait_ge(turned, tile + 1)
                if tile >= 2:
                    dve.wait_ge(up_done, tile - 1)
                nc.vector.tensor_copy(xt[:, tile % 2, :], bank_turn[tile % 2][:, 0:P]).then_inc(xt_ready, 1)

            def take_w1(tile, e):
                if tile >= 2:
                    dve.wait_ge(up_done, tile - 1)
                nc.vector.tensor_scalar(w1_now[:, tile % 2, :], m.w1[:, bass.ds(e * DFF, DFF)], 1.0, None, ALU.mult
                                        ).then_inc(w1_ready, 1)

            def take_y(tile, e):
                r = tile % RING
                dve.wait_ge(down_done, tile + 1)
                if tile >= RING:
                    dve.wait_ge(y_out[r], 16 * (tile // RING))
                nc.vector.tensor_tensor(y_rows[:, r, :], bank_down[tile % 2][:, 0:D], m.b2[:, bass.ds(e * D, D)], ALU.add
                                        ).then_inc(y_ready, 1)

            def front_1(tile):
                p = tile % 2
                column = lambda n: par[:, tile, n:n + 1]
                products = bank_up[p][:, 0:2 * I1].rearrange("p (i c) -> p i c", c=2)
                dve.wait_ge(up_done, tile + 1)
                if tile >= 2:
                    dve.wait_ge(sig_ready, tile - 1)
                    dve.wait_ge(pre_ready, tile - 1)
                nc.vector.tensor_scalar(g_cl[:, p, :], products[:, :, 0], column(PAR_HIGH), column(PAR_LOW),
                                        ALU.min, ALU.max).then_inc(s_sum, 1)
                nc.vector.tensor_scalar(u_cl[:, p, :], products[:, :, 1], column(PAR_HIGH + 1), column(PAR_LOW + 1),
                                        ALU.min, ALU.max).then_inc(s_sum, 1)
                dve.wait_ge(s_sum, tile * 3 + 2)
                nc.vector.scalar_tensor_tensor(gu[:, p, :], u_cl[:, p, :], column(PAR_SHIFT), g_cl[:, p, :],
                                               ALU.add, ALU.mult).then_inc(s_sum, 1)

            def back_1(tile):
                p = tile % 2
                dve.wait_ge(sig_ready, tile + 1)
                dve.wait_ge(s_sum, tile * 3 + 3)
                if tile >= 2:
                    dve.wait_ge(mid_turned, tile - 1)
                nc.vector.scalar_tensor_tensor(te[:, p, :], gu[:, p, :], par[:, tile, PAR_SCALE:PAR_SCALE + 1],
                                               sig[:, p, :], ALU.mult, ALU.mult).then_inc(pre_ready, 1)

            def run_tiles(lo, hi):
                experts = {}
                if first:
                    for tile in range(lo, lo + 2):
                        experts[tile] = expert_of(nc, ENGINE.DVE, tile_expert, tile)
                        take_w1(tile, experts[tile])
                    take_x(lo)
                for tile in range(lo, hi + 2):
                    if first and tile + 1 < hi:
                        take_x(tile + 1)
                    if first and tile + 2 < hi:
                        experts[tile + 2] = expert_of(nc, ENGINE.DVE, tile_expert, tile + 2)
                        take_w1(tile + 2, experts[tile + 2])
                    if first and tile >= lo + 2:
                        take_y(tile - 2, experts.pop(tile - 2))
                    if not first and tile < hi:
                        front_1(tile)
                    if not first and lo + 1 <= tile <= hi:
                        back_1(tile - 1)
                    for late, stage in ((2, shared_clip), (4, shared_product), (5, shared_gate), (7, shared_add)):
                        if tile - late in shared_at:
                            stage(shared_at[tile - late])

            if not first:
                dve.wait_ge(par_ready, 1)
            run_tiles(0, TILES_USUAL)
            with dve.If(tiles_used(nc, ENGINE.DVE, used) > TILES_USUAL):
                run_tiles(TILES_USUAL, TILES)

            if not first:
                for b in range(BATCH + 1):
                    if b < BATCH:
                        dve.wait_ge(y_in[b], 32)
                        add_pairs(nc, m, b, 0, y_sel[:, b]).then_inc(half_added, 1)
                    if b:
                        dve.wait_ge(half_added, b)
                        add_pairs(nc, m, b - 1, 1, y_sel[:, b - 1]).then_inc(added, 1)

        @block.tensor
        def _(pe):
            ident = m.fconst[:, FC_IDENT:FC_IDENT + P]
            pe.wait_ge(m.experts_now, 16 * len(m.expert_loads))

            def shared_up(b):
                if b:
                    pe.wait_ge(s_added, b)
                    pe.wait_ge(s_biased, 2 * b)
                for n in range(2):
                    w = m.s_w1[:, :].rearrange("p (i c) -> p c i", c=2)[:, n, :]
                    last = nc.tensor.matmul(bank_shared[n][0:I1, :], w, m.x2_t[:, b, :], start=True, stop=True)
                last.then_inc(s_up, 1)

            def shared_down(b):
                pe.wait_ge(s_te_ready, 2 * b + 2)
                for t in range(TPB):
                    last = nc.tensor.matmul(bank_shared[0][:, t * P:(t + 1) * P], s_te[:, t * P:(t + 1) * P],
                                            m.s_w2[:, :], start=True, stop=True)
                last.then_inc(s_down, 1)

            pe.wait_ge(marks_ready, 1)
            shifts = [0] + list(range(2, NT + 1)) + [1]
            for n, shift in enumerate(shifts):
                first_out = max(shift - 1, 0)
                last = nc.tensor.matmul(bank_rank[:, first_out * E:(NT + 1) * E],
                                        m.bconst[:, BC_ONES if shift else BC_TRI, :],
                                        marks[:, first_out + 1 - shift:NT + 2 - shift, :].rearrange("p t e -> p (t e)"),
                                        start=(n == 0), stop=(n == NT))
            last.then_inc(ranks_done, 1)
            pe.wait_ge(tile_hot_ready, 2)
            for g in range(2 * NT):
                pe.wait_ge(row_hot_ready, g * HOT_PARTS // (2 * NT) + 1)
                last = nc.tensor.matmul(bank_pairs[:, 0:2 * TILES], row_hot[:, g, :],
                                        tile_hot[:, g, :, :].rearrange("p s a -> p (s a)"),
                                        start=(g == 0), stop=(g == 2 * NT - 1))
            last.then_inc(pairs_done, 1)
            if not first:
                pe.wait_ge(par_spread_ready, 1)
                nc.tensor.matmul(bank_par[:, 0:TILES * N_PAR], ones_e[:, :], par_spread[:, :, :].rearrange("e a c -> e (a c)"),
                                 start=True, stop=True).then_inc(par_filled, 1)
            pe.wait_ge(order_ready, 3)

            def turn(tile):
                pe.wait_ge(x_in[tile % RING], 16 * (tile // RING + 1))
                before = tile - (2 if first else 1)
                if before >= 0:
                    pe.wait_ge(xt_ready, before + 1)
                nc.tensor.transpose(bank_turn[tile % 2][:, 0:P], x_rows[:, tile % RING, :], ident).then_inc(turned, 1)

            def up_0(tile):
                pe.wait_ge(xt_ready, tile + 1)
                pe.wait_ge(w1_ready, tile + 1)
                if tile >= 2:
                    pe.wait_ge(act_ready, tile - 1)
                for c in range(FC):
                    last = nc.tensor.matmul(bank_up[tile % 2][:, c * P:(c + 1) * P], w1_now[:, tile % 2, c * P:(c + 1) * P],
                                            xt[:, tile % 2, :], start=True, stop=True)
                last.then_inc(up_done, 1)

            def up_1(tile, e):
                pe.wait_ge(xt_ready, tile + 1)
                if tile >= 2:
                    pe.wait_ge(s_sum, (tile - 2) * 3 + 2)
                nc.tensor.matmul(bank_up[tile % 2][:, 0:2 * I1], xt[:, tile % 2, :],
                                 m.e_w1[:, bass.ds(e * 2 * I1, 2 * I1)], start=True, stop=False)
                nc.tensor.matmul(bank_up[tile % 2][:, 0:2 * I1], m.fconst[:, FC_ROW0:FC_ROW0 + P],
                                 m.e_b1[:, bass.ds(e * 2 * I1, 2 * I1)], start=False, stop=True).then_inc(up_done, 1)

            def mid(tile):
                pe.wait_ge(pre_ready, tile + 1)
                if tile:
                    pe.wait_ge(act_ready, tile)
                nc.tensor.transpose(bank_mid[0:I1, 0:P], te[:, tile % 2, :], ident).then_inc(mid_turned, 1)

            def down(tile, e):
                pe.wait_ge(act_ready, tile + 1)
                if tile >= 2:
                    pe.wait_ge(y_ready, tile - 1)
                if first:
                    for c in range(FC):
                        last = nc.tensor.matmul(bank_down[tile % 2][:, 0:D], h_act[:, tile % 2, c * P:(c + 1) * P],
                                                m.w2[:, bass.ds(e * DFF + c * D, D)], start=(c == 0), stop=(c == FC - 1))
                else:
                    last = nc.tensor.matmul(bank_down[tile % 2][:, 0:D], te_t[:, tile % 2, :],
                                            m.e_w2[:, bass.ds(e * D, D)], start=True, stop=True)
                last.then_inc(down_done, 1)

            def run_tiles(lo, hi):
                experts = {}
                turn(lo)
                down_late = 2 if first else 3
                for tile in range(lo, hi + down_late):
                    if tile < hi:
                        experts[tile] = expert_of(nc, ENGINE.PE, tile_expert, tile)
                        if first:
                            up_0(tile)
                        else:
                            up_1(tile, experts[tile])
                    if tile + 1 < hi:
                        turn(tile + 1)
                    if not first and lo + 2 <= tile < hi + 2:
                        mid(tile - 2)
                    if tile >= lo + down_late:
                        down(tile - down_late, experts.pop(tile - down_late))
                    if tile in shared_at:
                        shared_up(shared_at[tile])
                    if tile - 6 in shared_at:
                        shared_down(shared_at[tile - 6])

            run_tiles(0, TILES_USUAL)
            with pe.If(tiles_used(nc, ENGINE.PE, used) > TILES_USUAL):
                run_tiles(TILES_USUAL, TILES)


def program(nc, io):
    with ExitStack() as ctx:
        def sb(name, shape, dt=F32):
            return ctx.enter_context(nc.sbuf_tensor(name, shape, dt))

        def dram(name, shape, dt=F32):
            return nc.dram_tensor(name, shape, dt, kind="Internal").ap()

        def sem(name):
            return ctx.enter_context(nc.semaphore(name))

        m = Memory()
        m.x, m.table, m.out, m.w_qkv_d = io["x"], io["table"], io["out"], io["w_qkv_d"]
        m.w_o_d, m.router_w_d, m.router_b_d, m.w1_d = io["w_o_d"], io["router_w_d"], io["router_b_d"], io["w1_d"]
        m.w2_d, m.b1_d, m.b2_d, m.e_w1_d = io["w2_d"], io["b1_d"], io["b2_d"], io["e_w1_d"]
        m.e_b1_d, m.e_w2_d, m.e_b2_d, m.e_act_d = io["e_b1_d"], io["e_w2_d"], io["e_b2_d"], io["e_act_d"]
        m.s_w1_d, m.s_b1_d, m.s_w2_d, m.s_b2_d = io["s_w1_d"], io["s_b1_d"], io["s_w2_d"], io["s_b2_d"]
        m.s_act_d, m.fconst_d, m.bconst_d, m.q_rows_d = io["s_act_d"], io["fconst_d"], io["bconst_d"], io["q_rows_d"]
        m.k_rows_d = io["k_rows_d"]
        m.h = sb("h", [P, NT, D])
        m.fconst = sb("fconst", [P, FC_END])
        m.bconst = sb("bconst", [P, BC_END, P], BF16)
        m.w_qkv = sb("w_qkv", [P, 2, 3 * D])
        m.w_o = sb("w_o", [P, 2, NG, D])
        m.router_w = sb("router_w", [P, 2, E])
        m.router_b = sb("router_b", [P, 2, E])
        m.parts_d = dram("parts_d", [BATCH, 2, 3, HD, H, SEQ], BF16)
        m.logits = sb("logits", [P, NT, E])
        m.gate = sb("gate", [P, 2, NT])
        m.x_rows_d = dram("x_rows_d", [TOK, D])
        m.y_rows_d = dram("y_rows_d", [PAIRS + SLOTS, D])
        m.bank = [ctx.enter_context(nc.psum_tensor(f"bank{i}", [P, 512], F32)) for i in range(8)]
        m.bconst_in, m.attn_w_in = sem("bconst_in"), sem("attn_w_in")
        m.out_done = sem("out_done")
        m.rows_out = [sem(f"rows_out_{layer}") for layer in range(2)]
        m.experts_in, m.experts2_in = sem("experts_in"), sem("experts2_in")

        m.rows_in = [sem(f"rows_in_{b}") for b in range(BATCH)]
        m.x_in = [[sem(f"x_in_{layer}_{r}") for r in range(RING)] for layer in range(2)]
        m.y_out = [[sem(f"y_out_{layer}_{r}") for r in range(RING)] for layer in range(2)]

        with ExitStack() as experts:
            def esb(name, shape, dt=F32):
                return experts.enter_context(nc.sbuf_tensor(name, shape, dt))

            m.w1, m.w2 = esb("w1", [P, E * DFF]), esb("w2", [P, E * DFF])
            m.b1, m.b2 = esb("b1", [P, E * FC]), esb("b2", [P, E * D])
            m.x2_t = esb("x2_t_0", [P, 2, SEQ])
            m.experts_now = m.experts_in
            m.expert_loads = [(m.b1[:, :], m.b1_d), (m.b2[:, :], m.b2_d.partition_broadcast(P))]
            for e in range(0, E, 4):
                for dest, src in ((m.w1, m.w1_d), (m.w2, m.w2_d)):
                    m.expert_loads.append((dest[:, e * DFF:(e + 4) * DFF], src[:, e * DFF:(e + 4) * DFF]))
            m.idx_col = esb("idx_col", [P, BATCH, TPB], I32)
            embed_phase(nc, m)
            attention_phase(nc, m, 0)
            moe_phase(nc, m, 0)
        m.e_w1, m.e_w2 = sb("e_w1", [P, E * 2 * I1]), sb("e_w2", [I1 + 1, E * D])
        m.e_b1 = sb("e_b1", [P, E * 2 * I1])
        m.act = sb("act", [P, 2, 5])
        m.s_w1, m.s_w2, m.s_b1 = sb("s_w1", [P, 2 * I1]), sb("s_w2", [I1 + 1, D]), sb("s_b1", [I1, 2])
        m.x2_t = sb("x2_t_1", [P, BATCH, SEQ])
        m.experts_now = m.experts2_in
        m.expert_loads = [
            (m.e_w1[:, :].rearrange("p (e f) -> p e f", e=E), m.e_w1_d.rearrange("e d f -> d e f")),
            (m.e_w2[0:I1, :].rearrange("p (e d) -> p e d", e=E), m.e_w2_d.rearrange("e i d -> i e d")),
            (m.e_b1[:, :], m.e_b1_d.partition_broadcast(P)),
            (m.e_w2[I1:I1 + 1, :], m.e_b2_d.unsqueeze(0)),
            (m.act[:, 0, :], m.e_act_d),
            (m.act[:, 1, :], m.s_act_d.partition_broadcast(P)),
            (m.s_w1[:, :], m.s_w1_d),
            (m.s_w2[0:I1, :], m.s_w2_d),
            (m.s_w2[I1:I1 + 1, :], m.s_b2_d.unsqueeze(0)),
            (m.s_b1[:, :], m.s_b1_d.rearrange("(i c) -> i c", c=2)),
        ]
        attention_phase(nc, m, 1)
        moe_phase(nc, m, 1)


def constants():
    p = np.arange(P)
    f = np.zeros((P, FC_END), np.float32)
    f[:, FC_IDENT:FC_IDENT + P] = np.eye(P)
    f[:, FC_RANK:FC_RANK + E] = E - np.arange(E)
    f[:, FC_J128:FC_J128 + NT] = P * np.arange(NT)
    f[:, FC_A128:FC_A128 + TILES] = P * np.arange(TILES)
    f[:, FC_TILE:FC_TILE + TILES] = np.arange(TILES)
    f[:, FC_TRASH:FC_TRASH + TILES] = PAIRS + P * np.arange(TILES)[None] + p[:, None]
    f[:, FC_KT:FC_KT + 2 * NT] = np.arange(2 * NT)
    f[:, FC_PART], f[:, FC_PART1] = p, p + 1
    f[:, FC_POW:FC_POW + TPB] = -0.5
    f[0, FC_ROW0:FC_ROW0 + P] = 1.0
    b = np.zeros((P, BC_END, P), np.float32)
    past = p[:, None] - p[None]
    b[:, BC_IDENT] = np.eye(P)
    b[:, BC_CAUSAL_Q] = np.where(past < 0, MASKED, 0.0)
    b[:, BC_CAUSAL_K] = b[:, BC_CAUSAL_Q].T
    b[:, BC_PAST_Q] = np.maximum(past, 0)
    b[:, BC_PAST_K] = b[:, BC_PAST_Q].T
    b[:, BC_TRI] = past < 0
    b[:, BC_ONES] = 1.0
    b[:, BC_IOTA] = p
    t = np.arange(SEQ)
    high, low = t // 256 * 256, t % 256
    one = np.ones(SEQ)
    q_rows = np.stack([0 * one, 0 * one, 0 * one, high, low, one, one])
    k_rows = np.stack([one, one, one, one, one, -high, -low])
    bf = np.dtype("bfloat16")
    return {"fconst_d": f, "bconst_d": b.astype(bf), "q_rows_d": q_rows.astype(bf), "k_rows_d": k_rows.astype(bf)}


def padded_out(w, bias):
    w = w.T.reshape(NG, GH, HD, D)
    out = np.zeros((NG, GH, 2 * HD, D), w.dtype)
    out[:, :, :HD] = w
    out[0, 0, HD] = bias
    return out.reshape(NG, GH * 2 * HD, D)


def projections(w):
    q, k, v = w.reshape(3, H, HD, D)
    return np.concatenate([q.transpose(1, 0, 2).reshape(D, D), k.transpose(1, 0, 2).reshape(D, D), v.reshape(D, D)]).T


def layout(a):
    c = np.ascontiguousarray
    return {
        "x": a["x"],
        "table": a["L0_tok_table"],
        "w_qkv_d": c(np.stack([projections(a["L0_attn_w_qkv"]), projections(a["L1_attn_w_qkv"])])),
        "w_o_d": c(np.stack([padded_out(a["L0_attn_w_proj"], a["L0_attn_b_proj"]),
                             padded_out(a["L1_attn_w_out"], a["L1_attn_b_out"])])),
        "router_w_d": c(np.stack([a["L0_ffn_router_w"].T, a["L1_ffn_gate_w"]], axis=1)),
        "router_b_d": c(np.stack([a["L0_ffn_router_b"], a["L1_ffn_gate_b"]])),
        "w1_d": c(a["L0_ffn_w1"].transpose(2, 0, 1).reshape(D, E * DFF)),
        "w2_d": c(a["L0_ffn_w2"].reshape(E, D, FC, P).transpose(3, 0, 2, 1).reshape(P, E * FC * D)),
        "b1_d": c(a["L0_ffn_b1"].reshape(E, FC, P).transpose(2, 0, 1).reshape(P, E * FC)),
        "b2_d": c(a["L0_ffn_b2"].reshape(E * D)),
        "e_w1_d": a["L1_ffn_expert_w1"], "e_b1_d": c(a["L1_ffn_expert_b1"].reshape(-1)),
        "e_w2_d": a["L1_ffn_expert_w2"], "e_b2_d": c(a["L1_ffn_expert_b2"].reshape(-1)),
        "e_act_d": np.tile(a["L1_ffn_expert_act"], (P // E, 1)),
        "s_w1_d": a["L1_ffn_shared_w1"], "s_b1_d": a["L1_ffn_shared_b1"],
        "s_w2_d": a["L1_ffn_shared_w2"], "s_b2_d": a["L1_ffn_shared_b2"], "s_act_d": a["L1_ffn_shared_act"],
    }


def kernel(**inputs):
    import concourse.bacc as bacc
    from concourse.bass_utils import run_bass_kernel_spmd

    nc = bacc.Bacc("TRN2", target_bir_lowering=False, num_devices=1)
    data = layout({name: np.asarray(a) for name, a in inputs.items()})
    data.update(constants())
    arrays, io = {}, {}
    for name, a in data.items():
        arrays[f"in_{name}"] = a
        io[name] = nc.dram_tensor(f"in_{name}", list(a.shape), mybir.dt.from_np(a.dtype), kind="ExternalInput").ap()
    io["out"] = nc.dram_tensor("out_0_dram", [BATCH, SEQ, D], F32, kind="ExternalOutput").ap()
    program(nc, io)
    r = run_bass_kernel_spmd(nc, [arrays], core_ids=[0])
    return r.results[0]["out_0_dram"]
```
